# Optimizing a Trainium2 kernel written in Bass

```python
import numpy as np
import jax
import jax.numpy as jnp

def _softmax(x, axis=-1):
    return jax.nn.softmax(x, axis=axis)

def _gelu(x):
    return jax.nn.gelu(x, approximate=True)

def _silu(x):
    return jax.nn.silu(x)

def _sigmoid(x):
    return jax.nn.sigmoid(x)

def _layernorm(x, axis=-1, eps=1e-05):
    m = jnp.mean(x, axis=axis, keepdims=True)
    v = jnp.var(x, axis=axis, keepdims=True)
    return (x - m) / jnp.sqrt(v + eps)

def _scatter_add(tgt, idx, src, axis=0):
    return tgt.at[idx].add(src)

def _segment_sum(src, seg, n):
    return jax.ops.segment_sum(src, seg, n)
kernel_name = 'mk_decoder_preln_d1_seqx_r8_7c8f73'

def setup_inputs(seed: int=0):
    np.random.seed(seed)
    _w = jnp.asarray

    def _rec_inputs():
        import jax
        import jax.numpy as jnp
        _rk = jax.random.key(seed)
        x = -0.0003929 + 0.9999 * jax.random.normal(jax.random.fold_in(_rk, 1), (4, 256, 256), jnp.float32)
        _lenS = 256 - jax.random.randint(jax.random.fold_in(_rk, 7), (4,), 0, max(1, 256 // 4) + 1, jnp.int32)
        _lenS2 = 256 - jax.random.randint(jax.random.fold_in(_rk, 8), (4,), 0, max(1, 256 // 4) + 1, jnp.int32)
        _ctx_2048P = jax.random.normal(jax.random.fold_in(_rk, 11), (4, 16, 256), jnp.float32)
        _ctx_2048c = jax.random.dirichlet(jax.random.fold_in(_rk, 511), 0.3 * jnp.ones((16,), jnp.float32), (4, 256))
        _ctx_2048t = jnp.einsum('bsk,bkd->bsd', _ctx_2048c, _ctx_2048P)
        _ctx_2048t = _ctx_2048t * jax.lax.rsqrt(jnp.mean(jnp.square(_ctx_2048t)) + 1e-12) * 0.953939
        ctx_2048 = -0.000514642 + 1.00011 * (_ctx_2048t + 0.3 * jax.random.normal(jax.random.fold_in(_rk, 611), (4, 256, 256), jnp.float32))
        return (x, ctx_2048)
    x, ctx_2048 = _rec_inputs()

    def _L0_attn_setup():
        import jax, jax.numpy as jnp
        import numpy as np
        D_MODEL = 256
        EXPAND = 2
        D_INNER = D_MODEL * EXPAND
        HEAD_DIM = 64
        NHEADS = D_INNER // HEAD_DIM
        D_STATE = 128
        NGROUPS = 1
        D_CONV = 4
        CHUNK = 32
        CONV_DIM = D_INNER + 2 * NGROUPS * D_STATE
        D_IN_PROJ = 2 * D_INNER + 2 * NGROUPS * D_STATE + NHEADS
        EPS = 1e-05

        def segsum(x):
            T = x.shape[-1]
            xc = jnp.cumsum(x, axis=-1)
            diff = xc[..., :, None] - xc[..., None, :]
            mask = jnp.tril(jnp.ones((T, T), dtype=bool))
            return jnp.where(mask, diff, -jnp.inf)

        def causal_conv1d(x, w, b):
            K = w.shape[1]
            L = x.shape[1]
            xp = jnp.pad(x, ((0, 0), (K - 1, 0), (0, 0)))
            y = b[None, None, :]
            for k in range(K):
                y = y + xp[:, k:k + L, :] * w[None, None, :, k]
            return jax.nn.silu(y)

        def ssd_chunked(x, dt, A, B, C, Dskip):
            b, l, h, p = x.shape
            g, n = (B.shape[2], B.shape[3])
            c = l // CHUNK
            xc = x.reshape(b, c, CHUNK, h, p)
            dtc = dt.reshape(b, c, CHUNK, h)
            Bh = jnp.repeat(B.reshape(b, c, CHUNK, g, n), h // g, axis=3)
            Ch = jnp.repeat(C.reshape(b, c, CHUNK, g, n), h // g, axis=3)
            dA = dtc * A[None, None, None, :]
            dAc = jnp.moveaxis(dA, 3, 1)
            A_cumsum = jnp.cumsum(dAc, axis=-1)
            Lmat = jnp.exp(segsum(dAc))
            Y_diag = jnp.einsum('bclhn,bcshn,bhcls,bcsh,bcshp->bclhp', Ch, Bh, Lmat, dtc, xc)
            decay_states = jnp.exp(A_cumsum[..., -1:] - A_cumsum)
            states = jnp.einsum('bclhn,bhcl,bclh,bclhp->bchpn', Bh, decay_states, dtc, xc)
            states = jnp.concatenate([jnp.zeros_like(states[:, :1]), states], axis=1)
            chunk_sums = jnp.pad(A_cumsum[..., -1], ((0, 0), (0, 0), (1, 0)))
            decay_chunk = jnp.exp(segsum(chunk_sums))
            new_states = jnp.einsum('bhzc,bchpn->bzhpn', decay_chunk, states)
            states_prev = new_states[:, :-1]
            state_decay_out = jnp.exp(A_cumsum)
            Y_off = jnp.einsum('bclhn,bchpn,bhcl->bclhp', Ch, states_prev, state_decay_out)
            Y = (Y_diag + Y_off).reshape(b, l, h, p) + x * Dskip[None, None, :, None]
            return Y

        def gated_rmsnorm(y, z, w):
            x = y * jax.nn.silu(z)
            gs = D_INNER // NGROUPS
            xg = x.reshape(x.shape[:-1] + (NGROUPS, gs))
            var = jnp.mean(xg * xg, axis=-1, keepdims=True)
            xg = xg * jax.lax.rsqrt(var + EPS)
            return xg.reshape(x.shape) * w[None, None, :]
        key = jax.random.key(seed)
        ks = jax.random.split(key, 9)
        B, L = (2, 256)
        return {'hidden_states': jax.random.normal(ks[0], (B, L, D_MODEL), jnp.float32), 'W_in': jax.random.normal(ks[1], (D_MODEL, D_IN_PROJ), jnp.float32) * 0.02, 'conv_w': jax.random.normal(ks[2], (CONV_DIM, D_CONV), jnp.float32) * 0.2, 'conv_b': jax.random.normal(ks[3], (CONV_DIM,), jnp.float32) * 0.02, 'A': -jnp.exp(jax.random.normal(ks[4], (NHEADS,), jnp.float32) * 0.5), 'D': jax.random.normal(ks[5], (NHEADS,), jnp.float32) * 0.5, 'dt_bias': jax.random.normal(ks[6], (NHEADS,), jnp.float32) * 0.5, 'norm_w': jnp.ones((D_INNER,), jnp.float32) + jax.random.normal(ks[7], (D_INNER,), jnp.float32) * 0.02, 'W_out': jax.random.normal(ks[8], (D_INNER, D_MODEL), jnp.float32) * 0.02}
    _L0_attn_all = _L0_attn_setup()
    _L0_attn_in = {k: v for k, v in _L0_attn_all.items() if k in ('W_in', 'conv_w', 'conv_b', 'A', 'D', 'dt_bias', 'norm_w', 'W_out')}
    del _L0_attn_all

    def _L0_xattn_setup():
        import jax, jax.numpy as jnp
        import numpy as np
        DIM = 256
        NHEADS = 32
        HEAD_DIM = DIM // NHEADS
        EPS = 1e-06

        def _rmsnorm(t):
            return t * jax.lax.rsqrt(jnp.mean(t * t, axis=-1, keepdims=True) + EPS)
        key = jax.random.key(seed)
        kx, kc, kq, kk, kv = jax.random.split(key, 5)
        x = jax.random.normal(kx, (2, 512, DIM), dtype=jnp.float32)
        context = jax.random.normal(kc, (2, 64, DIM), dtype=jnp.float32)
        std = 0.02
        Wq = jax.random.normal(kq, (DIM, DIM), dtype=jnp.float32) * std
        Wk = jax.random.normal(kk, (DIM, DIM), dtype=jnp.float32) * std
        Wv = jax.random.normal(kv, (DIM, DIM), dtype=jnp.float32) * std
        return {'x': x, 'context': context, 'Wq': Wq, 'Wk': Wk, 'Wv': Wv}
    _L0_xattn_all = _L0_xattn_setup()
    _L0_xattn_in = {k: v for k, v in _L0_xattn_all.items() if k in ('Wq', 'Wk', 'Wv')}
    del _L0_xattn_all

    def _L0_ffn_setup():
        import jax, jax.numpy as jnp
        import numpy as np
        B, S, H = (4, 128, 256)
        NH = 16
        HD = H // NH
        RD = HD // 2
        LAT = H // 4
        I = 128
        NE = 8
        NSH = 1
        NR = NE - NSH
        TOPK = 2
        EPS = 1e-05
        SCALING = 8.0

        def _w(key, shape, fan_in):
            return jax.random.normal(key, shape, dtype=jnp.float32) / np.sqrt(fan_in)

        def rmsnorm(x, w):
            rms = jax.lax.rsqrt(jnp.mean(x * x, axis=-1, keepdims=True) + EPS)
            return w * rms * x

        def rope_cos_sin(seq_len):
            inv_freq = 1.0 / 10000.0 ** (jnp.arange(0, RD, 2, dtype=jnp.float32) / RD)
            t = jnp.arange(seq_len, dtype=jnp.float32)
            ang = jnp.outer(t, inv_freq)
            emb = jnp.concatenate([ang, ang], axis=-1)
            return (jnp.cos(emb), jnp.sin(emb))

        def apply_rope(x, cos, sin):
            c = cos[None, :, None, :]
            s = sin[None, :, None, :]
            x1, x2 = jnp.split(x, 2, axis=-1)
            rot = jnp.concatenate([-x2, x1], axis=-1)
            return x * c + rot * s

        def expert_ffn(x, wg, wu, wd):
            h = jax.nn.silu(x @ wg) * (x @ wu) / SCALING
            return h @ wd

        def attention(x, kv_d_w, q_d_w, k_u_w, v_u_w, q_u_w, rope_k_w, rope_q_w, o_w):
            b, s, _ = x.shape
            kv_d = x @ kv_d_w
            q_d = x @ q_d_w
            k_p = (kv_d @ k_u_w).reshape(b, s, NH, RD)
            q_p = (q_d @ q_u_w).reshape(b, s, NH, RD)
            v = (kv_d @ v_u_w).reshape(b, s, NH, HD)
            k_r = (x @ rope_k_w).reshape(b, s, NH, RD)
            q_r = (q_d @ rope_q_w).reshape(b, s, NH, RD)
            cos, sin = rope_cos_sin(s)
            k_r = apply_rope(k_r, cos, sin)
            q_r = apply_rope(q_r, cos, sin)
            k = jnp.concatenate([k_p, k_r], axis=-1)
            q = jnp.concatenate([q_p, q_r], axis=-1)
            scale = 1.0 / np.sqrt(HD)
            scores = jnp.einsum('bqhd,bkhd->bhqk', q, k) * scale
            causal = jnp.tril(jnp.ones((s, s), dtype=bool))
            scores = jnp.where(causal[None, None], scores, jnp.finfo(scores.dtype).min)
            probs = jax.nn.softmax(scores, axis=-1)
            out = jnp.einsum('bhqk,bkhd->bqhd', probs, v).reshape(b, s, H)
            return out @ o_w

        def moe(x, sh_gate, sh_up, sh_down, r_gate, r_up, r_down, router_w, router_b):
            shared = expert_ffn(x, sh_gate, sh_up, sh_down)
            logits = x @ router_w + router_b
            probs = jax.nn.sigmoid(logits)
            scores, idx = jax.lax.top_k(probs, TOPK)
            scores = scores / jnp.sum(scores, axis=-1, keepdims=True)
            w = jnp.sum(jax.nn.one_hot(idx, NR, dtype=x.dtype) * scores[..., None], axis=-2)
            combined = jnp.zeros_like(x)
            for e in range(NR):
                combined = combined + w[..., e:e + 1] * expert_ffn(x, r_gate[e], r_up[e], r_down[e])
            return shared + combined
        key = jax.random.key(seed)
        ks = jax.random.split(key, 24)
        return {'x': jax.random.normal(ks[0], (B, S, H), dtype=jnp.float32), 'ln1_w': jnp.ones((H,), jnp.float32), 'ln2_w': jnp.ones((H,), jnp.float32), 'kv_d_w': _w(ks[1], (H, LAT), H), 'q_d_w': _w(ks[2], (H, LAT), H), 'k_u_w': _w(ks[3], (LAT, H // 2), LAT), 'v_u_w': _w(ks[4], (LAT, H), LAT), 'q_u_w': _w(ks[5], (LAT, H // 2), LAT), 'rope_k_w': _w(ks[6], (H, H // 2), H), 'rope_q_w': _w(ks[7], (LAT, H // 2), LAT), 'o_w': _w(ks[8], (H, H), H), 'sh_gate': _w(ks[9], (H, I), H), 'sh_up': _w(ks[10], (H, I), H), 'sh_down': _w(ks[11], (I, H), I), 'r_gate': _w(ks[12], (NR, H, I), H), 'r_up': _w(ks[13], (NR, H, I), H), 'r_down': _w(ks[14], (NR, I, H), I), 'router_w': _w(ks[15], (H, NR), H), 'router_b': jnp.zeros((NR,), jnp.float32)}
    _L0_ffn_all = _L0_ffn_setup()
    _L0_ffn_in = {k: v for k, v in _L0_ffn_all.items() if k in ('ln1_w', 'ln2_w', 'kv_d_w', 'q_d_w', 'k_u_w', 'v_u_w', 'q_u_w', 'rope_k_w', 'rope_q_w', 'o_w', 'sh_gate', 'sh_up', 'sh_down', 'r_gate', 'r_up', 'r_down', 'router_w', 'router_b')}
    del _L0_ffn_all
    return {'x': x, 'ctx_2048': ctx_2048, 'L0_attn_W_in': _L0_attn_in['W_in'], 'L0_attn_conv_w': _L0_attn_in['conv_w'], 'L0_attn_conv_b': _L0_attn_in['conv_b'], 'L0_attn_A': _L0_attn_in['A'], 'L0_attn_D': _L0_attn_in['D'], 'L0_attn_dt_bias': _L0_attn_in['dt_bias'], 'L0_attn_norm_w': _L0_attn_in['norm_w'], 'L0_attn_W_out': _L0_attn_in['W_out'], 'L0_xattn_Wq': _L0_xattn_in['Wq'], 'L0_xattn_Wk': _L0_xattn_in['Wk'], 'L0_xattn_Wv': _L0_xattn_in['Wv'], 'L0_ffn_ln1_w': _L0_ffn_in['ln1_w'], 'L0_ffn_ln2_w': _L0_ffn_in['ln2_w'], 'L0_ffn_kv_d_w': _L0_ffn_in['kv_d_w'], 'L0_ffn_q_d_w': _L0_ffn_in['q_d_w'], 'L0_ffn_k_u_w': _L0_ffn_in['k_u_w'], 'L0_ffn_v_u_w': _L0_ffn_in['v_u_w'], 'L0_ffn_q_u_w': _L0_ffn_in['q_u_w'], 'L0_ffn_rope_k_w': _L0_ffn_in['rope_k_w'], 'L0_ffn_rope_q_w': _L0_ffn_in['rope_q_w'], 'L0_ffn_o_w': _L0_ffn_in['o_w'], 'L0_ffn_sh_gate': _L0_ffn_in['sh_gate'], 'L0_ffn_sh_up': _L0_ffn_in['sh_up'], 'L0_ffn_sh_down': _L0_ffn_in['sh_down'], 'L0_ffn_r_gate': _L0_ffn_in['r_gate'], 'L0_ffn_r_up': _L0_ffn_in['r_up'], 'L0_ffn_r_down': _L0_ffn_in['r_down'], 'L0_ffn_router_w': _L0_ffn_in['router_w'], 'L0_ffn_router_b': _L0_ffn_in['router_b']}

def reference(x, ctx_2048, L0_attn_W_in, L0_attn_conv_w, L0_attn_conv_b, L0_attn_A, L0_attn_D, L0_attn_dt_bias, L0_attn_norm_w, L0_attn_W_out, L0_xattn_Wq, L0_xattn_Wk, L0_xattn_Wv, L0_ffn_ln1_w, L0_ffn_ln2_w, L0_ffn_kv_d_w, L0_ffn_q_d_w, L0_ffn_k_u_w, L0_ffn_v_u_w, L0_ffn_q_u_w, L0_ffn_rope_k_w, L0_ffn_rope_q_w, L0_ffn_o_w, L0_ffn_sh_gate, L0_ffn_sh_up, L0_ffn_sh_down, L0_ffn_r_gate, L0_ffn_r_up, L0_ffn_r_down, L0_ffn_router_w, L0_ffn_router_b):
    import jax
    import jax.numpy as jnp

    def _L0_attn_ref(hidden_states, W_in, conv_w, conv_b, A, D, dt_bias, norm_w, W_out):
        import jax, jax.numpy as jnp
        import numpy as np
        D_MODEL = 256
        EXPAND = 2
        D_INNER = D_MODEL * EXPAND
        HEAD_DIM = 64
        NHEADS = D_INNER // HEAD_DIM
        D_STATE = 128
        NGROUPS = 1
        D_CONV = 4
        CHUNK = 32
        CONV_DIM = D_INNER + 2 * NGROUPS * D_STATE
        D_IN_PROJ = 2 * D_INNER + 2 * NGROUPS * D_STATE + NHEADS
        EPS = 1e-05

        def segsum(x):
            T = x.shape[-1]
            xc = jnp.cumsum(x, axis=-1)
            diff = xc[..., :, None] - xc[..., None, :]
            mask = jnp.tril(jnp.ones((T, T), dtype=bool))
            return jnp.where(mask, diff, -jnp.inf)

        def causal_conv1d(x, w, b):
            K = w.shape[1]
            L = x.shape[1]
            xp = jnp.pad(x, ((0, 0), (K - 1, 0), (0, 0)))
            y = b[None, None, :]
            for k in range(K):
                y = y + xp[:, k:k + L, :] * w[None, None, :, k]
            return jax.nn.silu(y)

        def ssd_chunked(x, dt, A, B, C, Dskip):
            b, l, h, p = x.shape
            g, n = (B.shape[2], B.shape[3])
            c = l // CHUNK
            xc = x.reshape(b, c, CHUNK, h, p)
            dtc = dt.reshape(b, c, CHUNK, h)
            Bh = jnp.repeat(B.reshape(b, c, CHUNK, g, n), h // g, axis=3)
            Ch = jnp.repeat(C.reshape(b, c, CHUNK, g, n), h // g, axis=3)
            dA = dtc * A[None, None, None, :]
            dAc = jnp.moveaxis(dA, 3, 1)
            A_cumsum = jnp.cumsum(dAc, axis=-1)
            Lmat = jnp.exp(segsum(dAc))
            Y_diag = jnp.einsum('bclhn,bcshn,bhcls,bcsh,bcshp->bclhp', Ch, Bh, Lmat, dtc, xc)
            decay_states = jnp.exp(A_cumsum[..., -1:] - A_cumsum)
            states = jnp.einsum('bclhn,bhcl,bclh,bclhp->bchpn', Bh, decay_states, dtc, xc)
            states = jnp.concatenate([jnp.zeros_like(states[:, :1]), states], axis=1)
            chunk_sums = jnp.pad(A_cumsum[..., -1], ((0, 0), (0, 0), (1, 0)))
            decay_chunk = jnp.exp(segsum(chunk_sums))
            new_states = jnp.einsum('bhzc,bchpn->bzhpn', decay_chunk, states)
            states_prev = new_states[:, :-1]
            state_decay_out = jnp.exp(A_cumsum)
            Y_off = jnp.einsum('bclhn,bchpn,bhcl->bclhp', Ch, states_prev, state_decay_out)
            Y = (Y_diag + Y_off).reshape(b, l, h, p) + x * Dskip[None, None, :, None]
            return Y

        def gated_rmsnorm(y, z, w):
            x = y * jax.nn.silu(z)
            gs = D_INNER // NGROUPS
            xg = x.reshape(x.shape[:-1] + (NGROUPS, gs))
            var = jnp.mean(xg * xg, axis=-1, keepdims=True)
            xg = xg * jax.lax.rsqrt(var + EPS)
            return xg.reshape(x.shape) * w[None, None, :]
        b, l, _ = hidden_states.shape
        zxbcdt = hidden_states @ W_in
        z = zxbcdt[..., :D_INNER]
        xbc = zxbcdt[..., D_INNER:D_INNER + CONV_DIM]
        dt = zxbcdt[..., D_INNER + CONV_DIM:]
        xbc = causal_conv1d(xbc, conv_w, conv_b)
        x = xbc[..., :D_INNER].reshape(b, l, NHEADS, HEAD_DIM)
        Bs = xbc[..., D_INNER:D_INNER + NGROUPS * D_STATE].reshape(b, l, NGROUPS, D_STATE)
        Cs = xbc[..., D_INNER + NGROUPS * D_STATE:].reshape(b, l, NGROUPS, D_STATE)
        dt = jax.nn.softplus(dt + dt_bias[None, None, :])
        y = ssd_chunked(x, dt, A, Bs, Cs, D).reshape(b, l, D_INNER)
        y = gated_rmsnorm(y, z, norm_w)
        return y @ W_out

    def _L0_xattn_ref(x, context, Wq, Wk, Wv):
        import jax, jax.numpy as jnp
        import numpy as np
        DIM = 256
        NHEADS = 32
        HEAD_DIM = DIM // NHEADS
        EPS = 1e-06

        def _rmsnorm(t):
            return t * jax.lax.rsqrt(jnp.mean(t * t, axis=-1, keepdims=True) + EPS)
        b, n, _ = x.shape
        m = context.shape[1]
        q = x @ Wq.T
        k_raw = context @ Wk.T
        v_raw = context @ Wv.T
        q = q.reshape(b, n, NHEADS, HEAD_DIM).transpose(0, 2, 1, 3)
        kv = jnp.concatenate([k_raw, v_raw], axis=-1)
        kv = kv.reshape(b, m, NHEADS, HEAD_DIM, 2)
        k = kv[..., 0].transpose(0, 2, 1, 3)
        v = kv[..., 1].transpose(0, 2, 1, 3)
        q = _rmsnorm(q)
        k = _rmsnorm(k)
        scale = HEAD_DIM ** (-0.5)
        scores = jnp.einsum('bhnd,bhmd->bhnm', q, k) * scale
        attn = jax.nn.softmax(scores, axis=-1)
        out = jnp.einsum('bhnm,bhmd->bhnd', attn, v)
        return out.transpose(0, 2, 1, 3).reshape(b, n, NHEADS * HEAD_DIM)

    def _L0_ffn_ref(x, ln1_w, ln2_w, kv_d_w, q_d_w, k_u_w, v_u_w, q_u_w, rope_k_w, rope_q_w, o_w, sh_gate, sh_up, sh_down, r_gate, r_up, r_down, router_w, router_b):
        import jax, jax.numpy as jnp
        import numpy as np
        B, S, H = (4, 128, 256)
        NH = 16
        HD = H // NH
        RD = HD // 2
        LAT = H // 4
        I = 128
        NE = 8
        NSH = 1
        NR = NE - NSH
        TOPK = 2
        EPS = 1e-05
        SCALING = 8.0

        def _w(key, shape, fan_in):
            return jax.random.normal(key, shape, dtype=jnp.float32) / np.sqrt(fan_in)

        def rmsnorm(x, w):
            rms = jax.lax.rsqrt(jnp.mean(x * x, axis=-1, keepdims=True) + EPS)
            return w * rms * x

        def rope_cos_sin(seq_len):
            inv_freq = 1.0 / 10000.0 ** (jnp.arange(0, RD, 2, dtype=jnp.float32) / RD)
            t = jnp.arange(seq_len, dtype=jnp.float32)
            ang = jnp.outer(t, inv_freq)
            emb = jnp.concatenate([ang, ang], axis=-1)
            return (jnp.cos(emb), jnp.sin(emb))

        def apply_rope(x, cos, sin):
            c = cos[None, :, None, :]
            s = sin[None, :, None, :]
            x1, x2 = jnp.split(x, 2, axis=-1)
            rot = jnp.concatenate([-x2, x1], axis=-1)
            return x * c + rot * s

        def expert_ffn(x, wg, wu, wd):
            h = jax.nn.silu(x @ wg) * (x @ wu) / SCALING
            return h @ wd

        def attention(x, kv_d_w, q_d_w, k_u_w, v_u_w, q_u_w, rope_k_w, rope_q_w, o_w):
            b, s, _ = x.shape
            kv_d = x @ kv_d_w
            q_d = x @ q_d_w
            k_p = (kv_d @ k_u_w).reshape(b, s, NH, RD)
            q_p = (q_d @ q_u_w).reshape(b, s, NH, RD)
            v = (kv_d @ v_u_w).reshape(b, s, NH, HD)
            k_r = (x @ rope_k_w).reshape(b, s, NH, RD)
            q_r = (q_d @ rope_q_w).reshape(b, s, NH, RD)
            cos, sin = rope_cos_sin(s)
            k_r = apply_rope(k_r, cos, sin)
            q_r = apply_rope(q_r, cos, sin)
            k = jnp.concatenate([k_p, k_r], axis=-1)
            q = jnp.concatenate([q_p, q_r], axis=-1)
            scale = 1.0 / np.sqrt(HD)
            scores = jnp.einsum('bqhd,bkhd->bhqk', q, k) * scale
            causal = jnp.tril(jnp.ones((s, s), dtype=bool))
            scores = jnp.where(causal[None, None], scores, jnp.finfo(scores.dtype).min)
            probs = jax.nn.softmax(scores, axis=-1)
            out = jnp.einsum('bhqk,bkhd->bqhd', probs, v).reshape(b, s, H)
            return out @ o_w

        def moe(x, sh_gate, sh_up, sh_down, r_gate, r_up, r_down, router_w, router_b):
            shared = expert_ffn(x, sh_gate, sh_up, sh_down)
            logits = x @ router_w + router_b
            probs = jax.nn.sigmoid(logits)
            scores, idx = jax.lax.top_k(probs, TOPK)
            scores = scores / jnp.sum(scores, axis=-1, keepdims=True)
            w = jnp.sum(jax.nn.one_hot(idx, NR, dtype=x.dtype) * scores[..., None], axis=-2)
            combined = jnp.zeros_like(x)
            for e in range(NR):
                combined = combined + w[..., e:e + 1] * expert_ffn(x, r_gate[e], r_up[e], r_down[e])
            return shared + combined
        h = x + attention(rmsnorm(x, ln1_w), kv_d_w, q_d_w, k_u_w, v_u_w, q_u_w, rope_k_w, rope_q_w, o_w)
        out = h + moe(rmsnorm(h, ln2_w), sh_gate, sh_up, sh_down, r_gate, r_up, r_down, router_w, router_b)
        return out
    x = x + _L0_attn_ref(_layernorm(x, axis=-1), L0_attn_W_in, L0_attn_conv_w, L0_attn_conv_b, L0_attn_A, L0_attn_D, L0_attn_dt_bias, L0_attn_norm_w, L0_attn_W_out)
    x = x + _L0_xattn_ref(_layernorm(x, axis=-1), ctx_2048, L0_xattn_Wq, L0_xattn_Wk, L0_xattn_Wv)
    x = x + _L0_ffn_ref(_layernorm(x, axis=-1), L0_ffn_ln1_w, L0_ffn_ln2_w, L0_ffn_kv_d_w, L0_ffn_q_d_w, L0_ffn_k_u_w, L0_ffn_v_u_w, L0_ffn_q_u_w, L0_ffn_rope_k_w, L0_ffn_rope_q_w, L0_ffn_o_w, L0_ffn_sh_gate, L0_ffn_sh_up, L0_ffn_sh_down, L0_ffn_r_gate, L0_ffn_r_up, L0_ffn_r_down, L0_ffn_router_w, L0_ffn_router_b)
    return x

_drawn_inputs = setup_inputs


def setup_inputs(seed=0):
    import zlib

    import numpy as np

    out = dict(_drawn_inputs(seed))
    spreads = {'L0_ffn_ln1_w': (1.0, 0.6), 'L0_ffn_ln2_w': (1.0, 0.6), 'L0_ffn_router_b': (0.0, 2.0)}
    factors = {'L0_attn_A': 200.0,
     'L0_attn_dt_bias': 5.431,
     'L0_attn_norm_w': 63.377,
     'L0_xattn_Wq': 25.84,
     'ctx_2048': 3.28,
     'L0_xattn_Wk': 3.982,
     'L0_xattn_Wv': 3.83,
     'L0_ffn_sh_gate': 3.373,
     'L0_ffn_sh_up': 3.068,
     'L0_ffn_sh_down': 3.049,
     'L0_ffn_r_gate': 4.681,
     'L0_ffn_r_up': 4.284,
     'L0_ffn_r_down': 4.219,
     'L0_ffn_router_w': 6.439}
    for name, (base, spread) in spreads.items():
        noise = np.random.default_rng([zlib.crc32(name.encode()), seed]).standard_normal(out[name].shape)
        drawn = base * np.exp(spread * noise) if base else spread * noise
        out[name] = jnp.asarray(drawn.astype(out[name].dtype))
    for name, factor in factors.items():
        out[name] = (out[name] * factor).astype(out[name].dtype)
    return out
```

```python
from contextlib import ExitStack

import numpy as np

import concourse.bass as bass
from concourse import mybir

F32 = mybir.dt.float32
BF16 = mybir.dt.bfloat16
ALU = mybir.AluOpType
ACT = mybir.ActivationFunctionType
AX = mybir.AxisListType

P = 128
NB, SEQ, D = 4, 256, 256
T = SEQ // P
KD = D // P
DI, NHM, HP, NS = 512, 8, 64, 128
XF = DI // P
CF = XF + 2
TAPS = 4
WIN = 2 * DI + 2 * NS + NHM
XH, XD = 32, 8
AH, AR, AD = 16, 8, 16
LAT, NE, NR, FI = 64, 8, 7, 128
LN_EPS, X_EPS, RMS_EPS, GATE_EPS = 1e-5, 1e-6, 1e-5, 1e-5
NEG = -1e30

PACKS = {
    "mix": [("w_in", KD * WIN), ("conv_w", CF * TAPS), ("conv_b", CF), ("norm_w", XF), ("a", NHM), ("dt_bias", NHM),
            ("d_skip", XF), ("w_out", XF * D)],
    "cross": [("wq", KD * D), ("wk", KD * D), ("wv", KD * D)],
    "latent": [("ln1", KD), ("ln2", KD), ("down", KD * P), ("rope_k", KD * P), ("up", P), ("second", D),
               ("o_w", KD * D), ("router", KD * NR), ("router_b", NR)],
    "experts": [("gate_up", NE * KD * 2 * FI), ("down_w", NE * D)],
    "shape": [("ident", P), ("upto", P), ("after", P), ("block8", P), ("rope", 2 * SEQ), ("before", NR * NR)],
}
WIDTH = {pack: sum(n for _, n in parts) for pack, parts in PACKS.items()}

MIX = ["ln1", "dt", "inx", "cs", "inz", "ssd0", "ssd1", "out"]
CROSS_KV = ["ctx", "xk", "xv"]
CROSS = ["ln2", "xq"] + [f"x{n}" for n in range(8)]
SELF = ["ln3", "proj", "fk", "fq"] + [f"max{n}" for n in range(6)] + ["maxT"] + [f"f{n}" for n in range(4)] + ["oproj"]
MOE = ["ln4", "router"] + [f"e{n}" for n in range(NE)] + ["store"]


def schedule():
    order = []
    for b in range(NB):
        for s in MIX + CROSS_KV + CROSS + SELF + MOE:
            order.append((s, b))
    return order


SCHEDULE = schedule()

WORK = {
    "ln1": [("xnT", 1, 0)], "dt": [("dt_raw", 1, 0)], "inx": [("taps", 6, 2 * i + 1) for i in range(3)],
    "cs": [("ecs", 1, 0)], "inz": [("sz", 2, i) for i in range(2)],
    "ssd0": [("gm", 2, 0), ("dtx", 2, 0), ("state", 1, 0), ("y", 2, 0)],
    "ssd1": [("gm", 2, 1), ("dtx", 2, 1), ("yoff", 1, 0), ("y", 2, 1)],
    "out": [("gate_ln", 1, 0), ("x1", 1, 0)],
    "ctx": [("ctxT", 1, 0)], "xk": [("xk_full", 1, 0), ("xk_ln", 1, 0)], "xv": [("xv", 1, 0)],
    "ln2": [("xnT2", 1, 0)], "xq": [("xq_full", 1, 0), ("xq_ln", 1, 0)],
    "x2": [("xo", 3, 0)], "x5": [("xo", 3, 1)], "x7": [("xo", 3, 2)],
    "ln3": [("xnT3", 1, 0)],
    "proj": [("lat", 1, 0), ("k_rope", 1, 0), ("plain", 2, 0), ("plain", 2, 1), ("q_rope", 1, 0), ("fv", 1, 0)],
    "maxT": [("maxT", 1, 0)],
    **{f"f{n}": [("ao", 4, n)] for n in range(4)},
    "oproj": [("aoT", 1, 0), ("h", 1, 0)],
    "ln4": [("hT", 1, 0)], "router": [("logits", 1, 0)],
    **{f"e{n}": [("hidden", NE, n), ("acc", NE, n)] for n in range(NE)},
}
PAIR = {
    "ssd0": [("L", 2, 0)], "ssd1": [("L", 2, 1)],
    **{f"x{n}": [("xp", 16, 2 * n + i) for i in range(2)] for n in range(8)},
    **{f"max{n}": [("mx", 6, n)] for n in range(6)},
    **{f"f{n}": [("fp", 8, 2 * n + i) for i in range(2)] for n in range(4)},
}
OUTS = {
    "x0": [("xot", 3, 0)], "x3": [("xot", 3, 1)], "x6": [("xot", 3, 2)],
    **{f"f{n}": [("fot", 4, n)] for n in range(4)},
}


def plan(claims, slots):
    given, last, n = {}, [None] * slots, 0
    for step, b in SCHEDULE:
        for i, (name, per, k) in enumerate(claims.get(step, [])):
            given[step, b, i] = (n % slots, last[n % slots])
            last[n % slots] = (name, b * per + k + 1)
            n += 1
    return given


PROBS = {
    **{f"x{n}": [("xo_quad", 8, n)] * 2 for n in range(8)},
    **{f"f{n}": [("fo_ps", 4, n)] * 2 for n in range(4)},
}
PX = 4
SHARED = {
    "xn_0": {"ln1": [("xnT_ps", 1, 0)], "ln3": [("xnT3_ps", 1, 0)]},
    "xn_1": {"ln2": [("xnT2_ps", 1, 0)], "ln4": [("hT_ps", 1, 0)]},
    "full_k": {"xk": [("xk_diffs", 2, 1)], "proj": [("fk_diffs", 2, 1)]},
    "full_q": {"xq": [("xq_diffs", 2, 1)], "proj": [("fq_diffs", 2, 1)]},
    "parts_k": {"xk": [("xk_to_dram", 96, 95)], "fk": [("fk_to_dram", 96, 95)]},
    "parts_q": {"xq": [("xq_to_dram", 96, 95)], "fq": [("fq_to_dram", 96, 95)]},
}
SHARED_AT = {name: plan(claims, 1) for name, claims in SHARED.items()}
WORK_AT, PAIR_AT, OUT_AT, PROB_AT = plan(WORK, 3), plan(PAIR, 2), plan(OUTS, 2), plan(PROBS, PX)


def decoder_layer(nc, x, ctx_in, packs, masks16, out):
    stack = ExitStack()
    with stack:
        def sb(name, shape, dt=F32):
            return stack.enter_context(nc.sbuf_tensor(name, shape, dt))

        class Semaphores(dict):
            def __missing__(self, name):
                self[name] = stack.enter_context(nc.semaphore("s_" + name))
                return self[name]

        s = Semaphores()
        dram = [[nc.dram_tensor(f"scratch_{kind}_{b}", [XH, 3, XD, SEQ], BF16, kind="Internal").ap()
                 for kind in ("xk", "xq", "fk", "fq")] for b in range(NB)]
        KIND = {"xk": 0, "xq": 1, "fk": 2, "fq": 3}

        def after_last_user(engine, table, step, b, i=0):
            before_us = table[step, b, i][1]
            if before_us is not None:
                engine.wait_ge(s[before_us[0]], before_us[1])

        work_ps = [stack.enter_context(nc.psum_tensor(f"work{i}", [P, 512], F32)) for i in range(3)]
        pair_ps = [stack.enter_context(nc.psum_tensor(f"pair{i}", [P, 1024], F32)) for i in range(2)]
        outs_ps = stack.enter_context(nc.psum_tensor("outs", [P, 512], F32))

        def work(step, b, i=0):
            return work_ps[WORK_AT[step, b, i][0]]

        def pair(step, b, i=0):
            return pair_ps[PAIR_AT[step, b, i][0]]

        def outs(step, b):
            k = OUT_AT[step, b, 0][0]
            return outs_ps[:, k * 256:(k + 1) * 256]

        w = {name: sb("w_" + name, [P, n]) for name, n in WIDTH.items()}

        def part(pack, name):
            at = 0
            for n, width in PACKS[pack]:
                if n == name:
                    return w[pack][:, at:at + width]
                at += width
            raise KeyError(name)

        w_in = part("mix", "w_in").rearrange("p (k n) -> p k n", k=KD)
        conv_w, conv_b, d_skip = part("mix", "conv_w"), part("mix", "conv_b"), part("mix", "d_skip")
        norm_w, a_row, dt_bias = part("mix", "norm_w"), part("mix", "a"), part("mix", "dt_bias")
        w_out = part("mix", "w_out").rearrange("p (f n) -> p f n", f=XF)
        wq, wk, wv = (part("cross", n).rearrange("p (k n) -> p k n", k=KD) for n in ("wq", "wk", "wv"))
        ln1_w, ln2_w = part("latent", "ln1"), part("latent", "ln2")
        w_down = part("latent", "down").rearrange("p (k n) -> p k n", k=KD)
        w_rope_k = part("latent", "rope_k").rearrange("p (k n) -> p k n", k=KD)
        w_up, w_second = part("latent", "up"), part("latent", "second")
        w_o = part("latent", "o_w").rearrange("p (k n) -> p k n", k=KD)
        w_router = part("latent", "router").rearrange("p (k n) -> p k n", k=KD)
        router_b = part("latent", "router_b")
        gate_up = part("experts", "gate_up").rearrange("p (e k g n) -> p e k g n", e=NE, k=KD, g=2)
        down_w = part("experts", "down_w").rearrange("p (e n) -> p e n", e=NE)
        ident, upto, after, block8 = (part("shape", n) for n in ("ident", "upto", "after", "block8"))
        rope_cs = part("shape", "rope")
        before = part("shape", "before").rearrange("p (e j) -> p e j", e=NR)
        m16 = sb("m16", [P, 3, P], BF16)
        ident16, mask_q, mask_k = m16[:, 0, :], m16[:, 1, :], m16[:, 2, :]
        ones = sb("ones", [P, 1])
        eps = sb("eps", [P, 3])
        w_rope_k2 = sb("w_rope_k2", [P, KD, P])
        w_rope_q2 = sb("w_rope_q2", [P, P])

        def per_batch(name, shape, dt=F32, n=NB):
            tiles = [sb(f"{name}_{i}", shape, dt) for i in range(n)]
            return [tiles[b % n] for b in range(NB)]

        NF = 3
        x0 = per_batch("x0", [P, T, D], n=NF)
        ctx_t = per_batch("ctx", [P, T, D], n=1)
        stats = per_batch("stats", [P, 4, T, 6], n=2)
        mv = per_batch("mv", [P, 4, T, 2])
        rstd = per_batch("rstd", [P, 6, T])
        xn = [sb(f"xn{i}", [P, T, D]) for i in range(2)]
        xnT = per_batch("xnT", [P, KD, SEQ], n=2)
        conv = per_batch("conv", [P, CF, SEQ], n=1)
        xbc = conv
        sz = per_batch("sz", [P, XF, SEQ], n=1)
        sp = per_batch("sp", [P, 8, T * NHM], n=2)
        dt_t = per_batch("dt", [P, T, NHM])
        dA = per_batch("dA", [P, T, NHM])
        ecs = per_batch("ecs", [P, T, 2, NHM], n=2)
        R = per_batch("R", [P, NHM, P], n=1)
        L = per_batch("L", [P, NHM, P], n=1)
        Gm = per_batch("Gm", [P, P], n=1)
        btok = per_batch("btok", [P, P], n=1)
        dtx = per_batch("dtx", [P, DI], n=1)
        dtxd = per_batch("dtxd", [P, DI], n=1)
        state = per_batch("state", [P, DI], n=1)
        yoff = dtxd
        yg = per_batch("yg", [P, XF, SEQ], n=1)
        xD = yg
        ysq = sz
        x1 = per_batch("x1", [P, T, D], n=NF)
        ctxT = per_batch("ctxT", [P, KD, SEQ], n=1)
        rs = {k: sb("rs_" + k, [P, 512]) for k in ("xk", "xq")}
        full = {k: sb("full_" + k, [P, 512]) for k in ("xk", "xq")}
        full["fk"], full["fq"] = full["xk"], full["xq"]
        parts = {k: sb("parts_" + k, [P, 2, 3, SEQ], BF16) for k in ("xk", "xq")}
        parts["fk"], parts["fq"] = parts["xk"], parts["xq"]
        NST = 1
        xstack = {k: per_batch("stack_" + k, [P, XH // 2, SEQ], BF16, n=NST) for k in ("xk", "xq")}
        fstack = {k: per_batch("stack_" + k, [P, AH, SEQ], BF16, n=NST) for k in ("fk", "fq")}
        xvals = per_batch("xvals", [P, T, XH, 32], n=1)
        fvals = per_batch("fvals", [P, T, AH, 32], n=1)
        probs_sb = [sb(f"probs{i}", [P, 2, 512]) for i in range(PX)]

        def probs(step, b, i):
            return probs_sb[PROB_AT[step, b, i][0]]

        xot = per_batch("xot", [P, SEQ], n=1)
        xden = per_batch("xden", [P, T, 12], n=1)
        x2 = per_batch("x2", [P, T, D], n=2)
        y3 = x1
        lat = per_batch("lat", [P, SEQ], n=1)
        rope_t = sb("rope_t", [P, 2, SEQ])
        fmx = per_batch("fmx", [P, T, AH])
        fmr = per_batch("fmr", [P, T * AH])
        fmp = per_batch("fmp", [P, T, 3, AH], BF16, n=2)
        maxT = per_batch("maxT", [3 * AH, SEQ], BF16, n=1)
        fot = per_batch("fot", [P, SEQ], n=1)
        fden = per_batch("fden", [P, T, 4], n=1)
        ao = per_batch("ao", [P, T, D], n=1)
        aoT = per_batch("aoT", [P, KD, SEQ], n=1)
        h4 = x1
        hT = per_batch("hT", [P, KD, SEQ], n=1)
        rt = per_batch("rt", [P, 6, T, NR], n=2)
        cmp_ = per_batch("cmp", [P, 2, T, NR * NR], n=1)
        rsum = per_batch("rsum", [P, 2, T])
        gates = per_batch("gates", [P, T, NR])
        sg = per_batch("sg", [P, SEQ], n=2)
        hid = sg
        acc = x0

        block = stack.enter_context(nc.Block())

        @block.sync
        def _(sync):
            x_d = x.rearrange("b (t p) d -> b p t d", p=P)
            c_d = ctx_in.rearrange("b (t p) d -> b p t d", p=P)
            out_d = out.rearrange("b (t p) d -> b p t d", p=P)
            sync.dma_start(x0[0][:], x_d[0]).then_inc(s["x_in_first"], 16)
            for name in ("shape", "mix"):
                sync.dma_start(w[name][:], packs[name]).then_inc(s["w_first"], 16)
            for b in range(1, NF):
                sync.dma_start(x0[b][:], x_d[b]).then_inc(s["x_in"], 16)
            sync.dma_start(ctx_t[0][:], c_d[0]).then_inc(s["ctx_in"], 16)
            sync.dma_start(m16[:], masks16).then_inc(s["w_second"], 16)
            for name in ("cross", "latent"):
                sync.dma_start(w[name][:], packs[name]).then_inc(s["w_second"], 16)
            sync.dma_start(w["experts"][:], packs["experts"]).then_inc(s["w_experts"], 16)

            def ctx(b):
                if b + 1 < NB:
                    sync.wait_ge(s["ctxT"], b + 1)
                    sync.dma_start(ctx_t[b + 1][:], c_d[b + 1]).then_inc(s["ctx_in"], 16)

            def split(kind, b, stack_tile, used):
                d = dram[b][KIND[kind]]
                for half in range(2):
                    for g in range(3):
                        if g < 2:
                            sync.wait_ge(s[f"{kind}_rounded"], 2 * b + g + 1)
                        else:
                            sync.wait_ge(s[f"{kind}_diffs"], 2 * b + 2)
                        sync.dma_start(d[16 * half:16 * half + 16, g], parts[kind][:, half, g, :])\
                            .then_inc(s[f"{kind}_to_dram"], 16)
                sync.wait_ge(s[f"{kind}_to_dram"], 16 * 6 * (b + 1))
                if b >= NST:
                    sync.wait_ge(s[used[0]], used[1] * (b - NST + 1))
                elif kind == "fk":
                    sync.wait_ge(s["pool_init"], NST)
                if kind[1] == "k":
                    runs = [((0, 3), 0), ((0, 2), 24), ((0, 1), 40)]
                else:
                    runs = [(0, 0), (0, 8), (0, 16), (1, 24), (1, 32), (2, 40)]
                for a in range(2):
                    if kind[0] == "x":
                        src = d.rearrange("(q a) g d t -> a g d q t", a=2)[a]
                        row = 64 * a
                    else:
                        src = d.rearrange("(a q) g d t -> a g d q t", a=2)[a]
                        row = 48 * a
                    for run, base in runs:
                        if kind[1] == "k":
                            n = run[1]
                            sr = src[0:n].rearrange("g d q t -> (g d) q t")
                        else:
                            n, sr = 1, src[run]
                        sync.dma_start(stack_tile[row + base:row + base + 8 * n, :, :], sr)\
                            .then_inc(s[f"{kind}_stack"], 16)

            def maxes(b):
                sync.wait_ge(s["maxT"], b + 1)
                for c in range(3):
                    sync.dma_start(fstack["fq"][b][96 + c:97 + c, :, :], maxT[b][AH * c:AH * c + AH, :])\
                        .then_inc(s["max_stack"], 16)

            def store(b):
                sync.wait_ge(s["acc"], NE * (b + 1))
                sync.dma_start(out_d[b], acc[b][:]).then_inc(s["stored"], 16)
                if b + NF < NB:
                    sync.wait_ge(s["stored"], 16 * (b + 1))
                    sync.dma_start(x0[b + NF][:], x_d[b + NF]).then_inc(s["x_in"], 16)

            steps = {"ctx": ctx, "xk": lambda b: split("xk", b, xstack["xk"][b], ("xs_ps", 16)),
                     "xq": lambda b: split("xq", b, xstack["xq"][b], ("xs_ps", 16)),
                     "fk": lambda b: split("fk", b, fstack["fk"][b], ("fs_ps", 8)),
                     "fq": lambda b: split("fq", b, fstack["fq"][b], ("fs_ps", 8)),
                     "maxT": maxes, "store": store}
            for step, b in SCHEDULE:
                if step in steps:
                    steps[step](b)
            sync.wait_ge(s["stored"], 16 * NB)

        RUNS = {"xk": 6, "xq": 12, "fk": 6, "fq": 12}

        @block.tensor
        def _(pe):
            mm = nc.tensor.matmul

            def claim(table, step, b, i=0):
                after_last_user(pe, table, step, b, i)

            def transposes(step, b, ready, src, done):
                pe.wait_ge(s[ready], b + 1)
                claim(WORK_AT, step, b)
                ps = work(step, b)
                for k in range(KD):
                    for t in range(T):
                        last = nc.tensor.transpose(ps[:, k * SEQ + t * P:k * SEQ + (t + 1) * P],
                                                   src[:, t, k * P:(k + 1) * P], ident)
                last.then_inc(s[done], 1)

            def ln1(b):
                if b == 0:
                    pe.wait_ge(s["w_first"], 32)
                transposes("ln1", b, "xn", xn[0], "xnT_ps")

            def dt(b):
                pe.wait_ge(s["xnT"], b + 1)
                claim(WORK_AT, "dt", b)
                for t in range(T):
                    for k in range(KD):
                        last = mm(work("dt", b)[:, t * NHM:(t + 1) * NHM], xnT[b][:, k, t * P:(t + 1) * P],
                                  w_in[:, k, WIN - NHM:WIN], start=k == 0, stop=k == KD - 1)
                last.then_inc(s["dt_ps"], 1)

            def project(step, b, i, first, done):
                claim(WORK_AT, step, b, i)
                for f in range(2):
                    for k in range(KD):
                        last = mm(work(step, b, i)[:, f * SEQ:(f + 1) * SEQ],
                                  w_in[:, k, first + f * P:first + (f + 1) * P], xnT[b][:, k, :],
                                  start=k == 0, stop=k == KD - 1)
                last.then_inc(s[done], 1)

            def inx(b):
                for i in range(CF // 2):
                    project("inx", b, i, DI + 2 * i * P, "xbc_ps")

            def inz(b):
                for i in range(XF // 2):
                    project("inz", b, i, 2 * i * P, "z_ps")

            def cs(b):
                pe.wait_ge(s["dA"], b + 1)
                claim(WORK_AT, "cs", b)
                for t in range(T):
                    o = work("cs", b)[:, t * 2 * NHM:(t + 1) * 2 * NHM]
                    mm(o[:, 0:NHM], upto, dA[b][:, t, :], start=True, stop=True)
                    last = mm(o[:, NHM:2 * NHM], after, dA[b][:, t, :], start=True, stop=True)
                last.then_inc(s["cs_ps"], 1)

            def ssd(t, b):
                step, tok, n = f"ssd{t}", slice(t * P, (t + 1) * P), T * b + t
                pe.wait_ge(s["xbc"], b + 1)
                claim(WORK_AT, step, b, 0)
                g = work(step, b, 0)
                last = mm(g[:, 0:P], xbc[b][:, XF, tok], xbc[b][:, XF + 1, tok], start=True, stop=True)
                if t == 0:
                    last = nc.tensor.transpose(g[:, P:2 * P], xbc[b][:, XF, tok], ident)
                last.then_inc(s["g_ps"], 1)
                claim(WORK_AT, step, b, 1)
                for f in range(XF):
                    last = nc.tensor.transpose(work(step, b, 1)[:, f * P:(f + 1) * P], xbc[b][:, f, tok], ident)
                last.then_inc(s["xtok_ps"], 1)
                pe.wait_ge(s["R"], n + 1)
                claim(PAIR_AT, step, b)
                for i in range(2):
                    last = mm(pair(step, b)[:, 512 * i:512 * (i + 1)], after, R[b][:, 4 * i:4 * i + 4, :],
                              start=True, stop=True)
                last.then_inc(s["diff_ps"], 1)
                claim(WORK_AT, step, b, 2)
                if t == 0:
                    pe.wait_ge(s["dtxd"], b + 1)
                    mm(work(step, b, 2)[:, :], btok[b][:, :], dtxd[b][:, :], start=True, stop=True)\
                        .then_inc(s["state_ps"], 1)
                else:
                    pe.wait_ge(s["state"], b + 1)
                    mm(work(step, b, 2)[:, :], xbc[b][:, XF + 1, tok], state[b][:, :], start=True, stop=True)\
                        .then_inc(s["yoff_ps"], 1)
                pe.wait_ge(s["M"], n + 1)
                pe.wait_ge(s["dtx"], n + 1)
                if t == 1:
                    pe.wait_ge(s["yoff"], b + 1)
                claim(WORK_AT, step, b, 3)
                y = work(step, b, 3)
                for hp in range(XF):
                    for a in range(2):
                        head = 2 * hp + a
                        last = mm(y[64 * a:64 * a + 64, hp * P:(hp + 1) * P], dtx[b][:, head * HP:(head + 1) * HP],
                                  L[b][:, head, :], start=True, stop=t == 0)
                    if t == 1:
                        last = mm(y[:, hp * P:(hp + 1) * P], yoff[b][:, hp * P:(hp + 1) * P], ident,
                                  start=False, stop=True)
                last.then_inc(s["y_ps"], 1)

            def out_proj(b):
                pe.wait_ge(s["ysum"], b + 1)
                claim(WORK_AT, "out", b, 0)
                for t in range(T):
                    last = mm(work("out", b, 0)[:, t:t + 1], ysq[b][:, 0, t * P:(t + 1) * P], ones[:, :],
                              start=True, stop=True)
                last.then_inc(s["ss_ps"], 1)
                if b == 0:
                    pe.wait_ge(s["w_norm_out"], XF)
                claim(WORK_AT, "out", b, 1)
                for t in range(T):
                    for f in range(XF):
                        last = mm(work("out", b, 1)[:, t * D:(t + 1) * D], yg[b][:, f, t * P:(t + 1) * P],
                                  w_out[:, f, :], start=f == 0, stop=f == XF - 1)
                last.then_inc(s["out_ps"], 1)

            def ctx(b):
                if b == 0:
                    pe.wait_ge(s["w_second"], 48)
                pe.wait_ge(s["ctx_in"], 16 * (b + 1))
                claim(WORK_AT, "ctx", b)
                for k in range(KD):
                    for t in range(T):
                        last = nc.tensor.transpose(work("ctx", b)[:, k * SEQ + t * P:k * SEQ + (t + 1) * P],
                                                   ctx_t[b][:, t, k * P:(k + 1) * P], ident)
                last.then_inc(s["ctxT_ps"], 1)

            def normed_heads(kind, b, weight, src, src_ready):
                pe.wait_ge(s[src_ready], b + 1)
                claim(WORK_AT, kind, b, 0)
                for f in range(2):
                    for k in range(KD):
                        last = mm(work(kind, b, 0)[:, f * SEQ:(f + 1) * SEQ], weight[:, k, f * P:(f + 1) * P],
                                  src[b][:, k, :], start=k == 0, stop=k == KD - 1)
                last.then_inc(s[f"{kind}_ps"], 1)
                pe.wait_ge(s[f"{kind}_sq"], b + 1)
                claim(WORK_AT, kind, b, 1)
                mm(work(kind, b, 1)[:, :], block8, full[kind][:, :], start=True, stop=True)\
                    .then_inc(s[f"{kind}_sum"], 1)

            def xv(b):
                claim(WORK_AT, "xv", b)
                for t in range(T):
                    for k in range(KD):
                        last = mm(work("xv", b)[:, t * D:(t + 1) * D], ctxT[b][:, k, t * P:(t + 1) * P], wv[:, k, :],
                                  start=k == 0, stop=k == KD - 1)
                last.then_inc(s["xv_ps"], 1)

            def x_scores(b, n):
                step = f"x{n}"
                if n == 0:
                    pe.wait_ge(s["xk_stack"], 16 * RUNS["xk"] * (b + 1))
                    pe.wait_ge(s["xq_stack"], 16 * RUNS["xq"] * (b + 1))
                for i in range(2):
                    q = 2 * n + i
                    claim(PAIR_AT, step, b, i)
                    for a in range(2):
                        rows = slice(64 * a, 64 * a + 6 * XD)
                        for kt in range(T):
                            last = mm(pair(step, b, i)[:, a * 512 + kt * SEQ:a * 512 + (kt + 1) * SEQ],
                                      xstack["xk"][b][rows, q, kt * P:(kt + 1) * P], xstack["xq"][b][rows, q, :],
                                      start=True, stop=True)
                    last.then_inc(s["xs_ps"], 1)

            def x_values(b, n):
                rnd, i = n // 3, n % 3
                q = 16 * b + 2 * n
                if n == 0:
                    pe.wait_ge(s["xv"], b + 1)
                if i == 0:
                    claim(OUT_AT, f"x{3 * rnd}", b)
                pe.wait_ge(s["xp"], q + 2)
                o = outs(f"x{3 * rnd}", b)
                end = min(2, 7 - 3 * rnd)
                for kt in range(T):
                    for j in range(4):
                        head = 4 * n + j
                        last = mm(o[32 * j:32 * j + 32, :], xvals[b][:, kt, head, :],
                                  probs(f"x{n}", b, j // 2)[:, j % 2, kt * SEQ:(kt + 1) * SEQ],
                                  start=i == 0 and kt == 0, stop=i == end and kt == T - 1)
                last.then_inc(s["xo_quad"], 1)

            def x_back(b, rnd):
                step = ("x2", "x5", "x7")[rnd]
                pe.wait_ge(s["xot"], 3 * b + rnd + 1)
                claim(WORK_AT, step, b)
                for t in range(T):
                    last = nc.tensor.transpose(work(step, b)[:, t * P:(t + 1) * P], xot[b][:, t * P:(t + 1) * P],
                                               ident)
                last.then_inc(s["xback_ps"], 1)

            def cross(b, n):
                x_scores(b, n)
                x_values(b, n)
                if n in (2, 5, 7):
                    x_back(b, (2, 5, 7).index(n))

            def proj(b):
                if b == 0:
                    pe.wait_ge(s["pool_init"], NST + 10)
                pe.wait_ge(s["xnT3"], b + 1)
                claim(WORK_AT, "proj", b, 0)
                for k in range(KD):
                    last = mm(work("proj", b, 0)[:, 0:SEQ], w_down[:, k, :], xnT[b][:, k, :],
                              start=k == 0, stop=k == KD - 1)
                last.then_inc(s["lat_ps"], 1)
                claim(WORK_AT, "proj", b, 1)
                for i, weight in enumerate((w_rope_k, w_rope_k2)):
                    for k in range(KD):
                        last = mm(work("proj", b, 1)[:, i * SEQ:(i + 1) * SEQ], weight[:, k, :], xnT[b][:, k, :],
                                  start=k == 0, stop=k == KD - 1)
                last.then_inc(s["kr_ps"], 1)
                pe.wait_ge(s["lat"], b + 1)
                claim(WORK_AT, "proj", b, 2)
                kv, qd = slice(0, LAT), slice(LAT, 2 * LAT)
                mm(work("proj", b, 2)[:, 0:SEQ], w_up[kv, :], lat[b][kv, :], start=True, stop=True)\
                    .then_inc(s["plain_ps"], 1)
                claim(WORK_AT, "proj", b, 3)
                mm(work("proj", b, 3)[:, 0:SEQ], w_up[qd, :], lat[b][qd, :], start=True, stop=True)\
                    .then_inc(s["plain_ps"], 1)
                claim(WORK_AT, "proj", b, 4)
                mm(work("proj", b, 4)[:, 0:SEQ], w_second[qd, 0:P], lat[b][qd, :], start=True, stop=True)
                mm(work("proj", b, 4)[:, SEQ:2 * SEQ], w_rope_q2[qd, :], lat[b][qd, :], start=True, stop=True)\
                    .then_inc(s["qr_ps"], 1)
                claim(WORK_AT, "proj", b, 5)
                for t in range(T):
                    last = mm(work("proj", b, 5)[:, t * D:(t + 1) * D], lat[b][kv, t * P:(t + 1) * P],
                              w_second[kv, :], start=True, stop=True)
                last.then_inc(s["fv_ps"], 1)

            def f_max(b, n):
                step = f"max{n}"
                if n == 0:
                    pe.wait_ge(s["fk_stack"], 16 * RUNS["fk"] * (b + 1))
                    pe.wait_ge(s["fq_stack"], 16 * RUNS["fq"] * (b + 1))
                claim(PAIR_AT, step, b)
                ps = pair(step, b)
                if n < 2:
                    t, heads, keys = 0, range(8 * n, 8 * n + 8), P
                else:
                    t, heads, keys = 1, range(4 * (n - 2), 4 * (n - 2) + 4), SEQ
                for i, head in enumerate(heads):
                    o = ps[:, i * keys:(i + 1) * keys]
                    mm(o, fstack["fq"][b][0:96, head, t * P:(t + 1) * P], fstack["fk"][b][0:96, head, 0:keys],
                       start=True, stop=False)
                    last = mm(o[:, keys - P:keys], ident16, mask_q, start=False, stop=True)
                last.then_inc(s["fm_ps"], 1)

            def max_back(b):
                pe.wait_ge(s["max_parts"], b + 1)
                claim(WORK_AT, "maxT", b)
                o16 = work("maxT", b)[:, 0:P].bitcast(BF16)
                for t in range(T):
                    last = nc.tensor.transpose(o16[0:3 * AH, t * P:(t + 1) * P],
                                               fmp[b][:, t, :, :].rearrange("p c h -> p (c h)"), ident16)
                last.then_inc(s["maxT_ps"], 1)

            def f_scores(b, n):
                step = f"f{n}"
                if n == 0:
                    pe.wait_ge(s["max_stack"], 16 * 3 * (b + 1))
                for i in range(2):
                    claim(PAIR_AT, step, b, i)
                    for a in range(2):
                        head = 4 * n + 2 * i + a
                        o = pair(step, b, i)[:, 512 * a:512 * a + 384]
                        mm(o[:, 0:SEQ], fstack["fk"][b][0:99, head, 0:P], fstack["fq"][b][0:99, head, :],
                           start=True, stop=False)
                        mm(o[:, 0:P], ident16, mask_k, start=False, stop=True)
                        mm(o[:, SEQ:SEQ + P], fstack["fk"][b][0:99, head, P:SEQ], fstack["fq"][b][0:99, head, P:SEQ],
                           start=True, stop=False)
                        last = mm(o[:, SEQ:SEQ + P], ident16, mask_k, start=False, stop=True)
                    last.then_inc(s["fs_ps"], 1)

            def f_values(b, n):
                q = 8 * b + 2 * n
                if n == 0:
                    pe.wait_ge(s["fv"], b + 1)
                claim(OUT_AT, f"f{n}", b)
                pe.wait_ge(s["fp"], q + 2)
                o = outs(f"f{n}", b)
                for kt in range(T):
                    for j in range(4):
                        pr = probs(f"f{n}", b, j // 2)[:, j % 2, :]
                        last = mm(o[32 * j:32 * j + 32, kt * P:SEQ], fvals[b][:, kt, 4 * n + j, :],
                                  pr[:, 0:SEQ] if kt == 0 else pr[:, SEQ:SEQ + P], start=kt == 0, stop=kt == T - 1)
                last.then_inc(s["fo_ps"], 1)
                pe.wait_ge(s["fot"], 4 * b + n + 1)
                claim(WORK_AT, f"f{n}", b)
                for t in range(T):
                    last = nc.tensor.transpose(work(f"f{n}", b)[:, t * P:(t + 1) * P], fot[b][:, t * P:(t + 1) * P],
                                               ident)
                last.then_inc(s["fback_ps"], 1)

            def causal(b, n):
                f_scores(b, n)
                f_values(b, n)

            def oproj(b):
                pe.wait_ge(s["ao"], 4 * (b + 1))
                claim(WORK_AT, "oproj", b, 0)
                for k in range(KD):
                    for t in range(T):
                        last = nc.tensor.transpose(work("oproj", b)[:, k * SEQ + t * P:k * SEQ + (t + 1) * P],
                                                   ao[b][:, t, k * P:(k + 1) * P], ident)
                last.then_inc(s["aoT_ps"], 1)
                pe.wait_ge(s["aoT"], b + 1)
                claim(WORK_AT, "oproj", b, 1)
                for t in range(T):
                    for k in range(KD):
                        last = mm(work("oproj", b, 1)[:, t * D:(t + 1) * D], aoT[b][:, k, t * P:(t + 1) * P],
                                  w_o[:, k, :], start=k == 0, stop=k == KD - 1)
                last.then_inc(s["o_ps"], 1)

            def router(b):
                pe.wait_ge(s["hT"], b + 1)
                claim(WORK_AT, "router", b)
                for t in range(T):
                    for k in range(KD):
                        last = mm(work("router", b)[:, t * NR:(t + 1) * NR], hT[b][:, k, t * P:(t + 1) * P],
                                  w_router[:, k, :], start=k == 0, stop=k == KD - 1)
                last.then_inc(s["router_ps"], 1)

            def expert(b, e):
                n = NE * b + e
                if n == 0:
                    pe.wait_ge(s["w_experts"], 16)
                claim(WORK_AT, f"e{e}", b, 0)
                for g in range(2):
                    for k in range(KD):
                        last = mm(work(f"e{e}", b, 0)[:, g * SEQ:(g + 1) * SEQ], gate_up[:, e, k, g, :],
                                  hT[b][:, k, :], start=k == 0, stop=k == KD - 1)
                last.then_inc(s["gu_ps"], 1)
                if e > 0:
                    expert_down(b, e - 1)
                if e == NE - 1:
                    expert_down(b, e)

            def expert_down(b, e):
                n = NE * b + e
                pe.wait_ge(s["hidden"], n + 1)
                claim(WORK_AT, f"e{e}", b, 1)
                for t in range(T):
                    last = mm(work(f"e{e}", b, 1)[:, t * D:(t + 1) * D], hid[n % 2][:, t * P:(t + 1) * P],
                              down_w[:, e, :], start=True, stop=True)
                last.then_inc(s["down_ps"], 1)

            steps = {"ln1": ln1, "dt": dt, "inx": inx, "cs": cs, "inz": inz, "out": out_proj,
                     "ssd0": lambda b: ssd(0, b), "ssd1": lambda b: ssd(1, b), "ctx": ctx,
                     "xk": lambda b: normed_heads("xk", b, wk, ctxT, "ctxT"), "xv": xv,
                     "ln2": lambda b: transposes("ln2", b, "xn2", xn[1], "xnT2_ps"),
                     "xq": lambda b: normed_heads("xq", b, wq, xnT, "xnT2"),
                     "ln3": lambda b: transposes("ln3", b, "xn3", xn[0], "xnT3_ps"), "proj": proj,
                     "maxT": max_back, "oproj": oproj,
                     "ln4": lambda b: transposes("ln4", b, "xn4", xn[1], "hT_ps"), "router": router}
            for step, b in SCHEDULE:
                if step in steps:
                    steps[step](b)
                elif step[0] == "x" and step[1:].isdigit():
                    cross(b, int(step[1:]))
                elif step[0] == "f" and step[1:].isdigit():
                    causal(b, int(step[1:]))
                elif step.startswith("max"):
                    f_max(b, int(step[3:]))
                elif step[0] == "e":
                    expert(b, int(step[1:]))

        @block.scalar
        def _(act):
            count = [0]

            def run(out_, in_, func, **kw):
                return nc.scalar.activation(out_, in_, func, **kw)

            def then(ins):
                count[0] += 1
                ins.then_inc(s["act_chain"], 1)
                act.wait_ge(s["act_chain"], count[0])

            def inv_sqrt(b, ready, value, dst, scale, eps_i, done):
                act.wait_ge(s[ready], value)
                then(run(dst, rs_in[0], ACT.Ln, scale=scale, bias=eps[:, eps_i:eps_i + 1]))
                run(dst, dst, ACT.Exp, scale=-0.5).then_inc(s[done], 1)

            rs_in = [None]

            def ln(step, i, b):
                if step == "ln1" and b == 0:
                    act.wait_ge(s["eps"], 3)
                rs_in[0] = mv[b][:, i, :, 1]
                inv_sqrt(b, f"mv{i}", b + 1, rstd[b][:, i, :], 1.0, 0, f"rstd{i}")
                if i == 2:
                    rs_in[0] = rstd[b][:, 4, :]
                    inv_sqrt(b, "ms3", b + 1, rstd[b][:, 5, :], 1.0, 0, "rms3")

            def dt(b):
                act.wait_ge(s["dt_abs"], b + 1)
                then(run(sp[b][:, 2, :], sp[b][:, 1, :], ACT.Exp, scale=-1.0))
                run(sp[b][:, 3, :], sp[b][:, 2, :], ACT.Ln, bias=1.0).then_inc(s["dt_exp"], 1)

            def inx(b):
                for i in range(CF // 2):
                    act.wait_ge(s["xbc_ps"], 3 * b + i + 1)
                    if b > 0 and i == 0:
                        act.wait_ge(s["y_done"], 2 * b)
                    ps = work("inx", b, i)
                    for f in range(2):
                        c = 2 * i + f
                        last = run(conv[b][:, c, :], ps[:, f * SEQ:(f + 1) * SEQ], ACT.Identity,
                                   scale=conv_w[:, c * TAPS + 3:c * TAPS + 4], bias=conv_b[:, c:c + 1])
                    last.then_inc(s["conv_in"], 1)

            def cs(b):
                act.wait_ge(s["cs_ps"], b + 1)
                run(ecs[b][:, :, :, :].rearrange("p t c h -> p (t c h)"), work("cs", b)[:, 0:T * 2 * NHM], ACT.Exp)\
                    .then_inc(s["ecs"], 1)

            def inz(b):
                act.wait_ge(s["taps"], CF * (b + 1))
                run(xbc[b][:, :, :], conv[b][:, :, :], ACT.Silu).then_inc(s["xbc"], 1)
                if b > 0:
                    act.wait_ge(s["ysum"], b)
                    act.wait_ge(s["ss_ps"], b)
                for i in range(XF // 2):
                    act.wait_ge(s["z_ps"], 2 * b + i + 1)
                    run(sz[b][:, 2 * i:2 * i + 2, :].rearrange("p f n -> p (f n)"), work("inz", b, i)[:, :], ACT.Silu)\
                        .then_inc(s["sz"], 1)

            def ssd(t, b):
                n = T * b + t
                act.wait_ge(s["diff_ps"], n + 1)
                if n > 0:
                    act.wait_ge(s["y_ps"], n)
                run(L[b][:, :, :].rearrange("p h n -> p (h n)"), pair(f"ssd{t}", b)[:, :], ACT.Exp)\
                    .then_inc(s["L"], 1)

            def out_proj(b):
                act.wait_ge(s["y_done"], 2 * (b + 1))
                run(ysq[b][:, :, :], yg[b][:, :, :], ACT.Square).then_inc(s["ysq"], 1)
                act.wait_ge(s["ss_ps"], b + 1)
                run(rstd[b][:, 4, :], work("out", b, 0)[:, 0:T], ACT.Ln, scale=1.0 / DI, bias=eps[:, 0:1])\
                    .then_inc(s["gate_ln"], 1)
                act.wait_ge(s["gate_ln"], b + 1)
                run(rstd[b][:, 5, :], rstd[b][:, 4, :], ACT.Exp, scale=-0.5).then_inc(s["gate_rs"], 1)

            def normed_heads(kind, b):
                act.wait_ge(s[f"{kind}_ps"], b + 1)
                after_last_user(act, SHARED_AT["full_" + kind[1]], kind, b)
                if b > 0:
                    act.wait_ge(s[f"{kind}_full"], b)
                run(full[kind][:, :], work(kind, b, 0)[:, :], ACT.Square).then_inc(s[f"{kind}_sq"], 1)
                act.wait_ge(s[f"{kind}_sum"], b + 1)
                run(rs[kind][:, :], work(kind, b, 1)[:, :], ACT.Ln, scale=1.0 / XD, bias=eps[:, 1:2])\
                    .then_inc(s[f"{kind}_ln"], 1)
                act.wait_ge(s[f"{kind}_ln"], b + 1)
                run(rs[kind][:, :], rs[kind][:, :], ACT.Exp, scale=-0.5).then_inc(s[f"{kind}_rs"], 1)

            def cross(b, n):
                for i in range(2):
                    q = 16 * b + 2 * n + i
                    act.wait_ge(s["xs_ps"], q + 1)
                    after_last_user(act, PROB_AT, f"x{n}", b, i)
                    run(probs(f"x{n}", b, i)[:, :, :].rearrange("p a n -> p (a n)"), pair(f"x{n}", b, i)[:, :], ACT.Exp,
                        scale=float(XD) ** -0.5).then_inc(s["xp"], 1)

            def proj(b):
                act.wait_ge(s["lat_ps"], b + 1)
                if b > 0:
                    act.wait_ge(s["fv_ps"], b)
                run(lat[b][:, :], work("proj", b, 0)[:, 0:SEQ], ACT.Copy).then_inc(s["lat"], 1)
                act.wait_ge(s["plain_ps"], 2 * b + 1)
                after_last_user(act, SHARED_AT["full_k"], "proj", b)
                after_last_user(act, SHARED_AT["full_q"], "proj", b)
                run(full["fk"][:, 0:SEQ], work("proj", b, 2)[:, 0:SEQ], ACT.Copy).then_inc(s["plain"], 1)
                act.wait_ge(s["plain_ps"], 2 * b + 2)
                run(full["fq"][:, 0:SEQ], work("proj", b, 3)[:, 0:SEQ], ACT.Copy).then_inc(s["plain"], 1)

            def causal(b, n):
                for i in range(2):
                    q = 8 * b + 2 * n + i
                    act.wait_ge(s["fs_ps"], q + 1)
                    after_last_user(act, PROB_AT, f"f{n}", b, i)
                    run(probs(f"f{n}", b, i)[:, :, 0:384],
                        pair(f"f{n}", b, i)[:, :].rearrange("p (a n) -> p a n", a=2)[:, :, 0:384], ACT.Exp,
                        scale=float(AD) ** -0.5).then_inc(s["fp"], 1)

            def router(b):
                act.wait_ge(s["logits"], b + 1)
                run(rt[b][:, 1, :, :], rt[b][:, 0, :, :], ACT.Exp, scale=-1.0).then_inc(s["router_exp"], 1)

            def expert(b, e):
                n = NE * b + e
                act.wait_ge(s["gu_ps"], n + 1)
                if n >= 2:
                    act.wait_ge(s["down_ps"], n - 1)
                run(sg[n % 2][:, :], work(f"e{e}", b, 0)[:, 0:SEQ], ACT.Silu).then_inc(s["sg"], 1)

            steps = {"ln1": lambda b: ln("ln1", 0, b), "dt": dt, "inx": inx, "cs": cs, "inz": inz,
                     "ssd0": lambda b: ssd(0, b), "ssd1": lambda b: ssd(1, b), "out": out_proj,
                     "xk": lambda b: normed_heads("xk", b), "ln2": lambda b: ln("ln2", 1, b),
                     "xq": lambda b: normed_heads("xq", b),
                     "ln3": lambda b: ln("ln3", 2, b), "proj": proj, "ln4": lambda b: ln("ln4", 3, b),
                     "router": router}
            for step, b in SCHEDULE:
                if step in steps:
                    steps[step](b)
                elif step[0] == "x" and step[1:].isdigit():
                    cross(b, int(step[1:]))
                elif step[0] == "f" and step[1:].isdigit():
                    causal(b, int(step[1:]))
                elif step[0] == "e":
                    expert(b, int(step[1:]))

        @block.vector
        def _(dve):
            count = [0]
            vec = nc.vector

            def then(ins):
                count[0] += 1
                ins.then_inc(s["dve_chain"], 1)
                dve.wait_ge(s["dve_chain"], count[0])

            vec.memset(ones[:, :], 1.0)
            vec.memset(eps[:, 0:1], LN_EPS).then_inc(s["eps"], 1)
            vec.memset(eps[:, 1:2], X_EPS).then_inc(s["eps"], 1)
            vec.memset(eps[:, 2:3], 0.0).then_inc(s["eps"], 1)

            def ln(i, b, src, ready, value):
                dve.wait_ge(s[ready], value)
                for t in range(T):
                    then(vec.bn_stats(stats[b][:, i, t, :], src[:, t, :]))
                then(vec.bn_aggr(mv[b][:, i, 0, :], stats[b][:, i, 0, :]))
                last = vec.bn_aggr(mv[b][:, i, 1, :], stats[b][:, i, 1, :])
                if i < 3:
                    last.then_inc(s[f"mv{i}"], 1)
                else:
                    then(last)
                after_last_user(dve, SHARED_AT[f"xn_{i % 2}"], f"ln{i + 1}", b)

            def finish_ln(i, b, src, xn_sem):
                for t in range(T):
                    last = vec.tensor_scalar(xn[i][:, t, :], src[:, t, :], mv[b][:, i, t, 0:1],
                                             rstd[b][:, i, t:t + 1], ALU.subtract, ALU.mult)
                last.then_inc(s[xn_sem], 1)

            def copy_T(step, b, ready, dst, done, free=None):
                dve.wait_ge(s[ready], b + 1)
                if free is not None and free[1]:
                    dve.wait_ge(s[free[0]], free[1])
                vec.tensor_copy(dst[:, :, :].rearrange("p k n -> p (k n)"), work(step, b)[:, :]).then_inc(s[done], 1)

            def ln1(b):
                ln(0, b, x0[b], "x_in" if b else "x_in_first", 16 if b == 0 else 16 * max(b, NF - 1))
                dve.wait_ge(s["rstd0"], b + 1)
                finish_ln(0, b, x0[b], "xn")
                free_xnT(b, 0)
                copy_T("ln1", b, "xnT_ps", xnT[b], "xnT")

            def free_xnT(b, use):
                if use == 0:
                    if b >= 2:
                        dve.wait_ge(s["kr_ps"], b - 1)
                elif use == 1:
                    dve.wait_ge(s["z_ps"], 2 * (b + 1))
                    dve.wait_ge(s["dt_ps"], b + 1)
                else:
                    dve.wait_ge(s["xq_ps"], b + 1)

            def dt(b):
                dve.wait_ge(s["dt_ps"], b + 1)
                if b == 0:
                    dve.wait_ge(s["w_first"], 32)
                S = sp[b]
                vec.tensor_tensor(S[:, 0, :].rearrange("p (t h) -> p t h", t=T),
                                  work("dt", b)[:, 0:T * NHM].rearrange("p (t h) -> p t h", t=T),
                                  dt_bias[:, :].unsqueeze(1).to_broadcast([P, T, NHM]), ALU.add)\
                    .then_inc(s["dt_raw"], 1)
                dve.wait_ge(s["dt_raw"], b + 1)
                vec.scalar_tensor_tensor(out=S[:, 1, :], in0=S[:, 0, :], scalar=-1.0, in1=S[:, 0, :], op0=ALU.mult,
                                         op1=ALU.max).then_inc(s["dt_abs"], 1)
                dve.wait_ge(s["dt_exp"], b + 1)
                then(vec.tensor_scalar(S[:, 4, :], S[:, 2, :], 1.0, None, ALU.add))
                then(vec.tensor_scalar(S[:, 5, :], S[:, 4, :], -1.0, None, ALU.add))
                then(vec.tensor_tensor(S[:, 5, :], S[:, 2, :], S[:, 5, :], ALU.subtract))
                then(vec.reciprocal(S[:, 4, :], S[:, 4, :]))
                then(vec.tensor_tensor(S[:, 5, :], S[:, 5, :], S[:, 4, :], ALU.mult))
                then(vec.scalar_tensor_tensor(out=S[:, 6, :], in0=S[:, 0, :], scalar=0.0, in1=S[:, 3, :],
                                              op0=ALU.max, op1=ALU.add))
                then(vec.tensor_tensor(dt_t[b][:, :, :].rearrange("p t h -> p (t h)"), S[:, 6, :], S[:, 5, :], ALU.add))
                vec.tensor_tensor(dA[b][:, :, :], dt_t[b][:, :, :],
                                  a_row[:, :].unsqueeze(1).to_broadcast([P, T, NHM]), ALU.mult)\
                    .then_inc(s["dA"], 1)

            def inx(b):
                for i in range(CF // 2):
                    dve.wait_ge(s["conv_in"], 3 * b + i + 1)
                    for f in range(2):
                        c = 2 * i + f
                        for k in range(TAPS - 2, -1, -1):
                            back = TAPS - 1 - k
                            ins = vec.scalar_tensor_tensor(
                                out=conv[b][:, c, back:], in0=work("inx", b, i)[:, f * SEQ:(f + 1) * SEQ - back],
                                scalar=conv_w[:, c * TAPS + k:c * TAPS + k + 1], in1=conv[b][:, c, back:],
                                op0=ALU.mult, op1=ALU.add)
                            if k:
                                then(ins)
                            else:
                                ins.then_inc(s["taps"], 1)

            def ssd(t, b):
                n, step, tok = T * b + t, f"ssd{t}", slice(t * P, (t + 1) * P)
                dve.wait_ge(s["g_ps"], n + 1)
                if n > 0:
                    dve.wait_ge(s["y_ps"], n)
                if t == 0:
                    if b > 0:
                        dve.wait_ge(s["state_ps"], b)
                    then(vec.tensor_copy(btok[b][:, :], work(step, b, 0)[:, P:2 * P]))
                vec.tensor_tensor(Gm[b][:, :], work(step, b, 0)[:, 0:P], upto, ALU.mult).then_inc(s["gm"], 1)
                dve.wait_ge(s["xtok_ps"], n + 1)
                vec.tensor_tensor(dtx[b][:, :].rearrange("p (h d) -> p h d", h=NHM),
                                  work(step, b, 1)[:, :].rearrange("p (h d) -> p h d", h=NHM),
                                  dt_t[b][:, t, :].unsqueeze(2).to_broadcast([P, NHM, HP]), ALU.mult)\
                    .then_inc(s["dtx"], 1)
                if t == 0:
                    dve.wait_ge(s["dtx"], n + 1)
                    dve.wait_ge(s["ecs"], b + 1)
                    vec.tensor_tensor(dtxd[b][:, :].rearrange("p (h d) -> p h d", h=NHM),
                                      dtx[b][:, :].rearrange("p (h d) -> p h d", h=NHM),
                                      ecs[b][:, 0, 1, :].unsqueeze(2).to_broadcast([P, NHM, HP]), ALU.mult)\
                        .then_inc(s["dtxd"], 1)
                dve.wait_ge(s["L"], n + 1)
                dve.wait_ge(s["gm"], n + 1)
                vec.tensor_tensor(L[b][:, :, :], L[b][:, :, :], Gm[b][:, :].unsqueeze(1).to_broadcast([P, NHM, P]),
                                  ALU.mult).then_inc(s["M"], 1)
                if t == 0:
                    dve.wait_ge(s["state_ps"], b + 1)
                    if b > 0:
                        dve.wait_ge(s["yoff_ps"], b)
                    vec.tensor_copy(state[b][:, :], work(step, b, 2)[:, :]).then_inc(s["state"], 1)
                else:
                    dve.wait_ge(s["yoff_ps"], b + 1)
                    vec.tensor_tensor(yoff[b][:, :].rearrange("p (h d) -> p h d", h=NHM),
                                      work(step, b, 2)[:, :].rearrange("p (h d) -> p h d", h=NHM),
                                      ecs[b][:, 1, 0, :].unsqueeze(2).to_broadcast([P, NHM, HP]), ALU.mult)\
                        .then_inc(s["yoff"], 1)
                dve.wait_ge(s["y_ps"], n + 1)
                dve.wait_ge(s["xD"], b + 1)
                vec.tensor_tensor(yg[b][:, :, tok], work(step, b, 3)[:, :].rearrange("p (f n) -> p f n", f=XF),
                                  xD[b][:, :, tok], ALU.add).then_inc(s["y"], 1)
                dve.wait_ge(s["y"], n + 1)
                dve.wait_ge(s["sz"], 2 * (b + 1))
                vec.tensor_tensor(yg[b][:, :, tok], yg[b][:, :, tok], sz[b][:, :, tok], ALU.mult)\
                    .then_inc(s["y_done"], 1)

            def out_proj(b):
                if b == 0:
                    for f in range(XF):
                        vec.tensor_scalar(w_out[:, f, :], w_out[:, f, :], norm_w[:, f:f + 1], None, ALU.mult)\
                           .then_inc(s["w_norm_out"], 1)
                dve.wait_ge(s["out_ps"], b + 1)
                dve.wait_ge(s["gate_rs"], b + 1)
                for t in range(T):
                    last = vec.scalar_tensor_tensor(out=x1[b][:, t, :], in0=work("out", b, 1)[:, t * D:(t + 1) * D],
                                                    scalar=rstd[b][:, 5, t:t + 1], in1=x0[b][:, t, :], op0=ALU.mult,
                                                    op1=ALU.add)
                last.then_inc(s["x1"], 1)

            def ctx(b):
                if b > 0:
                    dve.wait_ge(s["xv_ps"], b)
                    dve.wait_ge(s["xk_ps"], b)
                copy_T("ctx", b, "ctxT_ps", ctxT[b], "ctxT")

            def split(kind, b):
                after_last_user(dve, SHARED_AT["parts_" + kind[1]], kind, b)
                vec.tensor_copy(parts[kind][:, :, 0, :], full[kind][:, :].rearrange("p (f n) -> p f n", f=2))\
                    .then_inc(s[f"{kind}_rounded"], 1)
                dve.wait_ge(s[f"{kind}_diffs"], 2 * b + 1)
                vec.tensor_copy(parts[kind][:, :, 1, :], full[kind][:, :].rearrange("p (f n) -> p f n", f=2))\
                    .then_inc(s[f"{kind}_rounded"], 1)

            def normed_heads(kind, b):
                dve.wait_ge(s[f"{kind}_rs"], b + 1)
                vec.tensor_tensor(full[kind][:, :], work(kind, b, 0)[:, :], rs[kind][:, :], ALU.mult)\
                    .then_inc(s[f"{kind}_full"], 1)
                dve.wait_ge(s[f"{kind}_full"], b + 1)
                split(kind, b)

            def xv(b):
                dve.wait_ge(s["xv_ps"], b + 1)
                if b == 0:
                    dve.wait_ge(s["pool_init"], NST + 4)
                else:
                    dve.wait_ge(s["xo_quad"], 8 * b)
                ps = work("xv", b)
                for t in range(T):
                    for i in range(3):
                        quads = len(range(i, XH // 4, 3))
                        for m in range(quads):
                            n = i + 3 * m
                            last = vec.tensor_copy(
                                xvals[b][:, t, 4 * n:4 * n + 4, 9 * i:9 * i + XD],
                                ps[:, t * D + 32 * n:t * D + 32 * n + 32].rearrange("p (j d) -> p j d", j=4))
                last.then_inc(s["xv"], 1)

            def cross(b, n):
                if n in (2, 5, 7):
                    rnd = (2, 5, 7).index(n)
                    ni = min(3, 8 - 3 * rnd)
                    step = ("x2", "x5", "x7")[rnd]
                    dve.wait_ge(s["xo_quad"], 8 * b + n + 1)
                    if b + rnd > 0:
                        dve.wait_ge(s["xback_ps"], 3 * b + rnd)
                    vec.tensor_copy(xot[b][:, :], outs(f"x{3 * rnd}", b)).then_inc(s["xot"], 1)
                    dve.wait_ge(s["xback_ps"], 3 * b + rnd + 1)
                    if b >= 2 and rnd == 0:
                        dve.wait_ge(s["base"], b - 1)
                    for t in range(T):
                        v = work(step, b)[:, t * P:(t + 1) * P].rearrange("p (j c) -> p j c", j=4)[:, :, 0:9 * ni]\
                            .rearrange("p j (i d) -> p i j d", i=ni)
                        den = xden[b][:, t, 0:4 * ni].rearrange("p (i j) -> p i j", j=4)
                        then(vec.reciprocal(den, v[:, :, :, XD]))
                        o = x2[b][:, t, 96 * rnd:96 * rnd + 32 * ni]
                        last = vec.tensor_tensor(o.rearrange("p (i j d) -> p i j d", i=ni, j=4), v[:, :, :, 0:XD],
                                                 den.unsqueeze(3).to_broadcast([P, ni, 4, XD]), ALU.mult)
                        if t == 0:
                            then(last)
                    last.then_inc(s["xo"], 1)
                    dve.wait_ge(s["xo"], 3 * b + rnd + 1)
                    if n == 7:
                        vec.tensor_tensor(x2[b][:, :, :], x2[b][:, :, :], x1[b][:, :, :], ALU.add)\
                            .then_inc(s["x2"], 1)

            def ln2(b):
                ln(1, b, x1[b], "x1", b + 1)
                dve.wait_ge(s["rstd1"], b + 1)
                finish_ln(1, b, x1[b], "xn2")
                free_xnT(b, 1)
                copy_T("ln2", b, "xnT2_ps", xnT[b], "xnT2")

            def ln3(b):
                ln(2, b, x2[b], "x2", b + 1)
                dve.wait_ge(s["rstd2"], b + 1)
                r = rstd[b]
                then(vec.tensor_tensor(r[:, 4, :], r[:, 2, :], r[:, 2, :], ALU.mult))
                vec.tensor_tensor(r[:, 4, :], r[:, 4, :], mv[b][:, 2, :, 1], ALU.mult).then_inc(s["ms3"], 1)
                for t in range(T):
                    last = vec.tensor_scalar(y3[b][:, t, :], x2[b][:, t, :], mv[b][:, 2, t, 0:1], r[:, 2, t:t + 1],
                                             ALU.subtract, ALU.mult)
                then(last)
                dve.wait_ge(s["rms3"], b + 1)
                for t in range(T):
                    last = vec.tensor_scalar(xn[0][:, t, :], y3[b][:, t, :], r[:, 5, t:t + 1], None, ALU.mult)
                last.then_inc(s["xn3"], 1)
                dve.wait_ge(s["xnT3_ps"], b + 1)
                if b == 0:
                    dve.wait_ge(s["w_second"], 48)
                free_xnT(b, 2)
                for k in range(KD):
                    last = vec.tensor_scalar(xnT[b][:, k, :], work("ln3", b)[:, k * SEQ:(k + 1) * SEQ],
                                             ln1_w[:, k:k + 1], None, ALU.mult)
                last.then_inc(s["xnT3"], 1)

            def proj(b):
                for kind, i, ps_ready, done in (("fk", 1, "kr_ps", "k_rope"), ("fq", 4, "qr_ps", "q_rope")):
                    dve.wait_ge(s[ps_ready], b + 1)
                    after_last_user(dve, SHARED_AT["full_" + kind[1]], "proj", b)
                    vec.tensor_tensor(full[kind][:, SEQ:2 * SEQ], work("proj", b, i)[:, 0:SEQ], rope_cs[:, 0:SEQ],
                                      ALU.mult)
                    if b > 0:
                        dve.wait_ge(s[f"{kind}_full"], b)
                    vec.tensor_tensor(rope_t[:, KIND[kind] - 2, :], work("proj", b, i)[:, SEQ:2 * SEQ],
                                      rope_cs[:, SEQ:2 * SEQ], ALU.mult).then_inc(s[done], 1)
                dve.wait_ge(s["fv_ps"], b + 1)
                if b == 0:
                    dve.wait_ge(s["pool_init"], NST + 4)
                else:
                    dve.wait_ge(s["fo_ps"], 4 * b)
                vec.tensor_copy(fvals[b][:, :, :, 0:AD],
                                work("proj", b, 5)[:, :].rearrange("p (t h d) -> p t h d", t=T, h=AH))\
                    .then_inc(s["fv"], 1)

            def f_split(kind, b):
                dve.wait_ge(s[f"{kind}_full"], b + 1)
                dve.wait_ge(s["plain"], 2 * b + (1 if kind == "fk" else 2))
                split(kind, b)

            def f_max(b, n):
                dve.wait_ge(s["fm_ps"], 6 * b + n + 1)
                ps = pair(f"max{n}", b)
                if n < 2:
                    src = ps[:, :].rearrange("p (h k) -> p h k", h=8)
                    dst = fmx[b][:, 0, 8 * n:8 * n + 8]
                else:
                    src = ps[:, :].rearrange("p (h k) -> p h k", h=4)
                    dst = fmx[b][:, 1, 4 * (n - 2):4 * (n - 2) + 4]
                vec.tensor_reduce(dst, src, AX.X, ALU.max, negate=True).then_inc(s["mx"], 1)

            def maxT_(b):
                dve.wait_ge(s["mx"], 6 * (b + 1))
                f, r = fmx[b][:, :, :], fmr[b][:, :].rearrange("p (t h) -> p t h", t=T)
                then(vec.tensor_copy(fmp[b][:, :, 0, :], f))
                then(vec.tensor_tensor(r, f, fmp[b][:, :, 0, :], ALU.subtract))
                then(vec.tensor_copy(fmp[b][:, :, 1, :], r))
                vec.tensor_tensor(fmp[b][:, :, 2, :], r, fmp[b][:, :, 1, :], ALU.subtract).then_inc(s["max_parts"], 1)
                dve.wait_ge(s["maxT_ps"], b + 1)
                if b > 0:
                    dve.wait_ge(s["max_stack"], 48 * b)
                vec.tensor_copy(maxT[b][:, :], work("maxT", b)[:, 0:P].bitcast(BF16)[0:3 * AH, 0:SEQ])\
                    .then_inc(s["maxT"], 1)

            def causal(b, n):
                dve.wait_ge(s["fo_ps"], 4 * b + n + 1)
                if b + n > 0:
                    dve.wait_ge(s["fback_ps"], 4 * b + n)
                vec.tensor_copy(fot[b][:, :], outs(f"f{n}", b)).then_inc(s["fot"], 1)
                dve.wait_ge(s["fback_ps"], 4 * b + n + 1)
                if b > 0 and n == 0:
                    dve.wait_ge(s["aoT_ps"], b)
                v = work(f"f{n}", b)[:, 0:T * P].rearrange("p (t j c) -> p t j c", t=T, j=4)
                then(vec.reciprocal(fden[b][:, :, :], v[:, :, :, AD]))
                for t in range(T):
                    last = vec.tensor_tensor(ao[b][:, t, 64 * n:64 * n + 64].rearrange("p (j d) -> p j d", j=4),
                                             v[:, t, :, 0:AD], fden[b][:, t, :].unsqueeze(2).to_broadcast([P, 4, AD]),
                                             ALU.mult)
                last.then_inc(s["ao"], 1)
                dve.wait_ge(s["ao"], 4 * b + n + 1)

            def oproj(b):
                copy_T("oproj", b, "aoT_ps", aoT[b], "aoT", ("o_ps", b))
                dve.wait_ge(s["o_ps"], b + 1)
                vec.tensor_tensor(h4[b][:, :, :], work("oproj", b, 1)[:, :].rearrange("p (t n) -> p t n", t=T),
                                  y3[b][:, :, :], ALU.add).then_inc(s["h"], 1)

            def ln4(b):
                ln(3, b, h4[b], "h", b + 1)
                m2 = sp[b][:, 7, 0:T]
                then(vec.tensor_tensor(m2, mv[b][:, 3, :, 0], mv[b][:, 3, :, 0], ALU.mult))
                vec.tensor_tensor(mv[b][:, 3, :, 1], mv[b][:, 3, :, 1], m2, ALU.add).then_inc(s["mv3"], 1)
                dve.wait_ge(s["rstd3"], b + 1)
                for t in range(T):
                    last = vec.tensor_scalar(xn[1][:, t, :], h4[b][:, t, :], rstd[b][:, 3, t:t + 1], None, ALU.mult)
                last.then_inc(s["xn4"], 1)
                dve.wait_ge(s["hT_ps"], b + 1)
                if b > 0:
                    dve.wait_ge(s["router_ps"], b)
                    dve.wait_ge(s["gu_ps"], NE * b)
                for k in range(KD):
                    last = vec.tensor_scalar(hT[b][:, k, :], work("ln4", b)[:, k * SEQ:(k + 1) * SEQ],
                                             ln2_w[:, k:k + 1], None, ALU.mult)
                last.then_inc(s["hT"], 1)

            def router(b):
                r = rt[b]
                dve.wait_ge(s["router_ps"], b + 1)
                vec.tensor_tensor(r[:, 0, :, :], work("router", b)[:, 0:T * NR].rearrange("p (t e) -> p t e", t=T),
                                  router_b[:, :].unsqueeze(1).to_broadcast([P, T, NR]), ALU.add)\
                    .then_inc(s["logits"], 1)
                dve.wait_ge(s["router_exp"], b + 1)
                then(vec.tensor_scalar(r[:, 2, :, :], r[:, 1, :, :], 1.0, None, ALU.add))
                then(vec.reciprocal(r[:, 3, :, :], r[:, 2, :, :]))
                prob = r[:, 3, :, :]
                for t in range(T):
                    mine = prob[:, t, :].unsqueeze(2).to_broadcast([P, NR, NR])
                    other = prob[:, t, :].unsqueeze(1).to_broadcast([P, NR, NR])
                    c = [cmp_[b][:, i, t, :].rearrange("p (e j) -> p e j", e=NR) for i in range(2)]
                    then(vec.tensor_tensor(c[0], other, mine, ALU.is_gt))
                    then(vec.tensor_tensor(c[1], other, mine, ALU.is_equal))
                    then(vec.tensor_tensor(c[1], c[1], before, ALU.mult))
                    then(vec.tensor_tensor(c[0], c[0], c[1], ALU.add))
                    then(vec.tensor_reduce(r[:, 4, t, :], c[0], AX.X, ALU.add))
                then(vec.tensor_scalar(r[:, 5, :, :], r[:, 4, :, :], 1.5, None, ALU.is_lt))
                then(vec.tensor_tensor(r[:, 5, :, :], r[:, 5, :, :], prob, ALU.mult))
                then(vec.tensor_reduce(rsum[b][:, 0, :], r[:, 5, :, :], AX.X, ALU.add))
                then(vec.reciprocal(rsum[b][:, 1, :], rsum[b][:, 0, :]))
                then(vec.tensor_tensor(gates[b][:, :, :], r[:, 5, :, :],
                                       rsum[b][:, 1, :].unsqueeze(2).to_broadcast([P, T, NR]), ALU.mult))
                then(vec.tensor_scalar(gates[b][:, :, :], gates[b][:, :, :], 1.0 / 8, None, ALU.mult))

            def expert(b, e):
                n = NE * b + e
                dve.wait_ge(s["sg"], n + 1)
                if n >= 2:
                    dve.wait_ge(s["down_ps"], n - 1)
                vec.tensor_tensor(hid[n % 2][:, :], sg[n % 2][:, :], work(f"e{e}", b, 0)[:, SEQ:2 * SEQ], ALU.mult)\
                    .then_inc(s["hidden"], 1)
                if e > 0:
                    add_expert(b, e - 1)
                if e == NE - 1:
                    add_expert(b, e)

            def add_expert(b, e):
                n = NE * b + e
                dve.wait_ge(s["down_ps"], n + 1)
                ps = work(f"e{e}", b, 1)
                if e == 0:
                    dve.wait_ge(s["base"], b + 1)
                    vec.scalar_tensor_tensor(out=acc[b][:, :, :], in0=ps[:, :].rearrange("p (t n) -> p t n", t=T),
                                             scalar=1.0 / 8, in1=acc[b][:, :, :], op0=ALU.mult, op1=ALU.add)\
                       .then_inc(s["acc"], 1)
                else:
                    dve.wait_ge(s["acc"], n)
                    for t in range(T):
                        last = vec.scalar_tensor_tensor(out=acc[b][:, t, :], in0=ps[:, t * D:(t + 1) * D],
                                                        scalar=gates[b][:, t, e - 1:e], in1=acc[b][:, t, :],
                                                        op0=ALU.mult, op1=ALU.add)
                    last.then_inc(s["acc"], 1)

            steps = {"ln1": ln1, "dt": dt, "inx": inx, "ssd0": lambda b: ssd(0, b), "ssd1": lambda b: ssd(1, b),
                     "out": out_proj, "ctx": ctx, "xk": lambda b: normed_heads("xk", b), "xv": xv, "ln2": ln2,
                     "xq": lambda b: normed_heads("xq", b), "ln3": ln3, "proj": proj,
                     "fk": lambda b: f_split("fk", b), "fq": lambda b: f_split("fq", b), "maxT": maxT_,
                     "oproj": oproj, "ln4": ln4, "router": router}
            for step, b in SCHEDULE:
                if step in steps:
                    steps[step](b)
                elif step[0] == "x" and step[1:].isdigit():
                    cross(b, int(step[1:]))
                elif step[0] == "f" and step[1:].isdigit():
                    causal(b, int(step[1:]))
                elif step.startswith("max"):
                    f_max(b, int(step[3:]))
                elif step[0] == "e":
                    expert(b, int(step[1:]))

        @block.gpsimd
        def _(pool):
            gp = nc.gpsimd
            for i in range(NST):
                gp.memset(fstack["fk"][i][96:99, :, :], 1.0).then_inc(s["pool_init"], 1)
                pool.wait_ge(s["pool_init"], i + 1)
            gp.memset(xvals[0][:, :, :, :], 0.0).then_inc(s["pool_init"], 1)
            gp.memset(fvals[0][:, :, :, :], 0.0).then_inc(s["pool_init"], 1)
            pool.wait_ge(s["pool_init"], NST + 2)
            for n in range(XH // 4):
                i = n % 3
                last = gp.memset(xvals[0][:, :, 4 * n:4 * n + 4, 9 * i + XD:9 * i + XD + 1], 1.0)
            last.then_inc(s["pool_init"], 1)
            gp.memset(fvals[0][:, :, :, AD:AD + 1], 1.0).then_inc(s["pool_init"], 1)
            pool.wait_ge(s["w_second"], 48)

            def turned(dst, src):
                v = dst.rearrange("p (h a d) -> p h a d", a=2, d=AR // 2)
                u = src.rearrange("p (h a d) -> p h a d", a=2, d=AR // 2)
                gp.tensor_scalar(v[:, :, 0, :], u[:, :, 1, :], -1.0, None, ALU.mult)\
                    .then_inc(s["pool_init"], 1)
                return gp.tensor_copy(v[:, :, 1, :], u[:, :, 0, :])

            for k in range(KD):
                turned(w_rope_k2[:, k, :], w_rope_k[:, k, :]).then_inc(s["pool_init"], 1)
            pool.wait_ge(s["pool_init"], NST + 8)
            turned(w_rope_q2[LAT:2 * LAT, :], w_second[LAT:2 * LAT, 0:P]).then_inc(s["pool_init"], 1)
            pool.wait_ge(s["pool_init"], NST + 10)

            def ssd(t, b):
                if t == 0:
                    pool.wait_ge(s["xbc"], b + 1)
                    if b > 0:
                        pool.wait_ge(s["out_ps"], b)
                        pool.wait_ge(s["ysq"], b)
                    gp.tensor_tensor(xD[b][:, :, :], xbc[b][:, 0:XF, :],
                                     d_skip[:, :].unsqueeze(2).to_broadcast([P, XF, SEQ]), ALU.mult)\
                        .then_inc(s["xD"], 1)

            def decays(t, b):
                n = T * b + t
                pool.wait_ge(s["dA"], b + 1)
                if n > 0:
                    pool.wait_ge(s["diff_ps"], n)
                gp.tensor_tensor(R[b][:, :, :], upto.unsqueeze(1).to_broadcast([P, NHM, P]),
                                 dA[b][:, t, :].unsqueeze(2).to_broadcast([P, NHM, P]), ALU.mult)\
                    .then_inc(s["R"], 1)

            def out_proj(b):
                pool.wait_ge(s["ysq"], b + 1)
                gp.tensor_tensor(ysq[b][:, 0:2, :], ysq[b][:, 0:2, :], ysq[b][:, 2:4, :], ALU.add)\
                    .then_inc(s["ysum2"], 1)
                pool.wait_ge(s["ysum2"], b + 1)
                gp.tensor_tensor(ysq[b][:, 0, :], ysq[b][:, 0, :], ysq[b][:, 1, :], ALU.add).then_inc(s["ysum"], 1)

            def split(kind, b):
                pool.wait_ge(s[f"{kind}_rounded"], 2 * b + 1)
                f3 = r3 = full[kind][:, :].rearrange("p (f n) -> p f n", f=2)
                gp.tensor_tensor(r3, f3, parts[kind][:, :, 0, :], ALU.subtract).then_inc(s[f"{kind}_diffs"], 1)
                pool.wait_ge(s[f"{kind}_rounded"], 2 * b + 2)
                gp.tensor_tensor(parts[kind][:, :, 2, :], r3, parts[kind][:, :, 1, :], ALU.subtract)\
                    .then_inc(s[f"{kind}_diffs"], 1)

            def proj(b):
                for kind, done in (("fk", "k_rope"), ("fq", "q_rope")):
                    pool.wait_ge(s[done], b + 1)
                    gp.tensor_tensor(full[kind][:, SEQ:2 * SEQ], full[kind][:, SEQ:2 * SEQ],
                                     rope_t[:, KIND[kind] - 2, :], ALU.add)\
                        .then_inc(s[f"{kind}_full"], 1)

            def router(b):
                pool.wait_ge(s["h"], b + 1)
                gp.tensor_tensor(acc[b][:, :, :], x2[b][:, :, :], h4[b][:, :, :], ALU.add).then_inc(s["base"], 1)

            def ssd0(b):
                ssd(0, b)
                decays(0, b)

            steps = {"ssd0": ssd0, "ssd1": lambda b: decays(1, b), "out": out_proj,
                     "xk": lambda b: split("xk", b), "xq": lambda b: split("xq", b), "proj": proj,
                     "fk": lambda b: split("fk", b), "fq": lambda b: split("fq", b), "router": router}
            for step, b in SCHEDULE:
                if step in steps:
                    steps[step](b)


def _rows(a, k):
    a = np.asarray(a)
    return a.reshape(k, P, -1).transpose(1, 0, 2).reshape(P, -1)


def _spread(row):
    return np.broadcast_to(np.asarray(row), (P, np.asarray(row).shape[0]))


def _shape_tables():
    i = np.arange(P)
    ident = np.eye(P, dtype=np.float32)
    upto = (i[:, None] <= i[None, :]).astype(np.float32)
    after = (i[:, None] > i[None, :]).astype(np.float32)
    block8 = (i[:, None] // XD == i[None, :] // XD).astype(np.float32)
    inv = (1.0 / 10000.0 ** (np.arange(0, AR, 2, dtype=np.float32) / AR)).astype(np.float32)
    ang = np.outer(np.arange(SEQ, dtype=np.float32), inv).astype(np.float32)
    ang = ang[:, i % (AR // 2)].T
    rope = np.concatenate([np.cos(ang), np.sin(ang)], axis=1).astype(np.float32)
    e = np.arange(NR)
    before = (e[None, :] < e[:, None]).astype(np.float32).reshape(-1)
    shape = np.concatenate([ident, upto, after, block8, rope, _spread(before)], axis=1)
    later = np.where(i[None, :] > i[:, None], np.float32(NEG), np.float32(0))
    masks = np.stack([ident, later, later.T], axis=1)
    return shape, masks


def kernel(**inputs):
    import ml_dtypes
    import concourse.bacc as _bacc
    from concourse.bass_utils import run_bass_kernel_spmd as _run

    g = {k: np.asarray(v) for k, v in inputs.items()}
    m, c, f = ({k[len(pre):]: v for k, v in g.items() if k.startswith(pre)} for pre in ("L0_attn_", "L0_xattn_", "L0_ffn_"))
    kv = np.concatenate([c["Wk"], c["Wv"]], axis=0).reshape(XH * XD, 2, D)
    shape, masks = _shape_tables()
    arrays = {
        "mix": [_rows(m["W_in"], KD), _rows(m["conv_w"], CF), _rows(m["conv_b"], CF), _rows(m["norm_w"], XF),
                _spread(m["A"]), _spread(m["dt_bias"]), _rows(np.repeat(m["D"], HP), XF), _rows(m["W_out"], XF)],
        "cross": [_rows(c["Wq"].T, KD), _rows(kv[:, 0].T, KD), _rows(kv[:, 1].T, KD)],
        "latent": [_rows(f["ln1_w"], KD), _rows(f["ln2_w"], KD),
                   _rows(np.concatenate([f["kv_d_w"], f["q_d_w"]], axis=1), KD), _rows(f["rope_k_w"], KD),
                   np.concatenate([f["k_u_w"], f["q_u_w"]], axis=0),
                   np.concatenate([f["v_u_w"], np.concatenate([f["rope_q_w"], f["rope_q_w"]], axis=1)], axis=0),
                   _rows(f["o_w"], KD), _rows(f["router_w"], KD), _spread(f["router_b"])],
        "experts": [], "shape": [shape],
    }
    gate = np.concatenate([f["sh_gate"][None], f["r_gate"]], axis=0)
    up = np.concatenate([f["sh_up"][None], f["r_up"]], axis=0)
    down = np.concatenate([f["sh_down"][None], f["r_down"]], axis=0)
    gu = np.stack([gate, up], axis=2).reshape(NE, KD, P, 2, FI).transpose(2, 0, 1, 3, 4).reshape(P, -1)
    arrays["experts"] = [gu, down.transpose(1, 0, 2).reshape(P, -1)]

    nc = _bacc.Bacc("TRN2", target_bir_lowering=False, num_devices=1)
    data, packs = {}, {}
    for name, parts in arrays.items():
        data["pack_" + name] = np.ascontiguousarray(np.concatenate(parts, axis=1))
        packs[name] = nc.dram_tensor("pack_" + name, [P, WIDTH[name]], F32, kind="ExternalInput").ap()
    data["masks16"] = masks.astype(ml_dtypes.bfloat16)
    masks16 = nc.dram_tensor("masks16", [P, 3, P], BF16, kind="ExternalInput").ap()
    for name in ("x", "ctx_2048"):
        data[name + "_in"] = np.ascontiguousarray(g[name])
    x_ap = nc.dram_tensor("x_in", [NB, SEQ, D], F32, kind="ExternalInput").ap()
    c_ap = nc.dram_tensor("ctx_2048_in", [NB, SEQ, D], F32, kind="ExternalInput").ap()
    out = nc.dram_tensor("out_0", [NB, SEQ, D], F32, kind="ExternalOutput").ap()
    decoder_layer(nc, x_ap, c_ap, packs, masks16, out)
    r = _run(nc, [data], core_ids=[0])
    return r.results[0]["out_0"]
```

```python
from contextlib import ExitStack

import numpy as np

import concourse.bass as bass
from concourse import mybir

F32 = mybir.dt.float32
BF16 = mybir.dt.bfloat16
ALU = mybir.AluOpType
ACT = mybir.ActivationFunctionType
AX = mybir.AxisListType

P = 128
NB, SEQ, D = 4, 256, 256
T = SEQ // P
KD = D // P
DI, NHM, HP, NS = 512, 8, 64, 128
XF = DI // P
CF = XF + 2
TAPS = 4
WIN = 2 * DI + 2 * NS + NHM
XH, XD = 32, 8
AH, AR, AD = 16, 8, 16
LAT, NE, NR, FI = 64, 8, 7, 128
LN_EPS, X_EPS, RMS_EPS, GATE_EPS = 1e-5, 1e-6, 1e-5, 1e-5
NEG = -1e30

PACKS = {
    "mix": [("w_in", KD * WIN), ("conv_w", CF * TAPS), ("conv_b", CF), ("norm_w", XF), ("a", NHM), ("dt_bias", NHM),
            ("d_skip", XF), ("w_out", XF * D)],
    "cross": [("wq", KD * D), ("wk", KD * D), ("wv", KD * D)],
    "latent": [("ln1", KD), ("ln2", KD), ("down", KD * P), ("rope_k", KD * P), ("up", P), ("second", D),
               ("o_w", KD * D), ("router", KD * NR), ("router_b", NR)],
    "experts": [("gate_up", NE * KD * 2 * FI), ("down_w", NE * D)],
    "shape": [("ident", P), ("upto", P), ("after", P), ("block8", P), ("rope", 2 * SEQ), ("before", NR * NR)],
}
WIDTH = {pack: sum(n for _, n in parts) for pack, parts in PACKS.items()}

GAP = {
    "ctx": 0, "xk_p": 2, "xv": 3, "xk_s": 2, "xk_f": 3, "xk_m": 3,
    "l1a": 0, "l1b": 2, "l1c": 2, "dta": 1, "inx": 3, "dtb": 2, "cs": 2, "inz": 3,
    "s0a": 4, "s0b": 4, "s0c": 3, "s1a": 2, "s1b": 3, "s1c": 3, "oa": 2, "ob": 4,
    "l2a": 4, "l2b": 2, "l2c": 2, "xq_p": 2, "xq_s": 3, "xq_f": 3, "xq_m": 3,
    "x0": 14, "x1": 3, "x2": 3, "x3": 3, "xb0": 3, "x4": 1, "x5": 3, "x6": 3, "xb1": 3, "x7": 1, "x8": 3, "xb2": 2,
    "l3a": 2, "l3m": 2, "l3b": 2, "l3c": 2, "pa": 1, "pb": 3, "fk_f": 3, "fq_f": 2, "fk_m": 1, "fq_m": 2,
    "max0": 14, "max1": 2, "max2": 2, "max3": 2, "max4": 2, "max5": 2, "mta": 2, "mtb": 2,
    "f0": 5, "f1": 3, "fb0": 2, "f2": 1, "fb1": 2, "f3": 1, "fb2": 2, "f4": 1, "fb3": 3, "opa": 2, "opb": 2,
    "l4a": 2, "l4b": 2, "l4c": 2, "ra": 2, "rb": 3, "e0": 1, "e1": 3, "e2": 3, "e3": 3, "e4": 3, "e5": 3, "e6": 3,
    "e7": 3, "store": 5,
}
PERIOD = 130


def schedule():
    at, start = 0, {}
    for step, gap in GAP.items():
        at += gap
        start[step] = at
    return sorted(((step, b) for b in range(NB) for step in GAP), key=lambda sb: (start[sb[0]] + PERIOD * sb[1], sb[1]))


SCHEDULE = schedule()

WORK = {
    "l1b": [("xnT", 1, 0, "l1c")], "dta": [("dt_raw", 1, 0, "dta")],
    "inx": [("taps", 6, 2 * i + 1, "inx") for i in range(3)],
    "cs": [("ecs", 1, 0, "cs")], "inz": [("sz", 2, i, "inz") for i in range(2)],
    "s0a": [("gm", 2, 0, "s0a"), ("dtx", 2, 0, "s0a")], "s0b": [("state", 1, 0, "s0b")], "s0c": [("y", 2, 0, "s0c")],
    "s1a": [("gm", 2, 1, "s1a"), ("dtx", 2, 1, "s1a")], "s1b": [("yoff", 1, 0, "s1b")], "s1c": [("y", 2, 1, "s1c")],
    "ob": [("gate_ln", 1, 0, "ob"), ("x1", 1, 0, "ob")],
    "ctx": [("ctxT", 1, 0, "ctx")], "xk_p": [("xk_full", 1, 0, "xk_f")], "xk_s": [("xk_ln", 1, 0, "xk_s")],
    "xv": [("xv", 1, 0, "xv")],
    "l2b": [("xnT2", 1, 0, "l2c")], "xq_p": [("xq_full", 1, 0, "xq_f")], "xq_s": [("xq_ln", 1, 0, "xq_s")],
    **{f"xb{n}": [("xo", 3, n, f"xb{n}")] for n in range(3)},
    "l3b": [("xnT3", 1, 0, "l3c")],
    "pa": [("lat", 1, 0, "pa"), ("k_rope", 1, 0, "pa")],
    "pb": [("plain", 2, 0, "pb"), ("plain", 2, 1, "pb"), ("q_rope", 1, 0, "pb"), ("fv", 1, 0, "pb")],
    "mtb": [("maxT", 1, 0, "mtb")],
    **{f"f{n + 1}": [("ao", 4, n, f"fb{n}")] for n in range(4)},
    "opa": [("aoT", 1, 0, "opa")], "opb": [("h", 1, 0, "opb")],
    "l4b": [("hT", 1, 0, "l4c")], "ra": [("logits", 1, 0, "ra")],
    **{f"e{n}": [("hidden", NE, n, f"e{n}")] + [("acc", NE, n - 1, f"e{n}")] * (n > 0) for n in range(NE)},
    "store": [("acc", NE, NE - 1, "store")],
}
PAIR = {
    "s0a": [("L", 2, 0, "s0a")], "s1a": [("L", 2, 1, "s1a")],
    **{f"x{n}": [("xp", 16, 2 * n + i, f"x{n}") for i in range(2)] for n in range(8)},
    **{f"max{n}": [("mx", 6, n, f"max{n}")] for n in range(6)},
    **{f"f{n}": [("fp", 8, 2 * n + i, f"f{n}") for i in range(2)] for n in range(4)},
}
OUTS = {"x1": [("xot", 3, 0, "x3")], "x4": [("xot", 3, 1, "x6")], "x7": [("xot", 3, 2, "x8")]}
PROBS = {
    **{f"x{n}": [("xo_quad", 8, n, f"x{n + 1}")] * 2 for n in range(8)},
    **{f"f{n}": [("fo_ps", 4, n, f"f{n + 1}")] * 2 for n in range(4)},
}
PX = 4
SHARED = {
    "xn_0": {"l1b": [("xnT_ps", 1, 0, "l1b")], "l3b": [("xnT3_ps", 1, 0, "l3b")]},
    "xn_1": {"l2b": [("xnT2_ps", 1, 0, "l2b")], "l4b": [("hT_ps", 1, 0, "l4b")]},
    "full_k": {"xk_p": [("xk_diffs", 2, 1, "xk_m")], "pa": [("fk_diffs", 2, 1, "fk_m")]},
    "full_q": {"xq_p": [("xq_diffs", 2, 1, "xq_m")], "pb": [("fq_diffs", 2, 1, "fq_m")]},
    "parts_k": {"xk_f": [("xk_to_dram", 96, 95, "xk_m")], "fk_f": [("fk_to_dram", 96, 95, "fk_m")]},
    "parts_q": {"xq_f": [("xq_to_dram", 96, 95, "xq_m")], "fq_f": [("fq_to_dram", 96, 95, "fq_m")]},
}


def plan(claims, slots):
    position = {sb: n for n, sb in enumerate(SCHEDULE)}
    given, last = {}, [(-1, None, None, i - slots) for i in range(slots)]
    for n, (step, b) in enumerate(SCHEDULE):
        for i, (name, per, k, until) in enumerate(claims.get(step, [])):
            slot = min(range(slots), key=lambda j: (last[j][0], last[j][3]))
            assert last[slot][0] <= n and (last[slot][0] < n or last[slot][2] == step), ("no slot", step, b)
            given[step, b, i] = (slot, last[slot][1])
            last[slot] = (position[until, b], (name, b * per + k + 1), step, len(given))
    return given


SHARED_AT = {name: plan(claims, 1) for name, claims in SHARED.items()}
WORK_AT, PAIR_AT, OUT_AT, PROB_AT = plan(WORK, 3), plan(PAIR, 2), plan(OUTS, 2), plan(PROBS, PX)


def decoder_layer(nc, x, ctx_in, packs, masks16, out):
    stack = ExitStack()
    with stack:
        def sb(name, shape, dt=F32):
            return stack.enter_context(nc.sbuf_tensor(name, shape, dt))

        class Semaphores(dict):
            def __missing__(self, name):
                self[name] = stack.enter_context(nc.semaphore("s_" + name))
                return self[name]

        s = Semaphores()
        dram = [[nc.dram_tensor(f"scratch_{kind}_{b}", [XH, 3, XD, SEQ], BF16, kind="Internal").ap()
                 for kind in ("xk", "xq", "fk", "fq")] for b in range(NB)]
        KIND = {"xk": 0, "xq": 1, "fk": 2, "fq": 3}

        def after_last_user(engine, table, step, b, i=0):
            before_us = table[step, b, i][1]
            if before_us is not None:
                engine.wait_ge(s[before_us[0]], before_us[1])

        work_ps = [stack.enter_context(nc.psum_tensor(f"work{i}", [P, 512], F32)) for i in range(3)]
        pair_ps = [stack.enter_context(nc.psum_tensor(f"pair{i}", [P, 1024], F32)) for i in range(2)]
        outs_ps = stack.enter_context(nc.psum_tensor("outs", [P, 512], F32))

        def work(step, b, i=0):
            return work_ps[WORK_AT[step, b, i][0]]

        def pair(step, b, i=0):
            return pair_ps[PAIR_AT[step, b, i][0]]

        def outs(step, b):
            k = OUT_AT[step, b, 0][0]
            return outs_ps[:, k * 256:(k + 1) * 256]

        w = {name: sb("w_" + name, [P, n]) for name, n in WIDTH.items()}

        def part(pack, name):
            at = 0
            for n, width in PACKS[pack]:
                if n == name:
                    return w[pack][:, at:at + width]
                at += width
            raise KeyError(name)

        w_in = part("mix", "w_in").rearrange("p (k n) -> p k n", k=KD)
        conv_w, conv_b, d_skip = part("mix", "conv_w"), part("mix", "conv_b"), part("mix", "d_skip")
        norm_w, a_row, dt_bias = part("mix", "norm_w"), part("mix", "a"), part("mix", "dt_bias")
        w_out = part("mix", "w_out").rearrange("p (f n) -> p f n", f=XF)
        wq, wk, wv = (part("cross", n).rearrange("p (k n) -> p k n", k=KD) for n in ("wq", "wk", "wv"))
        ln1_w, ln2_w = part("latent", "ln1"), part("latent", "ln2")
        w_down = part("latent", "down").rearrange("p (k n) -> p k n", k=KD)
        w_rope_k = part("latent", "rope_k").rearrange("p (k n) -> p k n", k=KD)
        w_up, w_second = part("latent", "up"), part("latent", "second")
        w_o = part("latent", "o_w").rearrange("p (k n) -> p k n", k=KD)
        w_router = part("latent", "router").rearrange("p (k n) -> p k n", k=KD)
        router_b = part("latent", "router_b")
        gate_up = part("experts", "gate_up").rearrange("p (e k g n) -> p e k g n", e=NE, k=KD, g=2)
        down_w = part("experts", "down_w").rearrange("p (e n) -> p e n", e=NE)
        ident, upto, after, block8 = (part("shape", n) for n in ("ident", "upto", "after", "block8"))
        rope_cs = part("shape", "rope")
        before = part("shape", "before").rearrange("p (e j) -> p e j", e=NR)
        m16 = sb("m16", [P, 3, P], BF16)
        ident16, mask_q, mask_k = m16[:, 0, :], m16[:, 1, :], m16[:, 2, :]
        ones = sb("ones", [P, 1])
        eps = sb("eps", [P, 3])
        w_rope_k2 = sb("w_rope_k2", [P, KD, P])
        w_rope_q2 = sb("w_rope_q2", [P, P])

        def per_batch(name, shape, dt=F32, n=NB):
            tiles = [sb(f"{name}_{i}", shape, dt) for i in range(n)]
            return [tiles[b % n] for b in range(NB)]

        NF = 3
        x0 = per_batch("x0", [P, T, D], n=NF)
        ctx_t = per_batch("ctx", [P, T, D], n=1)
        stats = per_batch("stats", [P, 4, T, 6], n=2)
        mv = per_batch("mv", [P, 4, T, 2])
        rstd = per_batch("rstd", [P, 6, T])
        xn = [sb(f"xn{i}", [P, T, D]) for i in range(2)]
        xnT = per_batch("xnT", [P, KD, SEQ], n=2)
        conv = per_batch("conv", [P, CF, SEQ], n=1)
        xbc = conv
        sz = per_batch("sz", [P, XF, SEQ], n=1)
        sp = per_batch("sp", [P, 8, T * NHM], n=2)
        dt_t = per_batch("dt", [P, T, NHM])
        dA = per_batch("dA", [P, T, NHM])
        ecs = per_batch("ecs", [P, T, 2, NHM], n=2)
        R = per_batch("R", [P, NHM, P], n=1)
        L = per_batch("L", [P, NHM, P], n=1)
        Gm = per_batch("Gm", [P, P], n=1)
        btok = per_batch("btok", [P, P], n=1)
        dtx = per_batch("dtx", [P, DI], n=1)
        dtxd = per_batch("dtxd", [P, DI], n=1)
        state = per_batch("state", [P, DI], n=1)
        yoff = dtxd
        yg = per_batch("yg", [P, XF, SEQ], n=1)
        xD = yg
        ysq = sz
        x1 = per_batch("x1", [P, T, D], n=NF)
        ctxT = per_batch("ctxT", [P, KD, SEQ], n=1)
        rs = {k: sb("rs_" + k, [P, 512]) for k in ("xk", "xq")}
        full = {k: sb("full_" + k, [P, 512]) for k in ("xk", "xq")}
        full["fk"], full["fq"] = full["xk"], full["xq"]
        parts = {k: sb("parts_" + k, [P, 2, 3, SEQ], BF16) for k in ("xk", "xq")}
        parts["fk"], parts["fq"] = parts["xk"], parts["xq"]
        NST = 1
        xstack = {k: per_batch("stack_" + k, [P, XH // 2, SEQ], BF16, n=NST) for k in ("xk", "xq")}
        fstack = {k: per_batch("stack_" + k, [P, AH, SEQ], BF16, n=NST) for k in ("fk", "fq")}
        xvals = per_batch("xvals", [P, T, XH, 32], n=1)
        fvals = per_batch("fvals", [P, T, AH, 32], n=1)
        probs_sb = [sb(f"probs{i}", [P, 2, 512]) for i in range(PX)]

        def probs(step, b, i):
            return probs_sb[PROB_AT[step, b, i][0]]

        xot = per_batch("xot", [P, SEQ], n=1)
        xden = per_batch("xden", [P, T, 12], n=1)
        x2 = per_batch("x2", [P, T, D], n=2)
        y3 = x1
        lat = per_batch("lat", [P, SEQ], n=1)
        rope_t = sb("rope_t", [P, 2, SEQ])
        fmx = per_batch("fmx", [P, T, AH])
        fmr = per_batch("fmr", [P, T * AH])
        fmp = per_batch("fmp", [P, T, 3, AH], BF16, n=2)
        maxT = per_batch("maxT", [3 * AH, SEQ], BF16, n=1)
        fot = per_batch("fot", [P, SEQ], n=1)
        fden = per_batch("fden", [P, T, 4], n=1)
        ao = per_batch("ao", [P, T, D], n=1)
        aoT = per_batch("aoT", [P, KD, SEQ], n=1)
        h4 = x1
        hT = per_batch("hT", [P, KD, SEQ], n=1)
        rt = per_batch("rt", [P, 6, T, NR], n=2)
        cmp_ = per_batch("cmp", [P, 2, T, NR * NR], n=1)
        rsum = per_batch("rsum", [P, 2, T])
        gates = per_batch("gates", [P, T, NR])
        sg = per_batch("sg", [P, SEQ], n=2)
        hid = sg
        acc = x0

        block = stack.enter_context(nc.Block())

        @block.sync
        def _(sync):
            x_d = x.rearrange("b (t p) d -> b p t d", p=P)
            c_d = ctx_in.rearrange("b (t p) d -> b p t d", p=P)
            out_d = out.rearrange("b (t p) d -> b p t d", p=P)
            sync.dma_start(x0[0][:], x_d[0]).then_inc(s["x_in_first"], 16)
            for name in ("shape", "mix"):
                sync.dma_start(w[name][:], packs[name]).then_inc(s["w_first"], 16)
            for b in range(1, NF):
                sync.dma_start(x0[b][:], x_d[b]).then_inc(s["x_in"], 16)
            sync.dma_start(ctx_t[0][:], c_d[0]).then_inc(s["ctx_in"], 16)
            sync.dma_start(m16[:], masks16).then_inc(s["w_second"], 16)
            for name in ("cross", "latent"):
                sync.dma_start(w[name][:], packs[name]).then_inc(s["w_second"], 16)
            sync.dma_start(w["experts"][:], packs["experts"]).then_inc(s["w_experts"], 16)

            def ctx(b):
                if b + 1 < NB:
                    sync.wait_ge(s["ctxT"], b + 1)
                    sync.dma_start(ctx_t[b + 1][:], c_d[b + 1]).then_inc(s["ctx_in"], 16)

            def split(kind, b, stack_tile, used):
                d = dram[b][KIND[kind]]
                for half in range(2):
                    for g in range(3):
                        if g < 2:
                            sync.wait_ge(s[f"{kind}_rounded"], 2 * b + g + 1)
                        else:
                            sync.wait_ge(s[f"{kind}_diffs"], 2 * b + 2)
                        sync.dma_start(d[16 * half:16 * half + 16, g], parts[kind][:, half, g, :])\
                            .then_inc(s[f"{kind}_to_dram"], 16)
                sync.wait_ge(s[f"{kind}_to_dram"], 16 * 6 * (b + 1))
                if b >= NST:
                    sync.wait_ge(s[used[0]], used[1] * (b - NST + 1))
                elif kind == "fk":
                    sync.wait_ge(s["pool_init"], NST)
                if kind[1] == "k":
                    runs = [((0, 3), 0), ((0, 2), 24), ((0, 1), 40)]
                else:
                    runs = [(0, 0), (0, 8), (0, 16), (1, 24), (1, 32), (2, 40)]
                for a in range(2):
                    if kind[0] == "x":
                        src = d.rearrange("(q a) g d t -> a g d q t", a=2)[a]
                        row = 64 * a
                    else:
                        src = d.rearrange("(a q) g d t -> a g d q t", a=2)[a]
                        row = 48 * a
                    for run, base in runs:
                        if kind[1] == "k":
                            n = run[1]
                            sr = src[0:n].rearrange("g d q t -> (g d) q t")
                        else:
                            n, sr = 1, src[run]
                        sync.dma_start(stack_tile[row + base:row + base + 8 * n, :, :], sr)\
                            .then_inc(s[f"{kind}_stack"], 16)

            def maxes(b):
                sync.wait_ge(s["maxT"], b + 1)
                for c in range(3):
                    sync.dma_start(fstack["fq"][b][96 + c:97 + c, :, :], maxT[b][AH * c:AH * c + AH, :])\
                        .then_inc(s["max_stack"], 16)

            def store(b):
                sync.wait_ge(s["acc"], NE * (b + 1))
                sync.dma_start(out_d[b], acc[b][:]).then_inc(s["stored"], 16)
                if b + NF < NB:
                    sync.wait_ge(s["stored"], 16 * (b + 1))
                    sync.dma_start(x0[b + NF][:], x_d[b + NF]).then_inc(s["x_in"], 16)

            steps = {"ctx": ctx, "xk_m": lambda b: split("xk", b, xstack["xk"][b], ("xs_ps", 16)),
                     "xq_m": lambda b: split("xq", b, xstack["xq"][b], ("xs_ps", 16)),
                     "fk_m": lambda b: split("fk", b, fstack["fk"][b], ("fs_ps", 8)),
                     "fq_m": lambda b: split("fq", b, fstack["fq"][b], ("fs_ps", 8)),
                     "mtb": maxes, "store": store}
            for step, b in SCHEDULE:
                if step in steps:
                    steps[step](b)
            sync.wait_ge(s["stored"], 16 * NB)

        RUNS = {"xk": 6, "xq": 12, "fk": 6, "fq": 12}

        @block.tensor
        def _(pe):
            mm = nc.tensor.matmul

            def claim(table, step, b, i=0):
                after_last_user(pe, table, step, b, i)

            def transposes(step, b, ready, src, done):
                pe.wait_ge(s[ready], b + 1)
                claim(WORK_AT, step, b)
                ps = work(step, b)
                for k in range(KD):
                    for t in range(T):
                        last = nc.tensor.transpose(ps[:, k * SEQ + t * P:k * SEQ + (t + 1) * P],
                                                   src[:, t, k * P:(k + 1) * P], ident)
                last.then_inc(s[done], 1)

            def ln1(b):
                if b == 0:
                    pe.wait_ge(s["w_first"], 32)
                transposes("l1b", b, "xn", xn[0], "xnT_ps")

            def dt(b):
                pe.wait_ge(s["xnT"], b + 1)
                claim(WORK_AT, "dta", b)
                for t in range(T):
                    for k in range(KD):
                        last = mm(work("dta", b)[:, t * NHM:(t + 1) * NHM], xnT[b][:, k, t * P:(t + 1) * P],
                                  w_in[:, k, WIN - NHM:WIN], start=k == 0, stop=k == KD - 1)
                last.then_inc(s["dt_ps"], 1)

            def project(step, b, i, first, done):
                claim(WORK_AT, step, b, i)
                for f in range(2):
                    for k in range(KD):
                        last = mm(work(step, b, i)[:, f * SEQ:(f + 1) * SEQ],
                                  w_in[:, k, first + f * P:first + (f + 1) * P], xnT[b][:, k, :],
                                  start=k == 0, stop=k == KD - 1)
                last.then_inc(s[done], 1)

            def inx(b):
                for i in range(CF // 2):
                    project("inx", b, i, DI + 2 * i * P, "xbc_ps")

            def inz(b):
                for i in range(XF // 2):
                    project("inz", b, i, 2 * i * P, "z_ps")

            def cs(b):
                pe.wait_ge(s["dA"], b + 1)
                claim(WORK_AT, "cs", b)
                for t in range(T):
                    o = work("cs", b)[:, t * 2 * NHM:(t + 1) * 2 * NHM]
                    mm(o[:, 0:NHM], upto, dA[b][:, t, :], start=True, stop=True)
                    last = mm(o[:, NHM:2 * NHM], after, dA[b][:, t, :], start=True, stop=True)
                last.then_inc(s["cs_ps"], 1)

            def ssd_a(t, b):
                step, tok, n = f"s{t}a", slice(t * P, (t + 1) * P), T * b + t
                pe.wait_ge(s["xbc"], b + 1)
                claim(WORK_AT, step, b, 0)
                g = work(step, b, 0)
                last = mm(g[:, 0:P], xbc[b][:, XF, tok], xbc[b][:, XF + 1, tok], start=True, stop=True)
                if t == 0:
                    last = nc.tensor.transpose(g[:, P:2 * P], xbc[b][:, XF, tok], ident)
                last.then_inc(s["g_ps"], 1)
                claim(WORK_AT, step, b, 1)
                for f in range(XF):
                    last = nc.tensor.transpose(work(step, b, 1)[:, f * P:(f + 1) * P], xbc[b][:, f, tok], ident)
                last.then_inc(s["xtok_ps"], 1)
                pe.wait_ge(s["R"], n + 1)
                claim(PAIR_AT, step, b)
                for i in range(2):
                    last = mm(pair(step, b)[:, 512 * i:512 * (i + 1)], after, R[b][:, 4 * i:4 * i + 4, :],
                              start=True, stop=True)
                last.then_inc(s["diff_ps"], 1)

            def ssd_b(t, b):
                step, tok = f"s{t}b", slice(t * P, (t + 1) * P)
                claim(WORK_AT, step, b, 0)
                if t == 0:
                    pe.wait_ge(s["dtxd"], b + 1)
                    mm(work(step, b)[:, :], btok[b][:, :], dtxd[b][:, :], start=True, stop=True)\
                        .then_inc(s["state_ps"], 1)
                else:
                    pe.wait_ge(s["state"], b + 1)
                    mm(work(step, b)[:, :], xbc[b][:, XF + 1, tok], state[b][:, :], start=True, stop=True)\
                        .then_inc(s["yoff_ps"], 1)

            def ssd_c(t, b):
                step, n = f"s{t}c", T * b + t
                pe.wait_ge(s["M"], n + 1)
                pe.wait_ge(s["dtx"], n + 1)
                if t == 1:
                    pe.wait_ge(s["yoff"], b + 1)
                claim(WORK_AT, step, b)
                y = work(step, b)
                for hp in range(XF):
                    for a in range(2):
                        head = 2 * hp + a
                        last = mm(y[64 * a:64 * a + 64, hp * P:(hp + 1) * P], dtx[b][:, head * HP:(head + 1) * HP],
                                  L[b][:, head, :], start=True, stop=t == 0)
                    if t == 1:
                        last = mm(y[:, hp * P:(hp + 1) * P], yoff[b][:, hp * P:(hp + 1) * P], ident,
                                  start=False, stop=True)
                last.then_inc(s["y_ps"], 1)

            def out_proj(b):
                pe.wait_ge(s["ysum"], b + 1)
                claim(WORK_AT, "ob", b, 0)
                for t in range(T):
                    last = mm(work("ob", b, 0)[:, t:t + 1], ysq[b][:, 0, t * P:(t + 1) * P], ones[:, :],
                              start=True, stop=True)
                last.then_inc(s["ss_ps"], 1)
                if b == 0:
                    pe.wait_ge(s["w_norm_out"], XF)
                claim(WORK_AT, "ob", b, 1)
                for t in range(T):
                    for f in range(XF):
                        last = mm(work("ob", b, 1)[:, t * D:(t + 1) * D], yg[b][:, f, t * P:(t + 1) * P],
                                  w_out[:, f, :], start=f == 0, stop=f == XF - 1)
                last.then_inc(s["out_ps"], 1)

            def ctx(b):
                if b == 0:
                    pe.wait_ge(s["w_second"], 48)
                pe.wait_ge(s["ctx_in"], 16 * (b + 1))
                claim(WORK_AT, "ctx", b)
                for k in range(KD):
                    for t in range(T):
                        last = nc.tensor.transpose(work("ctx", b)[:, k * SEQ + t * P:k * SEQ + (t + 1) * P],
                                                   ctx_t[b][:, t, k * P:(k + 1) * P], ident)
                last.then_inc(s["ctxT_ps"], 1)

            def heads_p(kind, b, weight, src, src_ready):
                pe.wait_ge(s[src_ready], b + 1)
                claim(WORK_AT, f"{kind}_p", b)
                for f in range(2):
                    for k in range(KD):
                        last = mm(work(f"{kind}_p", b)[:, f * SEQ:(f + 1) * SEQ], weight[:, k, f * P:(f + 1) * P],
                                  src[b][:, k, :], start=k == 0, stop=k == KD - 1)
                last.then_inc(s[f"{kind}_ps"], 1)

            def heads_s(kind, b):
                pe.wait_ge(s[f"{kind}_sq"], b + 1)
                claim(WORK_AT, f"{kind}_s", b)
                mm(work(f"{kind}_s", b)[:, :], block8, full[kind][:, :], start=True, stop=True)\
                    .then_inc(s[f"{kind}_sum"], 1)

            def xv(b):
                claim(WORK_AT, "xv", b)
                for t in range(T):
                    for k in range(KD):
                        last = mm(work("xv", b)[:, t * D:(t + 1) * D], ctxT[b][:, k, t * P:(t + 1) * P], wv[:, k, :],
                                  start=k == 0, stop=k == KD - 1)
                last.then_inc(s["xv_ps"], 1)

            def x_scores(b, n):
                step = f"x{n}"
                if n == 0:
                    pe.wait_ge(s["xk_stack"], 16 * RUNS["xk"] * (b + 1))
                    pe.wait_ge(s["xq_stack"], 16 * RUNS["xq"] * (b + 1))
                for i in range(2):
                    q = 2 * n + i
                    claim(PAIR_AT, step, b, i)
                    for a in range(2):
                        rows = slice(64 * a, 64 * a + 6 * XD)
                        for kt in range(T):
                            last = mm(pair(step, b, i)[:, a * 512 + kt * SEQ:a * 512 + (kt + 1) * SEQ],
                                      xstack["xk"][b][rows, q, kt * P:(kt + 1) * P], xstack["xq"][b][rows, q, :],
                                      start=True, stop=True)
                    last.then_inc(s["xs_ps"], 1)

            def x_values(b, n):
                rnd, i = n // 3, n % 3
                q = 16 * b + 2 * n
                if n == 0:
                    pe.wait_ge(s["xv"], b + 1)
                if i == 0:
                    claim(OUT_AT, f"x{3 * rnd + 1}", b)
                pe.wait_ge(s["xp"], q + 2)
                o = outs(f"x{3 * rnd + 1}", b)
                end = min(2, 7 - 3 * rnd)
                for kt in range(T):
                    for j in range(4):
                        head = 4 * n + j
                        last = mm(o[32 * j:32 * j + 32, :], xvals[b][:, kt, head, :],
                                  probs(f"x{n}", b, j // 2)[:, j % 2, kt * SEQ:(kt + 1) * SEQ],
                                  start=i == 0 and kt == 0, stop=i == end and kt == T - 1)
                last.then_inc(s["xo_quad"], 1)

            def x_back(b, rnd):
                step = f"xb{rnd}"
                pe.wait_ge(s["xot"], 3 * b + rnd + 1)
                claim(WORK_AT, step, b)
                for t in range(T):
                    last = nc.tensor.transpose(work(step, b)[:, t * P:(t + 1) * P], xot[b][:, t * P:(t + 1) * P],
                                               ident)
                last.then_inc(s["xback_ps"], 1)

            def cross(b, n):
                if n < 8:
                    x_scores(b, n)
                if n > 0:
                    x_values(b, n - 1)

            def proj_a(b):
                pe.wait_ge(s["xnT3"], b + 1)
                claim(WORK_AT, "pa", b, 0)
                for k in range(KD):
                    last = mm(work("pa", b, 0)[:, 0:SEQ], w_down[:, k, :], xnT[b][:, k, :],
                              start=k == 0, stop=k == KD - 1)
                last.then_inc(s["lat_ps"], 1)
                if b == 0:
                    pe.wait_ge(s["pool_init"], NST + 10)
                claim(WORK_AT, "pa", b, 1)
                for i, weight in enumerate((w_rope_k, w_rope_k2)):
                    for k in range(KD):
                        last = mm(work("pa", b, 1)[:, i * SEQ:(i + 1) * SEQ], weight[:, k, :], xnT[b][:, k, :],
                                  start=k == 0, stop=k == KD - 1)
                last.then_inc(s["kr_ps"], 1)

            def proj_b(b):
                pe.wait_ge(s["lat"], b + 1)
                kv, qd = slice(0, LAT), slice(LAT, 2 * LAT)
                for i, rows in enumerate((kv, qd)):
                    claim(WORK_AT, "pb", b, i)
                    mm(work("pb", b, i)[:, 0:SEQ], w_up[rows, :], lat[b][rows, :], start=True, stop=True)\
                        .then_inc(s["plain_ps"], 1)
                claim(WORK_AT, "pb", b, 2)
                mm(work("pb", b, 2)[:, 0:SEQ], w_second[qd, 0:P], lat[b][qd, :], start=True, stop=True)
                mm(work("pb", b, 2)[:, SEQ:2 * SEQ], w_rope_q2[qd, :], lat[b][qd, :], start=True, stop=True)\
                    .then_inc(s["qr_ps"], 1)
                claim(WORK_AT, "pb", b, 3)
                for t in range(T):
                    last = mm(work("pb", b, 3)[:, t * D:(t + 1) * D], lat[b][kv, t * P:(t + 1) * P],
                              w_second[kv, :], start=True, stop=True)
                last.then_inc(s["fv_ps"], 1)

            def f_max(b, n):
                step = f"max{n}"
                if n == 0:
                    pe.wait_ge(s["fk_stack"], 16 * RUNS["fk"] * (b + 1))
                    pe.wait_ge(s["fq_stack"], 16 * RUNS["fq"] * (b + 1))
                claim(PAIR_AT, step, b)
                ps = pair(step, b)
                if n < 2:
                    t, heads, keys = 0, range(8 * n, 8 * n + 8), P
                else:
                    t, heads, keys = 1, range(4 * (n - 2), 4 * (n - 2) + 4), SEQ
                for i, head in enumerate(heads):
                    o = ps[:, i * keys:(i + 1) * keys]
                    mm(o, fstack["fq"][b][0:96, head, t * P:(t + 1) * P], fstack["fk"][b][0:96, head, 0:keys],
                       start=True, stop=False)
                    last = mm(o[:, keys - P:keys], ident16, mask_q, start=False, stop=True)
                last.then_inc(s["fm_ps"], 1)

            def max_back(b):
                pe.wait_ge(s["max_parts"], b + 1)
                claim(WORK_AT, "mtb", b)
                o16 = work("mtb", b)[:, 0:P].bitcast(BF16)
                for t in range(T):
                    last = nc.tensor.transpose(o16[0:3 * AH, t * P:(t + 1) * P],
                                               fmp[b][:, t, :, :].rearrange("p c h -> p (c h)"), ident16)
                last.then_inc(s["maxT_ps"], 1)

            def f_scores(b, n):
                step = f"f{n}"
                if n == 0:
                    pe.wait_ge(s["max_stack"], 16 * 3 * (b + 1))
                for i in range(2):
                    claim(PAIR_AT, step, b, i)
                    for a in range(2):
                        head = 4 * n + 2 * i + a
                        o = pair(step, b, i)[:, 512 * a:512 * a + 384]
                        mm(o[:, 0:SEQ], fstack["fk"][b][0:99, head, 0:P], fstack["fq"][b][0:99, head, :],
                           start=True, stop=False)
                        mm(o[:, 0:P], ident16, mask_k, start=False, stop=True)
                        mm(o[:, SEQ:SEQ + P], fstack["fk"][b][0:99, head, P:SEQ], fstack["fq"][b][0:99, head, P:SEQ],
                           start=True, stop=False)
                        last = mm(o[:, SEQ:SEQ + P], ident16, mask_k, start=False, stop=True)
                    last.then_inc(s["fs_ps"], 1)

            def f_values(b, n):
                q = 8 * b + 2 * n
                if n == 0:
                    pe.wait_ge(s["fv"], b + 1)
                claim(WORK_AT, f"f{n + 1}", b)
                pe.wait_ge(s["fp"], q + 2)
                o = work(f"f{n + 1}", b)[:, 0:SEQ]
                for kt in range(T):
                    for j in range(4):
                        pr = probs(f"f{n}", b, j // 2)[:, j % 2, :]
                        last = mm(o[32 * j:32 * j + 32, kt * P:SEQ], fvals[b][:, kt, 4 * n + j, :],
                                  pr[:, 0:SEQ] if kt == 0 else pr[:, SEQ:SEQ + P], start=kt == 0, stop=kt == T - 1)
                last.then_inc(s["fo_ps"], 1)

            def f_back(b, n):
                pe.wait_ge(s["fot"], 4 * b + n + 1)
                for t in range(T):
                    last = nc.tensor.transpose(work(f"f{n + 1}", b)[:, SEQ + t * P:SEQ + (t + 1) * P], fot[b][:, t * P:(t + 1) * P],
                                               ident)
                last.then_inc(s["fback_ps"], 1)

            def causal(b, n):
                if n < 4:
                    f_scores(b, n)
                if n > 0:
                    f_values(b, n - 1)

            def oproj_a(b):
                pe.wait_ge(s["ao"], 4 * (b + 1))
                claim(WORK_AT, "opa", b)
                for k in range(KD):
                    for t in range(T):
                        last = nc.tensor.transpose(work("opa", b)[:, k * SEQ + t * P:k * SEQ + (t + 1) * P],
                                                   ao[b][:, t, k * P:(k + 1) * P], ident)
                last.then_inc(s["aoT_ps"], 1)

            def oproj_b(b):
                pe.wait_ge(s["aoT"], b + 1)
                claim(WORK_AT, "opb", b)
                for t in range(T):
                    for k in range(KD):
                        last = mm(work("opb", b)[:, t * D:(t + 1) * D], aoT[b][:, k, t * P:(t + 1) * P],
                                  w_o[:, k, :], start=k == 0, stop=k == KD - 1)
                last.then_inc(s["o_ps"], 1)

            def router(b):
                pe.wait_ge(s["hT"], b + 1)
                claim(WORK_AT, "ra", b)
                for t in range(T):
                    for k in range(KD):
                        last = mm(work("ra", b)[:, t * NR:(t + 1) * NR], hT[b][:, k, t * P:(t + 1) * P],
                                  w_router[:, k, :], start=k == 0, stop=k == KD - 1)
                last.then_inc(s["router_ps"], 1)

            def expert(b, e):
                n = NE * b + e
                if n == 0:
                    pe.wait_ge(s["w_experts"], 16)
                claim(WORK_AT, f"e{e}", b, 0)
                for g in range(2):
                    for k in range(KD):
                        last = mm(work(f"e{e}", b, 0)[:, g * SEQ:(g + 1) * SEQ], gate_up[:, e, k, g, :],
                                  hT[b][:, k, :], start=k == 0, stop=k == KD - 1)
                last.then_inc(s["gu_ps"], 1)
                if e > 0:
                    expert_down(b, e - 1)

            def expert_down(b, e):
                n, at = NE * b + e, ("store", b, 0) if e == NE - 1 else (f"e{e + 1}", b, 1)
                pe.wait_ge(s["hidden"], n + 1)
                claim(WORK_AT, *at)
                for t in range(T):
                    last = mm(work(*at)[:, t * D:(t + 1) * D], hid[n % 2][:, t * P:(t + 1) * P],
                              down_w[:, e, :], start=True, stop=True)
                last.then_inc(s["down_ps"], 1)

            steps = {"l1b": ln1, "dta": dt, "inx": inx, "cs": cs, "inz": inz, "ob": out_proj,
                     **{f"s{t}{c}": (lambda b, f=f, t=t: f(t, b)) for t in range(T)
                        for c, f in (("a", ssd_a), ("b", ssd_b), ("c", ssd_c))},
                     "ctx": ctx, "xk_p": lambda b: heads_p("xk", b, wk, ctxT, "ctxT"), "xv": xv,
                     "xk_s": lambda b: heads_s("xk", b), "xq_s": lambda b: heads_s("xq", b),
                     "l2b": lambda b: transposes("l2b", b, "xn2", xn[1], "xnT2_ps"),
                     "xq_p": lambda b: heads_p("xq", b, wq, xnT, "xnT2"),
                     **{f"x{n}": lambda b, n=n: cross(b, n) for n in range(9)},
                     **{f"xb{n}": lambda b, n=n: x_back(b, n) for n in range(3)},
                     "l3b": lambda b: transposes("l3b", b, "xn3", xn[0], "xnT3_ps"), "pa": proj_a, "pb": proj_b,
                     **{f"max{n}": lambda b, n=n: f_max(b, n) for n in range(6)}, "mtb": max_back,
                     **{f"f{n}": lambda b, n=n: causal(b, n) for n in range(5)},
                     **{f"fb{n}": lambda b, n=n: f_back(b, n) for n in range(4)},
                     "opa": oproj_a, "opb": oproj_b,
                     "l4b": lambda b: transposes("l4b", b, "xn4", xn[1], "hT_ps"), "ra": router,
                     **{f"e{n}": lambda b, n=n: expert(b, n) for n in range(NE)},
                     "store": lambda b: expert_down(b, NE - 1)}
            for step, b in SCHEDULE:
                if step in steps:
                    steps[step](b)

        @block.scalar
        def _(act):
            count = [0]

            tables = [None]

            def run(out_, in_, func, **kw):
                if func in (ACT.Ln, ACT.Exp) and tables[0] != "ln_exp":
                    nc.scalar.preload_act_table_set("natural_log_exp_and_others")
                    tables[0] = "ln_exp"
                elif func == ACT.Silu:
                    tables[0] = "silu"
                return nc.scalar.activation(out_, in_, func, **kw)

            def then(ins):
                count[0] += 1
                ins.then_inc(s["act_chain"], 1)
                act.wait_ge(s["act_chain"], count[0])

            def inv_sqrt(b, ready, value, dst, scale, eps_i, done):
                act.wait_ge(s[ready], value)
                then(run(dst, rs_in[0], ACT.Ln, scale=scale, bias=eps[:, eps_i:eps_i + 1]))
                run(dst, dst, ACT.Exp, scale=-0.5).then_inc(s[done], 1)

            rs_in = [None]

            def ln(i, b):
                if i == 0 and b == 0:
                    act.wait_ge(s["eps"], 3)
                rs_in[0] = mv[b][:, i, :, 1]
                inv_sqrt(b, f"mv{i}", b + 1, rstd[b][:, i, :], 1.0, 0, f"rstd{i}")

            def rms3(b):
                rs_in[0] = rstd[b][:, 4, :]
                inv_sqrt(b, "ms3", b + 1, rstd[b][:, 5, :], 1.0, 0, "rms3")

            def dt(b):
                act.wait_ge(s["dt_abs"], b + 1)
                then(run(sp[b][:, 2, :], sp[b][:, 1, :], ACT.Exp, scale=-1.0))
                run(sp[b][:, 3, :], sp[b][:, 2, :], ACT.Ln, bias=1.0).then_inc(s["dt_exp"], 1)

            def inx(b):
                for i in range(CF // 2):
                    act.wait_ge(s["xbc_ps"], 3 * b + i + 1)
                    if b > 0 and i == 0:
                        act.wait_ge(s["y_done"], 2 * b)
                    ps = work("inx", b, i)
                    for f in range(2):
                        c = 2 * i + f
                        last = run(conv[b][:, c, :], ps[:, f * SEQ:(f + 1) * SEQ], ACT.Identity,
                                   scale=conv_w[:, c * TAPS + 3:c * TAPS + 4], bias=conv_b[:, c:c + 1])
                    last.then_inc(s["conv_in"], 1)

            def cs(b):
                act.wait_ge(s["cs_ps"], b + 1)
                run(ecs[b][:, :, :, :].rearrange("p t c h -> p (t c h)"), work("cs", b)[:, 0:T * 2 * NHM], ACT.Exp)\
                    .then_inc(s["ecs"], 1)

            def inz(b):
                act.wait_ge(s["taps"], CF * (b + 1))
                run(xbc[b][:, :, :], conv[b][:, :, :], ACT.Silu).then_inc(s["xbc"], 1)
                if b > 0:
                    act.wait_ge(s["ysum"], b)
                    act.wait_ge(s["ss_ps"], b)
                for i in range(XF // 2):
                    act.wait_ge(s["z_ps"], 2 * b + i + 1)
                    run(sz[b][:, 2 * i:2 * i + 2, :].rearrange("p f n -> p (f n)"), work("inz", b, i)[:, :], ACT.Silu)\
                        .then_inc(s["sz"], 1)

            def ssd_a(t, b):
                n = T * b + t
                act.wait_ge(s["diff_ps"], n + 1)
                if n > 0:
                    act.wait_ge(s["y_ps"], n)
                run(L[b][:, :, :].rearrange("p h n -> p (h n)"), pair(f"s{t}a", b)[:, :], ACT.Exp)\
                    .then_inc(s["L"], 1)

            def out_a(b):
                act.wait_ge(s["y_done"], 2 * (b + 1))
                run(ysq[b][:, :, :], yg[b][:, :, :], ACT.Square).then_inc(s["ysq"], 1)

            def out_b(b):
                act.wait_ge(s["ss_ps"], b + 1)
                run(rstd[b][:, 4, :], work("ob", b, 0)[:, 0:T], ACT.Ln, scale=1.0 / DI, bias=eps[:, 0:1])\
                    .then_inc(s["gate_ln"], 1)
                act.wait_ge(s["gate_ln"], b + 1)
                run(rstd[b][:, 5, :], rstd[b][:, 4, :], ACT.Exp, scale=-0.5).then_inc(s["gate_rs"], 1)

            def heads_p(kind, b):
                act.wait_ge(s[f"{kind}_ps"], b + 1)
                after_last_user(act, SHARED_AT["full_" + kind[1]], f"{kind}_p", b)
                run(full[kind][:, :], work(f"{kind}_p", b)[:, :], ACT.Square).then_inc(s[f"{kind}_sq"], 1)

            def heads_s(kind, b):
                act.wait_ge(s[f"{kind}_sum"], b + 1)
                if b > 0:
                    act.wait_ge(s[f"{kind}_full"], b)
                run(rs[kind][:, :], work(f"{kind}_s", b)[:, :], ACT.Ln, scale=1.0 / XD, bias=eps[:, 1:2])\
                    .then_inc(s[f"{kind}_ln"], 1)
                act.wait_ge(s[f"{kind}_ln"], b + 1)
                run(rs[kind][:, :], rs[kind][:, :], ACT.Exp, scale=-0.5).then_inc(s[f"{kind}_rs"], 1)

            def cross(b, n):
                for i in range(2):
                    q = 16 * b + 2 * n + i
                    act.wait_ge(s["xs_ps"], q + 1)
                    after_last_user(act, PROB_AT, f"x{n}", b, i)
                    run(probs(f"x{n}", b, i)[:, :, :].rearrange("p a n -> p (a n)"), pair(f"x{n}", b, i)[:, :], ACT.Exp,
                        scale=float(XD) ** -0.5).then_inc(s["xp"], 1)

            def proj_a(b):
                act.wait_ge(s["lat_ps"], b + 1)
                if b > 0:
                    act.wait_ge(s["fv_ps"], b)
                run(lat[b][:, :], work("pa", b, 0)[:, 0:SEQ], ACT.Copy).then_inc(s["lat"], 1)

            def proj_b(b):
                for i, kind in enumerate(("fk", "fq")):
                    act.wait_ge(s["plain_ps"], 2 * b + i + 1)
                    after_last_user(act, SHARED_AT["full_" + kind[1]], ("pa", "pb")[i], b)
                    run(full[kind][:, 0:SEQ], work("pb", b, i)[:, 0:SEQ], ACT.Copy).then_inc(s["plain"], 1)

            def causal(b, n):
                for i in range(2):
                    q = 8 * b + 2 * n + i
                    act.wait_ge(s["fs_ps"], q + 1)
                    after_last_user(act, PROB_AT, f"f{n}", b, i)
                    run(probs(f"f{n}", b, i)[:, :, 0:384],
                        pair(f"f{n}", b, i)[:, :].rearrange("p (a n) -> p a n", a=2)[:, :, 0:384], ACT.Exp,
                        scale=float(AD) ** -0.5).then_inc(s["fp"], 1)

            def router(b):
                act.wait_ge(s["logits"], b + 1)
                run(rt[b][:, 1, :, :], rt[b][:, 0, :, :], ACT.Exp, scale=-1.0).then_inc(s["router_exp"], 1)

            def expert(b, e):
                n = NE * b + e
                act.wait_ge(s["gu_ps"], n + 1)
                if n >= 2:
                    act.wait_ge(s["down_ps"], n - 1)
                run(sg[n % 2][:, :], work(f"e{e}", b, 0)[:, 0:SEQ], ACT.Silu).then_inc(s["sg"], 1)

            steps = {**{f"l{i + 1}a": lambda b, i=i: ln(i, b) for i in range(4)}, "l3m": rms3,
                     "dta": dt, "inx": inx, "cs": cs, "inz": inz,
                     "s0a": lambda b: ssd_a(0, b), "s1a": lambda b: ssd_a(1, b), "oa": out_a, "ob": out_b,
                     **{f"{kind}_p": lambda b, kind=kind: heads_p(kind, b) for kind in ("xk", "xq")},
                     **{f"{kind}_s": lambda b, kind=kind: heads_s(kind, b) for kind in ("xk", "xq")},
                     **{f"x{n}": lambda b, n=n: cross(b, n) for n in range(8)}, "pa": proj_a, "pb": proj_b,
                     **{f"f{n}": lambda b, n=n: causal(b, n) for n in range(4)},
                     "ra": router, **{f"e{n}": lambda b, n=n: expert(b, n) for n in range(NE)}}
            for step, b in SCHEDULE:
                if step in steps:
                    steps[step](b)

        @block.vector
        def _(dve):
            count = [0]
            vec = nc.vector

            def then(ins):
                count[0] += 1
                ins.then_inc(s["dve_chain"], 1)
                dve.wait_ge(s["dve_chain"], count[0])

            vec.memset(ones[:, :], 1.0)
            vec.memset(eps[:, 0:1], LN_EPS).then_inc(s["eps"], 1)
            vec.memset(eps[:, 1:2], X_EPS).then_inc(s["eps"], 1)
            vec.memset(eps[:, 2:3], 0.0).then_inc(s["eps"], 1)

            def ln(i, b, src, ready, value):
                dve.wait_ge(s[ready], value)
                for t in range(T):
                    then(vec.bn_stats(stats[b][:, i, t, :], src[:, t, :]))
                then(vec.bn_aggr(mv[b][:, i, 0, :], stats[b][:, i, 0, :]))
                last = vec.bn_aggr(mv[b][:, i, 1, :], stats[b][:, i, 1, :])
                if i < 3:
                    last.then_inc(s[f"mv{i}"], 1)
                    return
                then(last)
                m2 = sp[b][:, 7, 0:T]
                then(vec.tensor_tensor(m2, mv[b][:, 3, :, 0], mv[b][:, 3, :, 0], ALU.mult))
                vec.tensor_tensor(mv[b][:, 3, :, 1], mv[b][:, 3, :, 1], m2, ALU.add).then_inc(s["mv3"], 1)

            def ln_apply(i, b, src, xn_sem):
                after_last_user(dve, SHARED_AT[f"xn_{i % 2}"], f"l{i + 1}b", b)
                dve.wait_ge(s[f"rstd{i}"], b + 1)
                for t in range(T):
                    last = vec.tensor_scalar(xn[i % 2][:, t, :], src[:, t, :], mv[b][:, i, t, 0:1],
                                             rstd[b][:, i, t:t + 1], ALU.subtract, ALU.mult)
                last.then_inc(s[xn_sem], 1)

            def copy_T(step, b, ready, dst, done, free=None):
                dve.wait_ge(s[ready], b + 1)
                if free is not None and free[1]:
                    dve.wait_ge(s[free[0]], free[1])
                vec.tensor_copy(dst[:, :, :].rearrange("p k n -> p (k n)"), work(step, b)[:, :]).then_inc(s[done], 1)

            def l1c(b):
                free_xnT(b, 0)
                copy_T("l1b", b, "xnT_ps", xnT[b], "xnT")

            def free_xnT(b, use):
                if use == 0:
                    if b >= 2:
                        dve.wait_ge(s["kr_ps"], b - 1)
                elif use == 1:
                    dve.wait_ge(s["z_ps"], 2 * (b + 1))
                    dve.wait_ge(s["dt_ps"], b + 1)
                else:
                    dve.wait_ge(s["xq_ps"], b + 1)

            def dt(b):
                dve.wait_ge(s["dt_ps"], b + 1)
                if b == 0:
                    dve.wait_ge(s["w_first"], 32)
                S = sp[b]
                vec.tensor_tensor(S[:, 0, :].rearrange("p (t h) -> p t h", t=T),
                                  work("dta", b)[:, 0:T * NHM].rearrange("p (t h) -> p t h", t=T),
                                  dt_bias[:, :].unsqueeze(1).to_broadcast([P, T, NHM]), ALU.add)\
                    .then_inc(s["dt_raw"], 1)
                dve.wait_ge(s["dt_raw"], b + 1)
                vec.scalar_tensor_tensor(out=S[:, 1, :], in0=S[:, 0, :], scalar=-1.0, in1=S[:, 0, :], op0=ALU.mult,
                                         op1=ALU.max).then_inc(s["dt_abs"], 1)

            def dt_b(b):
                S = sp[b]
                dve.wait_ge(s["dt_exp"], b + 1)
                then(vec.tensor_scalar(S[:, 4, :], S[:, 2, :], 1.0, None, ALU.add))
                then(vec.tensor_scalar(S[:, 5, :], S[:, 4, :], -1.0, None, ALU.add))
                then(vec.tensor_tensor(S[:, 5, :], S[:, 2, :], S[:, 5, :], ALU.subtract))
                then(vec.reciprocal(S[:, 4, :], S[:, 4, :]))
                then(vec.tensor_tensor(S[:, 5, :], S[:, 5, :], S[:, 4, :], ALU.mult))
                then(vec.scalar_tensor_tensor(out=S[:, 6, :], in0=S[:, 0, :], scalar=0.0, in1=S[:, 3, :],
                                              op0=ALU.max, op1=ALU.add))
                then(vec.tensor_tensor(dt_t[b][:, :, :].rearrange("p t h -> p (t h)"), S[:, 6, :], S[:, 5, :], ALU.add))
                vec.tensor_tensor(dA[b][:, :, :], dt_t[b][:, :, :],
                                  a_row[:, :].unsqueeze(1).to_broadcast([P, T, NHM]), ALU.mult)\
                    .then_inc(s["dA"], 1)

            def inx(b):
                for i in range(CF // 2):
                    dve.wait_ge(s["conv_in"], 3 * b + i + 1)
                    for f in range(2):
                        c = 2 * i + f
                        for k in range(TAPS - 2, -1, -1):
                            back = TAPS - 1 - k
                            ins = vec.scalar_tensor_tensor(
                                out=conv[b][:, c, back:], in0=work("inx", b, i)[:, f * SEQ:(f + 1) * SEQ - back],
                                scalar=conv_w[:, c * TAPS + k:c * TAPS + k + 1], in1=conv[b][:, c, back:],
                                op0=ALU.mult, op1=ALU.add)
                            if k:
                                then(ins)
                            else:
                                ins.then_inc(s["taps"], 1)

            def ssd_a(t, b):
                n, step = T * b + t, f"s{t}a"
                dve.wait_ge(s["g_ps"], n + 1)
                if n > 0:
                    dve.wait_ge(s["y_ps"], n)
                if t == 0:
                    then(vec.tensor_copy(btok[b][:, :], work(step, b, 0)[:, P:2 * P]))
                vec.tensor_tensor(Gm[b][:, :], work(step, b, 0)[:, 0:P], upto, ALU.mult).then_inc(s["gm"], 1)
                dve.wait_ge(s["xtok_ps"], n + 1)
                vec.tensor_tensor(dtx[b][:, :].rearrange("p (h d) -> p h d", h=NHM),
                                  work(step, b, 1)[:, :].rearrange("p (h d) -> p h d", h=NHM),
                                  dt_t[b][:, t, :].unsqueeze(2).to_broadcast([P, NHM, HP]), ALU.mult)\
                    .then_inc(s["dtx"], 1)

            def ssd_b(t, b):
                n, step = T * b + t, f"s{t}b"
                if t == 0:
                    dve.wait_ge(s["dtx"], n + 1)
                    dve.wait_ge(s["ecs"], b + 1)
                    vec.tensor_tensor(dtxd[b][:, :].rearrange("p (h d) -> p h d", h=NHM),
                                      dtx[b][:, :].rearrange("p (h d) -> p h d", h=NHM),
                                      ecs[b][:, 0, 1, :].unsqueeze(2).to_broadcast([P, NHM, HP]), ALU.mult)\
                        .then_inc(s["dtxd"], 1)
                dve.wait_ge(s["L"], n + 1)
                dve.wait_ge(s["gm"], n + 1)
                vec.tensor_tensor(L[b][:, :, :], L[b][:, :, :], Gm[b][:, :].unsqueeze(1).to_broadcast([P, NHM, P]),
                                  ALU.mult).then_inc(s["M"], 1)
                if t == 0:
                    dve.wait_ge(s["state_ps"], b + 1)
                    if b > 0:
                        dve.wait_ge(s["yoff_ps"], b)
                    vec.tensor_copy(state[b][:, :], work(step, b)[:, :]).then_inc(s["state"], 1)
                else:
                    dve.wait_ge(s["yoff_ps"], b + 1)
                    vec.tensor_tensor(yoff[b][:, :].rearrange("p (h d) -> p h d", h=NHM),
                                      work(step, b)[:, :].rearrange("p (h d) -> p h d", h=NHM),
                                      ecs[b][:, 1, 0, :].unsqueeze(2).to_broadcast([P, NHM, HP]), ALU.mult)\
                        .then_inc(s["yoff"], 1)

            def ssd_c(t, b):
                n, step, tok = T * b + t, f"s{t}c", slice(t * P, (t + 1) * P)
                dve.wait_ge(s["y_ps"], n + 1)
                dve.wait_ge(s["xD"], b + 1)
                vec.tensor_tensor(yg[b][:, :, tok], work(step, b)[:, :].rearrange("p (f n) -> p f n", f=XF),
                                  xD[b][:, :, tok], ALU.add).then_inc(s["y"], 1)
                dve.wait_ge(s["y"], n + 1)
                dve.wait_ge(s["sz"], 2 * (b + 1))
                vec.tensor_tensor(yg[b][:, :, tok], yg[b][:, :, tok], sz[b][:, :, tok], ALU.mult)\
                    .then_inc(s["y_done"], 1)

            def out_proj(b):
                if b == 0:
                    for f in range(XF):
                        vec.tensor_scalar(w_out[:, f, :], w_out[:, f, :], norm_w[:, f:f + 1], None, ALU.mult)\
                           .then_inc(s["w_norm_out"], 1)
                dve.wait_ge(s["out_ps"], b + 1)
                dve.wait_ge(s["gate_rs"], b + 1)
                for t in range(T):
                    last = vec.scalar_tensor_tensor(out=x1[b][:, t, :], in0=work("ob", b, 1)[:, t * D:(t + 1) * D],
                                                    scalar=rstd[b][:, 5, t:t + 1], in1=x0[b][:, t, :], op0=ALU.mult,
                                                    op1=ALU.add)
                last.then_inc(s["x1"], 1)

            def ctx(b):
                if b > 0:
                    dve.wait_ge(s["xv_ps"], b)
                    dve.wait_ge(s["xk_ps"], b)
                copy_T("ctx", b, "ctxT_ps", ctxT[b], "ctxT")

            def split_hi(kind, b):
                after_last_user(dve, SHARED_AT["parts_" + kind[1]], f"{kind}_f", b)
                vec.tensor_copy(parts[kind][:, :, 0, :], full[kind][:, :].rearrange("p (f n) -> p f n", f=2))\
                    .then_inc(s[f"{kind}_rounded"], 1)

            def split_mid(kind, b):
                dve.wait_ge(s[f"{kind}_diffs"], 2 * b + 1)
                vec.tensor_copy(parts[kind][:, :, 1, :], full[kind][:, :].rearrange("p (f n) -> p f n", f=2))\
                    .then_inc(s[f"{kind}_rounded"], 1)

            def heads_f(kind, b):
                dve.wait_ge(s[f"{kind}_rs"], b + 1)
                vec.tensor_tensor(full[kind][:, :], work(f"{kind}_p", b)[:, :], rs[kind][:, :], ALU.mult)\
                    .then_inc(s[f"{kind}_full"], 1)
                dve.wait_ge(s[f"{kind}_full"], b + 1)
                split_hi(kind, b)

            def xv(b):
                dve.wait_ge(s["xv_ps"], b + 1)
                if b == 0:
                    dve.wait_ge(s["pool_init"], NST + 4)
                else:
                    dve.wait_ge(s["xo_quad"], 8 * b)
                ps = work("xv", b)
                for t in range(T):
                    for i in range(3):
                        quads = len(range(i, XH // 4, 3))
                        for m in range(quads):
                            n = i + 3 * m
                            last = vec.tensor_copy(
                                xvals[b][:, t, 4 * n:4 * n + 4, 9 * i:9 * i + XD],
                                ps[:, t * D + 32 * n:t * D + 32 * n + 32].rearrange("p (j d) -> p j d", j=4))
                last.then_inc(s["xv"], 1)

            def cross(b, n):
                if n in (3, 6, 8):
                    rnd = (3, 6, 8).index(n)
                    dve.wait_ge(s["xo_quad"], 8 * b + n)
                    if b + rnd > 0:
                        dve.wait_ge(s["xback_ps"], 3 * b + rnd)
                    vec.tensor_copy(xot[b][:, :], outs(f"x{3 * rnd + 1}", b)).then_inc(s["xot"], 1)

            def x_back(b, rnd):
                ni, step = min(3, 8 - 3 * rnd), f"xb{rnd}"
                dve.wait_ge(s["xback_ps"], 3 * b + rnd + 1)
                if b >= 2 and rnd == 0:
                    dve.wait_ge(s["base"], b - 1)
                for t in range(T):
                    v = work(step, b)[:, t * P:(t + 1) * P].rearrange("p (j c) -> p j c", j=4)[:, :, 0:9 * ni]\
                        .rearrange("p j (i d) -> p i j d", i=ni)
                    den = xden[b][:, t, 0:4 * ni].rearrange("p (i j) -> p i j", j=4)
                    then(vec.reciprocal(den, v[:, :, :, XD]))
                    o = x2[b][:, t, 96 * rnd:96 * rnd + 32 * ni]
                    last = vec.tensor_tensor(o.rearrange("p (i j d) -> p i j d", i=ni, j=4), v[:, :, :, 0:XD],
                                             den.unsqueeze(3).to_broadcast([P, ni, 4, XD]), ALU.mult)
                last.then_inc(s["xo"], 1)
                if rnd == 2:
                    dve.wait_ge(s["xo"], 3 * (b + 1))
                    vec.tensor_tensor(x2[b][:, :, :], x2[b][:, :, :], x1[b][:, :, :], ALU.add)\
                        .then_inc(s["x2"], 1)

            def l2c(b):
                free_xnT(b, 1)
                copy_T("l2b", b, "xnT2_ps", xnT[b], "xnT2")

            def l3m(b):
                dve.wait_ge(s["rstd2"], b + 1)
                r = rstd[b]
                then(vec.tensor_tensor(r[:, 4, :], r[:, 2, :], r[:, 2, :], ALU.mult))
                vec.tensor_tensor(r[:, 4, :], r[:, 4, :], mv[b][:, 2, :, 1], ALU.mult).then_inc(s["ms3"], 1)
                for t in range(T):
                    last = vec.tensor_scalar(y3[b][:, t, :], x2[b][:, t, :], mv[b][:, 2, t, 0:1], r[:, 2, t:t + 1],
                                             ALU.subtract, ALU.mult)
                then(last)

            def l3b(b):
                after_last_user(dve, SHARED_AT["xn_0"], "l3b", b)
                dve.wait_ge(s["rms3"], b + 1)
                for t in range(T):
                    last = vec.tensor_scalar(xn[0][:, t, :], y3[b][:, t, :], rstd[b][:, 5, t:t + 1], None, ALU.mult)
                last.then_inc(s["xn3"], 1)

            def l3c(b):
                dve.wait_ge(s["xnT3_ps"], b + 1)
                if b == 0:
                    dve.wait_ge(s["w_second"], 48)
                free_xnT(b, 2)
                for k in range(KD):
                    last = vec.tensor_scalar(xnT[b][:, k, :], work("l3b", b)[:, k * SEQ:(k + 1) * SEQ],
                                             ln1_w[:, k:k + 1], None, ALU.mult)
                last.then_inc(s["xnT3"], 1)

            def rope(kind, step, i, ps_ready, done, b):
                dve.wait_ge(s[ps_ready], b + 1)
                after_last_user(dve, SHARED_AT["full_" + kind[1]], step, b)
                vec.tensor_tensor(full[kind][:, SEQ:2 * SEQ], work(step, b, i)[:, 0:SEQ], rope_cs[:, 0:SEQ],
                                  ALU.mult)
                if b > 0:
                    dve.wait_ge(s[f"{kind}_full"], b)
                vec.tensor_tensor(rope_t[:, KIND[kind] - 2, :], work(step, b, i)[:, SEQ:2 * SEQ],
                                  rope_cs[:, SEQ:2 * SEQ], ALU.mult).then_inc(s[done], 1)

            def proj_a(b):
                rope("fk", "pa", 1, "kr_ps", "k_rope", b)

            def proj_b(b):
                rope("fq", "pb", 2, "qr_ps", "q_rope", b)
                dve.wait_ge(s["fv_ps"], b + 1)
                if b == 0:
                    dve.wait_ge(s["pool_init"], NST + 4)
                else:
                    dve.wait_ge(s["fo_ps"], 4 * b)
                vec.tensor_copy(fvals[b][:, :, :, 0:AD],
                                work("pb", b, 3)[:, :].rearrange("p (t h d) -> p t h d", t=T, h=AH))\
                    .then_inc(s["fv"], 1)

            def f_split(kind, b):
                dve.wait_ge(s[f"{kind}_full"], b + 1)
                dve.wait_ge(s["plain"], 2 * b + (1 if kind == "fk" else 2))
                split_hi(kind, b)

            def f_max(b, n):
                dve.wait_ge(s["fm_ps"], 6 * b + n + 1)
                ps = pair(f"max{n}", b)
                if n < 2:
                    src = ps[:, :].rearrange("p (h k) -> p h k", h=8)
                    dst = fmx[b][:, 0, 8 * n:8 * n + 8]
                else:
                    src = ps[:, :].rearrange("p (h k) -> p h k", h=4)
                    dst = fmx[b][:, 1, 4 * (n - 2):4 * (n - 2) + 4]
                vec.tensor_reduce(dst, src, AX.X, ALU.max, negate=True).then_inc(s["mx"], 1)

            def maxT_(b):
                dve.wait_ge(s["mx"], 6 * (b + 1))
                f, r = fmx[b][:, :, :], fmr[b][:, :].rearrange("p (t h) -> p t h", t=T)
                then(vec.tensor_copy(fmp[b][:, :, 0, :], f))
                then(vec.tensor_tensor(r, f, fmp[b][:, :, 0, :], ALU.subtract))
                then(vec.tensor_copy(fmp[b][:, :, 1, :], r))
                vec.tensor_tensor(fmp[b][:, :, 2, :], r, fmp[b][:, :, 1, :], ALU.subtract).then_inc(s["max_parts"], 1)

            def max_row(b):
                dve.wait_ge(s["maxT_ps"], b + 1)
                if b > 0:
                    dve.wait_ge(s["max_stack"], 48 * b)
                vec.tensor_copy(maxT[b][:, :], work("mtb", b)[:, 0:P].bitcast(BF16)[0:3 * AH, 0:SEQ])\
                    .then_inc(s["maxT"], 1)

            def causal(b, n):
                if n > 0:
                    dve.wait_ge(s["fo_ps"], 4 * b + n)
                    if b + n > 1:
                        dve.wait_ge(s["fback_ps"], 4 * b + n - 1)
                    vec.tensor_copy(fot[b][:, :], work(f"f{n}", b)[:, 0:SEQ]).then_inc(s["fot"], 1)

            def f_back(b, n):
                dve.wait_ge(s["fback_ps"], 4 * b + n + 1)
                if b > 0 and n == 0:
                    dve.wait_ge(s["aoT_ps"], b)
                v = work(f"f{n + 1}", b)[:, SEQ:SEQ + T * P].rearrange("p (t j c) -> p t j c", t=T, j=4)
                then(vec.reciprocal(fden[b][:, :, :], v[:, :, :, AD]))
                for t in range(T):
                    last = vec.tensor_tensor(ao[b][:, t, 64 * n:64 * n + 64].rearrange("p (j d) -> p j d", j=4),
                                             v[:, t, :, 0:AD], fden[b][:, t, :].unsqueeze(2).to_broadcast([P, 4, AD]),
                                             ALU.mult)
                last.then_inc(s["ao"], 1)

            def oproj_a(b):
                copy_T("opa", b, "aoT_ps", aoT[b], "aoT", ("o_ps", b))

            def oproj_b(b):
                dve.wait_ge(s["o_ps"], b + 1)
                vec.tensor_tensor(h4[b][:, :, :], work("opb", b)[:, :].rearrange("p (t n) -> p t n", t=T),
                                  y3[b][:, :, :], ALU.add).then_inc(s["h"], 1)

            def l4b(b):
                after_last_user(dve, SHARED_AT["xn_1"], "l4b", b)
                dve.wait_ge(s["rstd3"], b + 1)
                for t in range(T):
                    last = vec.tensor_scalar(xn[1][:, t, :], h4[b][:, t, :], rstd[b][:, 3, t:t + 1], None, ALU.mult)
                last.then_inc(s["xn4"], 1)

            def l4c(b):
                dve.wait_ge(s["hT_ps"], b + 1)
                if b > 0:
                    dve.wait_ge(s["router_ps"], b)
                    dve.wait_ge(s["gu_ps"], NE * b)
                for k in range(KD):
                    last = vec.tensor_scalar(hT[b][:, k, :], work("l4b", b)[:, k * SEQ:(k + 1) * SEQ],
                                             ln2_w[:, k:k + 1], None, ALU.mult)
                last.then_inc(s["hT"], 1)

            def router(b):
                r = rt[b]
                dve.wait_ge(s["router_ps"], b + 1)
                vec.tensor_tensor(r[:, 0, :, :], work("ra", b)[:, 0:T * NR].rearrange("p (t e) -> p t e", t=T),
                                  router_b[:, :].unsqueeze(1).to_broadcast([P, T, NR]), ALU.add)\
                    .then_inc(s["logits"], 1)

            def router_b_(b):
                r = rt[b]
                dve.wait_ge(s["router_exp"], b + 1)
                then(vec.tensor_scalar(r[:, 2, :, :], r[:, 1, :, :], 1.0, None, ALU.add))
                then(vec.reciprocal(r[:, 3, :, :], r[:, 2, :, :]))
                prob = r[:, 3, :, :]
                for t in range(T):
                    mine = prob[:, t, :].unsqueeze(2).to_broadcast([P, NR, NR])
                    other = prob[:, t, :].unsqueeze(1).to_broadcast([P, NR, NR])
                    c = [cmp_[b][:, i, t, :].rearrange("p (e j) -> p e j", e=NR) for i in range(2)]
                    then(vec.tensor_tensor(c[0], other, mine, ALU.is_gt))
                    then(vec.tensor_tensor(c[1], other, mine, ALU.is_equal))
                    then(vec.tensor_tensor(c[1], c[1], before, ALU.mult))
                    then(vec.tensor_tensor(c[0], c[0], c[1], ALU.add))
                    then(vec.tensor_reduce(r[:, 4, t, :], c[0], AX.X, ALU.add))
                then(vec.tensor_scalar(r[:, 5, :, :], r[:, 4, :, :], 1.5, None, ALU.is_lt))
                then(vec.tensor_tensor(r[:, 5, :, :], r[:, 5, :, :], prob, ALU.mult))
                then(vec.tensor_reduce(rsum[b][:, 0, :], r[:, 5, :, :], AX.X, ALU.add))
                then(vec.reciprocal(rsum[b][:, 1, :], rsum[b][:, 0, :]))
                then(vec.tensor_tensor(gates[b][:, :, :], r[:, 5, :, :],
                                       rsum[b][:, 1, :].unsqueeze(2).to_broadcast([P, T, NR]), ALU.mult))
                then(vec.tensor_scalar(gates[b][:, :, :], gates[b][:, :, :], 1.0 / 8, None, ALU.mult))

            def expert(b, e):
                n = NE * b + e
                dve.wait_ge(s["sg"], n + 1)
                if n >= 2:
                    dve.wait_ge(s["down_ps"], n - 1)
                vec.tensor_tensor(hid[n % 2][:, :], sg[n % 2][:, :], work(f"e{e}", b, 0)[:, SEQ:2 * SEQ], ALU.mult)\
                    .then_inc(s["hidden"], 1)
                if e > 0:
                    add_expert(b, e - 1)

            def add_expert(b, e):
                n = NE * b + e
                dve.wait_ge(s["down_ps"], n + 1)
                ps = work("store", b, 0) if e == NE - 1 else work(f"e{e + 1}", b, 1)
                if e == 0:
                    dve.wait_ge(s["base"], b + 1)
                    vec.scalar_tensor_tensor(out=acc[b][:, :, :], in0=ps[:, :].rearrange("p (t n) -> p t n", t=T),
                                             scalar=1.0 / 8, in1=acc[b][:, :, :], op0=ALU.mult, op1=ALU.add)\
                       .then_inc(s["acc"], 1)
                else:
                    dve.wait_ge(s["acc"], n)
                    for t in range(T):
                        last = vec.scalar_tensor_tensor(out=acc[b][:, t, :], in0=ps[:, t * D:(t + 1) * D],
                                                        scalar=gates[b][:, t, e - 1:e], in1=acc[b][:, t, :],
                                                        op0=ALU.mult, op1=ALU.add)
                    last.then_inc(s["acc"], 1)

            steps = {"l1a": lambda b: ln(0, b, x0[b], "x_in" if b else "x_in_first", 16 * max(b, NF - 1) if b else 16),
                     "l2a": lambda b: ln(1, b, x1[b], "x1", b + 1), "l3a": lambda b: ln(2, b, x2[b], "x2", b + 1),
                     "l4a": lambda b: ln(3, b, h4[b], "h", b + 1),
                     "l1b": lambda b: ln_apply(0, b, x0[b], "xn"), "l2b": lambda b: ln_apply(1, b, x1[b], "xn2"),
                     "l1c": l1c, "l2c": l2c, "l3m": l3m, "l3b": l3b, "l3c": l3c, "l4b": l4b, "l4c": l4c,
                     "dta": dt, "dtb": dt_b, "inx": inx,
                     **{f"s{t}{c}": (lambda b, f=f, t=t: f(t, b)) for t in range(T)
                        for c, f in (("a", ssd_a), ("b", ssd_b), ("c", ssd_c))}, "ob": out_proj,
                     "ctx": ctx, "xv": xv, "xk_f": lambda b: heads_f("xk", b), "xq_f": lambda b: heads_f("xq", b),
                     "fk_f": lambda b: f_split("fk", b), "fq_f": lambda b: f_split("fq", b),
                     **{f"{kind}_m": lambda b, kind=kind: split_mid(kind, b) for kind in KIND},
                     **{f"x{n}": lambda b, n=n: cross(b, n) for n in range(9)},
                     **{f"xb{n}": lambda b, n=n: x_back(b, n) for n in range(3)}, "pa": proj_a, "pb": proj_b,
                     **{f"max{n}": lambda b, n=n: f_max(b, n) for n in range(6)}, "mta": maxT_, "mtb": max_row,
                     **{f"f{n}": lambda b, n=n: causal(b, n) for n in range(5)},
                     **{f"fb{n}": lambda b, n=n: f_back(b, n) for n in range(4)},
                     "opa": oproj_a, "opb": oproj_b, "ra": router, "rb": router_b_,
                     **{f"e{n}": lambda b, n=n: expert(b, n) for n in range(NE)},
                     "store": lambda b: add_expert(b, NE - 1)}
            for step, b in SCHEDULE:
                if step in steps:
                    steps[step](b)

        @block.gpsimd
        def _(pool):
            gp = nc.gpsimd
            for i in range(NST):
                gp.memset(fstack["fk"][i][96:99, :, :], 1.0).then_inc(s["pool_init"], 1)
                pool.wait_ge(s["pool_init"], i + 1)
            gp.memset(xvals[0][:, :, :, :], 0.0).then_inc(s["pool_init"], 1)
            gp.memset(fvals[0][:, :, :, :], 0.0).then_inc(s["pool_init"], 1)
            pool.wait_ge(s["pool_init"], NST + 2)
            for n in range(XH // 4):
                i = n % 3
                last = gp.memset(xvals[0][:, :, 4 * n:4 * n + 4, 9 * i + XD:9 * i + XD + 1], 1.0)
            last.then_inc(s["pool_init"], 1)
            gp.memset(fvals[0][:, :, :, AD:AD + 1], 1.0).then_inc(s["pool_init"], 1)
            pool.wait_ge(s["w_second"], 48)

            def turned(dst, src):
                v = dst.rearrange("p (h a d) -> p h a d", a=2, d=AR // 2)
                u = src.rearrange("p (h a d) -> p h a d", a=2, d=AR // 2)
                gp.tensor_scalar(v[:, :, 0, :], u[:, :, 1, :], -1.0, None, ALU.mult)\
                    .then_inc(s["pool_init"], 1)
                return gp.tensor_copy(v[:, :, 1, :], u[:, :, 0, :])

            for k in range(KD):
                turned(w_rope_k2[:, k, :], w_rope_k[:, k, :]).then_inc(s["pool_init"], 1)
            pool.wait_ge(s["pool_init"], NST + 8)
            turned(w_rope_q2[LAT:2 * LAT, :], w_second[LAT:2 * LAT, 0:P]).then_inc(s["pool_init"], 1)
            pool.wait_ge(s["pool_init"], NST + 10)

            def skip(b):
                pool.wait_ge(s["xbc"], b + 1)
                if b > 0:
                    pool.wait_ge(s["out_ps"], b)
                    pool.wait_ge(s["ysq"], b)
                gp.tensor_tensor(xD[b][:, :, :], xbc[b][:, 0:XF, :],
                                 d_skip[:, :].unsqueeze(2).to_broadcast([P, XF, SEQ]), ALU.mult)\
                    .then_inc(s["xD"], 1)

            def decays(t, b):
                n = T * b + t
                pool.wait_ge(s["dA"], b + 1)
                if n > 0:
                    pool.wait_ge(s["diff_ps"], n)
                gp.tensor_tensor(R[b][:, :, :], upto.unsqueeze(1).to_broadcast([P, NHM, P]),
                                 dA[b][:, t, :].unsqueeze(2).to_broadcast([P, NHM, P]), ALU.mult)\
                    .then_inc(s["R"], 1)

            def out_proj(b):
                pool.wait_ge(s["ysq"], b + 1)
                gp.tensor_tensor(ysq[b][:, 0:2, :], ysq[b][:, 0:2, :], ysq[b][:, 2:4, :], ALU.add)\
                    .then_inc(s["ysum2"], 1)
                pool.wait_ge(s["ysum2"], b + 1)
                gp.tensor_tensor(ysq[b][:, 0, :], ysq[b][:, 0, :], ysq[b][:, 1, :], ALU.add).then_inc(s["ysum"], 1)

            def difference(kind, b, i):
                pool.wait_ge(s[f"{kind}_rounded"], 2 * b + i + 1)
                f3 = full[kind][:, :].rearrange("p (f n) -> p f n", f=2)
                gp.tensor_tensor(f3 if i == 0 else parts[kind][:, :, 2, :], f3, parts[kind][:, :, i, :],
                                 ALU.subtract).then_inc(s[f"{kind}_diffs"], 1)

            def rope(kind, done, b):
                pool.wait_ge(s[done], b + 1)
                gp.tensor_tensor(full[kind][:, SEQ:2 * SEQ], full[kind][:, SEQ:2 * SEQ],
                                 rope_t[:, KIND[kind] - 2, :], ALU.add).then_inc(s[f"{kind}_full"], 1)

            def router(b):
                pool.wait_ge(s["h"], b + 1)
                gp.tensor_tensor(acc[b][:, :, :], x2[b][:, :, :], h4[b][:, :, :], ALU.add).then_inc(s["base"], 1)

            steps = {"cs": lambda b: decays(0, b), "s0a": skip, "s0b": lambda b: decays(1, b), "oa": out_proj,
                     "pa": lambda b: rope("fk", "k_rope", b), "pb": lambda b: rope("fq", "q_rope", b),
                     **{f"{kind}_f": lambda b, kind=kind: difference(kind, b, 0) for kind in KIND},
                     **{f"{kind}_m": lambda b, kind=kind: difference(kind, b, 1) for kind in KIND}, "ra": router}
            for step, b in SCHEDULE:
                if step in steps:
                    steps[step](b)


def _rows(a, k):
    a = np.asarray(a)
    return a.reshape(k, P, -1).transpose(1, 0, 2).reshape(P, -1)


def _spread(row):
    return np.broadcast_to(np.asarray(row), (P, np.asarray(row).shape[0]))


def _shape_tables():
    i = np.arange(P)
    ident = np.eye(P, dtype=np.float32)
    upto = (i[:, None] <= i[None, :]).astype(np.float32)
    after = (i[:, None] > i[None, :]).astype(np.float32)
    block8 = (i[:, None] // XD == i[None, :] // XD).astype(np.float32)
    inv = (1.0 / 10000.0 ** (np.arange(0, AR, 2, dtype=np.float32) / AR)).astype(np.float32)
    ang = np.outer(np.arange(SEQ, dtype=np.float32), inv).astype(np.float32)
    ang = ang[:, i % (AR // 2)].T
    rope = np.concatenate([np.cos(ang), np.sin(ang)], axis=1).astype(np.float32)
    e = np.arange(NR)
    before = (e[None, :] < e[:, None]).astype(np.float32).reshape(-1)
    shape = np.concatenate([ident, upto, after, block8, rope, _spread(before)], axis=1)
    later = np.where(i[None, :] > i[:, None], np.float32(NEG), np.float32(0))
    masks = np.stack([ident, later, later.T], axis=1)
    return shape, masks


def kernel(**inputs):
    import ml_dtypes
    import concourse.bacc as _bacc
    from concourse.bass_utils import run_bass_kernel_spmd as _run

    g = {k: np.asarray(v) for k, v in inputs.items()}
    m, c, f = ({k[len(pre):]: v for k, v in g.items() if k.startswith(pre)} for pre in ("L0_attn_", "L0_xattn_", "L0_ffn_"))
    kv = np.concatenate([c["Wk"], c["Wv"]], axis=0).reshape(XH * XD, 2, D)
    shape, masks = _shape_tables()
    arrays = {
        "mix": [_rows(m["W_in"], KD), _rows(m["conv_w"], CF), _rows(m["conv_b"], CF), _rows(m["norm_w"], XF),
                _spread(m["A"]), _spread(m["dt_bias"]), _rows(np.repeat(m["D"], HP), XF), _rows(m["W_out"], XF)],
        "cross": [_rows(c["Wq"].T, KD), _rows(kv[:, 0].T, KD), _rows(kv[:, 1].T, KD)],
        "latent": [_rows(f["ln1_w"], KD), _rows(f["ln2_w"], KD),
                   _rows(np.concatenate([f["kv_d_w"], f["q_d_w"]], axis=1), KD), _rows(f["rope_k_w"], KD),
                   np.concatenate([f["k_u_w"], f["q_u_w"]], axis=0),
                   np.concatenate([f["v_u_w"], np.concatenate([f["rope_q_w"], f["rope_q_w"]], axis=1)], axis=0),
                   _rows(f["o_w"], KD), _rows(f["router_w"], KD), _spread(f["router_b"])],
        "experts": [], "shape": [shape],
    }
    gate = np.concatenate([f["sh_gate"][None], f["r_gate"]], axis=0)
    up = np.concatenate([f["sh_up"][None], f["r_up"]], axis=0)
    down = np.concatenate([f["sh_down"][None], f["r_down"]], axis=0)
    gu = np.stack([gate, up], axis=2).reshape(NE, KD, P, 2, FI).transpose(2, 0, 1, 3, 4).reshape(P, -1)
    arrays["experts"] = [gu, down.transpose(1, 0, 2).reshape(P, -1)]

    nc = _bacc.Bacc("TRN2", target_bir_lowering=False, num_devices=1)
    data, packs = {}, {}
    for name, parts in arrays.items():
        data["pack_" + name] = np.ascontiguousarray(np.concatenate(parts, axis=1))
        packs[name] = nc.dram_tensor("pack_" + name, [P, WIDTH[name]], F32, kind="ExternalInput").ap()
    data["masks16"] = masks.astype(ml_dtypes.bfloat16)
    masks16 = nc.dram_tensor("masks16", [P, 3, P], BF16, kind="ExternalInput").ap()
    for name in ("x", "ctx_2048"):
        data[name + "_in"] = np.ascontiguousarray(g[name])
    x_ap = nc.dram_tensor("x_in", [NB, SEQ, D], F32, kind="ExternalInput").ap()
    c_ap = nc.dram_tensor("ctx_2048_in", [NB, SEQ, D], F32, kind="ExternalInput").ap()
    out = nc.dram_tensor("out_0", [NB, SEQ, D], F32, kind="ExternalOutput").ap()
    decoder_layer(nc, x_ap, c_ap, packs, masks16, out)
    r = _run(nc, [data], core_ids=[0])
    return r.results[0]["out_0"]
```

```python
from contextlib import ExitStack

import numpy as np

import concourse.bass as bass
from concourse import mybir

F32 = mybir.dt.float32
BF16 = mybir.dt.bfloat16
ALU = mybir.AluOpType
ACT = mybir.ActivationFunctionType
AX = mybir.AxisListType

P = 128
NB, SEQ, D = 4, 256, 256
T = SEQ // P
KD = D // P
DI, NHM, HP, NS = 512, 8, 64, 128
XF = DI // P
CF = XF + 2
TAPS = 4
WIN = 2 * DI + 2 * NS + NHM
XH, XD = 32, 8
AH, AR, AD = 16, 8, 16
LAT, NE, NR, FI = 64, 8, 7, 128
EPS, X_EPS = 1e-5, 1e-6
NEG = -1e30

PACKS = {
    "mixer": [("conv_w", CF * TAPS), ("conv_b", CF), ("norm_w", XF), ("a", NHM), ("dt_bias", NHM), ("d_skip", XF)],
    "w_in": [("w_in", KD * WIN)],
    "w_out": [("w_out", XF * D)],
    "cross": [("wq", KD * D), ("wk", KD * D), ("wv", KD * D)],
    "latent": [("ln1", KD), ("ln2", KD), ("down", KD * P), ("rope_k", KD * P), ("up", P), ("second", D),
               ("o_w", KD * D), ("router", KD * NR), ("router_b", NR)],
    "experts": [("gate_up", NE * KD * 2 * FI), ("down_w", NE * D)],
    "shape": [("ident", P), ("upto", P), ("after", P), ("alike", P), ("rope", 2 * SEQ), ("before", NR * NR)],
}
WIDTH = {pack: sum(n for _, n in parts) for pack, parts in PACKS.items()}

CONTEXT_STEPS = (
    "ctx", "xk_p", "xk_s", "xk_f", "xk_m", "xv",
)
STEPS = (
    "l1a", "l1b", "l1c", "dta", "inx0", "inx1", "inx2", "dtb", "cs", "xbc", "z0", "z1", "z2", "s0a", "s0b", "s0c",
    "s1a", "s1b", "s1c", "oa", "ob", "l2a", "l2b", "l2c", "xq_p", "xq_s", "xq_f", "xq_m", "x0", "x1", "x2", "x3",
    "xb0", "x4", "x5", "x6", "xb1", "x7", "x8", "xb2", "l3a", "l3m", "l3b", "l3c", "pa", "pb", "fk_f", "fq_f",
    "fk_m", "fq_m", "max0", "max1", "max2", "max3", "max4", "max5", "mta", "mtb", "f0", "f1", "fb0", "f2", "fb1",
    "f3", "fb2", "f4", "fb3", "opa", "opb", "l4a", "l4b", "l4c", "ra", "rb", "e0", "e1", "e2", "e3", "e4", "e5",
    "e6", "e7", "e8", "store",
)
ORDER = (
    "0000a0000aaa1a0b00a00b00020000110000b111000110bb11111100211001010000100100b01c01010021000022222c1cc1"
    "11002000200220c2220000000000200202012200012001112012012210212201c1101d2020221d131222222d2d2d21211311"
    "31d3223323311131131313133313111111311111212312221131311332212233121223233132122222132212322323332233"
    "233223223333323333332222233333333333323333333333333333333333"
)
assert NB == 4


def schedule():
    left = {**{str(b): iter(STEPS) for b in range(NB)}, **{"abcd"[b]: iter(CONTEXT_STEPS) for b in range(NB)}}
    return [(next(left[c]), "0a1b2c3d".index(c) // 2) for c in ORDER]


SCHEDULE = schedule()

WORK = {
    "l1b": [("xnT", 1, 0, "l1c")], "dta": [("dt_raw", 1, 0, "dta")],
    **{f"inx{i}": [("taps", 6, 2 * i + 1, f"inx{i}")] for i in range(3)},
    "cs": [("ecs", 1, 0, "cs")], **{f"z{i}": [("sz", 2, i, f"z{i + 1}")] for i in range(2)},
    "s0a": [("gm", 2, 0, "s0a"), ("dtx", 2, 0, "s0a")], "s0b": [("state", 1, 0, "s0b")], "s0c": [("y", 2, 0, "s0c")],
    "s1a": [("gm", 2, 1, "s1a"), ("dtx", 2, 1, "s1a")], "s1b": [("yoff", 1, 0, "s1b")], "s1c": [("y", 2, 1, "s1c")],
    "ob": [("gate_ln", 1, 0, "ob"), ("x1", 1, 0, "ob")],
    "ctx": [("ctxT", 1, 0, "ctx")], "xk_p": [("xk_full", 1, 0, "xk_f")], "xk_s": [("xk_ln", 1, 0, "xk_s")],
    "xv": [("xv", 1, 0, "xv")],
    "l2b": [("xnT2", 1, 0, "l2c")], "xq_p": [("xq_full", 1, 0, "xq_f")], "xq_s": [("xq_ln", 1, 0, "xq_s")],
    **{f"xb{n}": [("xo", 3, n, f"xb{n}")] for n in range(3)},
    "l3b": [("xnT3", 1, 0, "l3c")],
    "pa": [("lat", 1, 0, "pa"), ("k_rope", 1, 0, "pa")],
    "pb": [("plain", 2, 0, "pb"), ("plain", 2, 1, "pb"), ("q_rope", 1, 0, "pb"), ("fv", 1, 0, "pb")],
    "mtb": [("maxT", 1, 0, "mtb")],
    **{f"f{n + 1}": [("ao", 4, n, f"fb{n}")] for n in range(4)},
    "opa": [("aoT", 1, 0, "opa")], "opb": [("h", 1, 0, "opb")],
    "l4b": [("hT", 1, 0, "l4c")], "ra": [("logits", 1, 0, "ra")],
    **{f"e{n}": [("hidden", NE, n, f"e{n + 1}")] * (n < NE) + [("acc", NE, n - 2, f"e{n}")] * (n > 1)
       for n in range(NE + 1)},
    "store": [("acc", NE, NE - 1, "store")],
}
PAIR = {
    "s0a": [("L", 2, 0, "s0a")], "s1a": [("L", 2, 1, "s1a")],
    **{f"x{n}": [("xp", 16, 2 * n + i, f"x{n}") for i in range(2)] for n in range(8)},
    **{f"max{n}": [("mx", 6, n, f"max{n}")] for n in range(6)},
    **{f"f{n}": [("fp", 8, 2 * n + i, f"f{n}") for i in range(2)] for n in range(4)},
}
OUTS = {"x1": [("xot", 3, 0, "x3")], "x4": [("xot", 3, 1, "x6")], "x7": [("xot", 3, 2, "x8")]}
PROBS = {
    **{f"x{n}": [("xo_quad", 8, n, f"x{n + 1}")] * 2 for n in range(8)},
    **{f"f{n}": [("fo_ps", 4, n, f"f{n + 1}")] * 2 for n in range(4)},
}
PX = 4
SHARED = {
    "xn_0": {"l1b": [("xnT_ps", 1, 0, "l1b")], "l3b": [("xnT3_ps", 1, 0, "l3b")]},
    "xn_1": {"l2b": [("xnT2_ps", 1, 0, "l2b")], "l4b": [("hT_ps", 1, 0, "l4b")]},
    "full_k": {"xk_p": [("xk_diffs", 2, 1, "xk_m")], "pa": [("fk_diffs", 2, 1, "fk_m")]},
    "full_q": {"xq_p": [("xq_diffs", 2, 1, "xq_m")], "pb": [("fq_diffs", 2, 1, "fq_m")]},
    "parts_k": {"xk_f": [("xk_to_dram", 48, 47, "xk_m")], "fk_f": [("fk_to_dram", 48, 47, "fk_m")]},
    "parts_q": {"xq_f": [("xq_to_dram", 48, 47, "xq_m")], "fq_f": [("fq_to_dram", 48, 47, "fq_m")]},
}


POSITION = {sb: n for n, sb in enumerate(SCHEDULE)}


def plan(claims, slots):
    given, last = {}, [(-1, None, None, i - slots) for i in range(slots)]
    for n, (step, b) in enumerate(SCHEDULE):
        for i, (name, per, k, until) in enumerate(claims.get(step, [])):
            slot = min(range(slots), key=lambda j: (last[j][0], last[j][3]))
            assert last[slot][0] <= n and (last[slot][0] < n or last[slot][2] == step), ("no slot", step, b)
            given[step, b, i] = (slot, [last[slot][1]])
            last[slot] = (POSITION[until, b], (name, b * per + k + 1), step, len(given))
    return given


BANKS = 7
KEEP_PAIR = 6


def plan_banks():
    single, pairs = {}, {}
    last = [(-1, None, None, i - BANKS) for i in range(BANKS)]
    for n, (step, b) in enumerate(SCHEDULE):
        def free(j):
            return last[j][0] < n

        for i, (name, per, k, until) in enumerate(PAIR.get(step, [])):
            fit = [j for j in range(0, BANKS - 1, 2) if free(j) and free(j + 1)]
            assert fit, ("no pair", step, b)
            at = min(fit, key=lambda j: (max(last[j][0], last[j + 1][0]), max(last[j][3], last[j + 1][3])))
            pairs[step, b, i] = (at, [last[at][1], last[at + 1][1]])
            for j in (at, at + 1):
                last[j] = (POSITION[until, b], (name, b * per + k + 1), step, len(single) + len(pairs))
        for i, (name, per, k, until) in enumerate(WORK.get(step, [])):
            fit = [j for j in range(BANKS) if free(j)]
            assert fit, ("no bank", step, b)
            at = min(fit, key=lambda j: (last[j][0] + KEEP_PAIR * (j < BANKS - 1 and free(j ^ 1)), last[j][3]))
            single[step, b, i] = (at, [last[at][1]])
            last[at] = (POSITION[until, b], (name, b * per + k + 1), step, len(single) + len(pairs))
    return single, pairs


SHARED_AT = {name: plan(claims, 1) for name, claims in SHARED.items()}
(WORK_AT, PAIR_AT), OUT_AT, PROB_AT = plan_banks(), plan(OUTS, 2), plan(PROBS, PX)


def decoder_layer(nc, x, ctx_in, packs, masks16, out):
    stack = ExitStack()
    with stack:
        def sb(name, shape, dt=F32):
            return stack.enter_context(nc.sbuf_tensor(name, shape, dt))

        class Semaphores(dict):
            def __missing__(self, name):
                self[name] = stack.enter_context(nc.semaphore("s_" + name))
                return self[name]

        s = Semaphores()
        dram = [[nc.dram_tensor(f"scratch_{kind}_{b}", [2, 3, P, SEQ] if kind[0] == "x" else [3, 2, P, SEQ], BF16,
                                kind="Internal").ap()
                 for kind in ("xk", "xq", "fk", "fq")] for b in range(NB)]
        KIND = {"xk": 0, "xq": 1, "fk": 2, "fq": 3}

        def after_last_user(engine, table, step, b, i=0):
            for user in table[step, b, i][1]:
                if user is not None:
                    engine.wait_ge(s[user[0]], user[1])

        pair_ps = [stack.enter_context(nc.psum_tensor(f"pair{i}", [P, 1024], F32)) for i in range(BANKS // 2)]
        last_ps = stack.enter_context(nc.psum_tensor("last_bank", [P, 512], F32))
        outs_ps = stack.enter_context(nc.psum_tensor("outs", [P, 512], F32))

        def work(step, b, i=0):
            k = WORK_AT[step, b, i][0]
            return last_ps[:, :] if k == BANKS - 1 else pair_ps[k // 2][:, 512 * (k % 2):512 * (k % 2) + 512]

        def down_at(b, e):
            return ("store", b, 0) if e == NE - 1 else (f"e{e + 2}", b, 1 if e + 2 < NE else 0)

        def pair(step, b, i=0):
            return pair_ps[PAIR_AT[step, b, i][0] // 2]

        def outs(step, b):
            k = OUT_AT[step, b, 0][0]
            return outs_ps[:, k * 256:(k + 1) * 256]

        w = {name: sb("w_" + name, [P, n]) for name, n in WIDTH.items()}

        def part(pack, name):
            at = 0
            for n, width in PACKS[pack]:
                if n == name:
                    return w[pack][:, at:at + width]
                at += width
            raise KeyError(name)

        w_in = part("w_in", "w_in").rearrange("p (k n) -> p k n", k=KD)
        conv_w, conv_b, d_skip = part("mixer", "conv_w"), part("mixer", "conv_b"), part("mixer", "d_skip")
        norm_w, a_row, dt_bias = part("mixer", "norm_w"), part("mixer", "a"), part("mixer", "dt_bias")
        w_out = part("w_out", "w_out").rearrange("p (f n) -> p f n", f=XF)
        wq, wk, wv = (part("cross", n).rearrange("p (k n) -> p k n", k=KD) for n in ("wq", "wk", "wv"))
        ln1_w, ln2_w = part("latent", "ln1"), part("latent", "ln2")
        w_down = part("latent", "down").rearrange("p (k n) -> p k n", k=KD)
        w_rope_k = part("latent", "rope_k").rearrange("p (k n) -> p k n", k=KD)
        w_up, w_second = part("latent", "up"), part("latent", "second")
        w_o = part("latent", "o_w").rearrange("p (k n) -> p k n", k=KD)
        w_router = part("latent", "router").rearrange("p (k n) -> p k n", k=KD)
        router_b = part("latent", "router_b")
        gate_up = part("experts", "gate_up").rearrange("p (e k g n) -> p e k g n", e=NE, k=KD, g=2)
        down_w = part("experts", "down_w").rearrange("p (e n) -> p e n", e=NE)
        ident, upto, after, alike = (part("shape", n) for n in ("ident", "upto", "after", "alike"))
        rope_cs = part("shape", "rope")
        before = part("shape", "before").rearrange("p (e j) -> p e j", e=NR)
        m16 = sb("m16", [P, 3, P], BF16)
        ident16, mask_q, mask_k = m16[:, 0, :], m16[:, 1, :], m16[:, 2, :]
        ones = sb("ones", [P, 1])
        eps = sb("eps", [P, 2])
        w_rope_k2 = sb("w_rope_k2", [P, KD, P])
        w_rope_q2 = sb("w_rope_q2", [P, P])

        def per_batch(name, shape, dt=F32, n=NB):
            tiles = [sb(f"{name}_{i}", shape, dt) for i in range(n)]
            return [tiles[b % n] for b in range(NB)]

        NF = 3
        x0 = per_batch("x0", [P, T, D])
        ctx_t = per_batch("ctx", [P, T, D], n=1)
        stats = per_batch("stats", [P, 4, T, 6], n=2)
        mv = per_batch("mv", [P, 4, T, 2])
        rstd = per_batch("rstd", [P, 6, T])
        xn = [sb(f"xn{i}", [P, T, D]) for i in range(2)]
        xnT = per_batch("xnT", [P, KD, SEQ], n=2)
        conv = per_batch("conv", [P, CF, SEQ], n=1)
        xbc = conv
        sz = per_batch("sz", [P, XF, SEQ], n=1)
        sp = per_batch("sp", [P, 8, T * NHM], n=2)
        dt_t = per_batch("dt", [P, T, NHM])
        dA = per_batch("dA", [P, T, NHM])
        ecs = per_batch("ecs", [P, T, 2, NHM], n=2)
        R = per_batch("R", [P, NHM, P], n=1)
        L = per_batch("L", [P, NHM, P], n=1)
        Gm = per_batch("Gm", [P, P], n=1)
        btok = per_batch("btok", [P, P], n=1)
        dtx = per_batch("dtx", [P, DI], n=1)
        dtxd = per_batch("dtxd", [P, DI], n=1)
        state = dtxd
        yoff = dtxd
        yg = per_batch("yg", [P, XF, SEQ], n=1)
        xD = yg
        ysq = sz
        x1 = per_batch("x1", [P, T, D], n=NF)
        ctxT = per_batch("ctxT", [P, KD, SEQ], n=1)
        rs = {k: sb("rs_" + k, [P, 512]) for k in ("xk", "xq")}
        full = {k: sb("full_" + k, [P, 512]) for k in ("xk", "xq")}
        full["fk"], full["fq"] = full["xk"], full["xq"]
        parts = {k: sb("parts_" + k, [P, 3, 2, SEQ], BF16) for k in ("xk", "xq")}
        parts["fk"], parts["fq"] = parts["xk"], parts["xq"]
        NST = 1
        xstack = {k: per_batch("stack_" + k, [P, XH // 2, SEQ], BF16, n=NST) for k in ("xk", "xq")}
        fstack = {k: per_batch("stack_" + k, [P, AH, SEQ], BF16, n=NST) for k in ("fk", "fq")}
        xvals = per_batch("xvals", [P, T, XH, 32], n=1)
        fvals = per_batch("fvals", [P, T, AH, 32], n=1)
        probs_sb = [sb(f"probs{i}", [P, 2, 512]) for i in range(PX)]

        def probs(step, b, i):
            return probs_sb[PROB_AT[step, b, i][0]]

        xot = per_batch("xot", [P, SEQ], n=1)
        xden = per_batch("xden", [P, T, 12], n=1)
        x2 = per_batch("x2", [P, T, D], n=2)
        y3 = x1
        lat = per_batch("lat", [P, SEQ], n=1)
        rope_t = sb("rope_t", [P, 2, SEQ])
        fmx = per_batch("fmx", [P, T, AH])
        fmr = per_batch("fmr", [P, T * AH], n=2)
        fmp = per_batch("fmp", [P, T, 3, AH], BF16, n=2)
        maxT = per_batch("maxT", [3 * AH, SEQ], BF16, n=1)
        fot = per_batch("fot", [P, SEQ], n=1)
        fden = per_batch("fden", [P, T, 4], n=1)
        ao = per_batch("ao", [P, T, D], n=1)
        aoT = per_batch("aoT", [P, KD, SEQ], n=1)
        h4 = x1
        hT = per_batch("hT", [P, KD, SEQ], n=1)
        rt = per_batch("rt", [P, 6, T, NR], n=2)
        cmp_ = per_batch("cmp", [P, 2, T, NR * NR], n=1)
        rsum = per_batch("rsum", [P, 2, T])
        gates = per_batch("gates", [P, T, NR])
        NG = 3
        sg = [sb(f"sg{i}", [P, SEQ]) for i in range(NG)]
        hid = sg
        acc = x0

        block = stack.enter_context(nc.Block())

        @block.sync
        def _(sync):
            x_d = x.rearrange("b (t p) d -> b p t d", p=P)
            c_d = ctx_in.rearrange("b (t p) d -> b p t d", p=P)
            out_d = out.rearrange("b (t p) d -> b p t d", p=P)
            sync.dma_start(x0[0][:], x_d[0]).then_inc(s["x_in_first"], 16)
            sync.dma_start(w["shape"][:], packs["shape"]).then_inc(s["w_tables"], 16)
            sync.dma_start(w["mixer"][:], packs["mixer"]).then_inc(s["w_xbc"], 16)
            w_in_d = packs["w_in"].rearrange("p (k n) -> p k n", k=KD)
            sync.dma_start(w_in[:, :, DI:WIN], w_in_d[:, :, DI:WIN]).then_inc(s["w_xbc"], 16)
            sync.dma_start(w_in[:, :, 0:DI], w_in_d[:, :, 0:DI]).then_inc(s["w_z"], 16)
            sync.dma_start(ctx_t[0][:], c_d[0]).then_inc(s["ctx_in"], 16)
            sync.dma_start(w["cross"][:], packs["cross"]).then_inc(s["w_cross"], 16)
            sync.dma_start(w["w_out"][:], packs["w_out"]).then_inc(s["w_out"], 16)
            for b in range(1, NB):
                sync.dma_start(x0[b][:], x_d[b]).then_inc(s["x_in"], 16)
            sync.dma_start(m16[:], masks16).then_inc(s["w_latent"], 16)
            sync.dma_start(w["latent"][:], packs["latent"]).then_inc(s["w_latent"], 16)
            sync.dma_start(w["experts"][:], packs["experts"]).then_inc(s["w_experts"], 16)

            def ctx(b):
                if b + 1 < NB:
                    sync.wait_ge(s["ctxT"], b + 1)
                    sync.dma_start(ctx_t[b + 1][:], c_d[b + 1]).then_inc(s["ctx_in"], 16)

            def split(kind, b, stack_tile, used):
                d = dram[b][KIND[kind]]
                for g in range(3):
                    if g < 2:
                        sync.wait_ge(s[f"{kind}_rounded"], 2 * b + g + 1)
                    else:
                        sync.wait_ge(s[f"{kind}_diffs"], 2 * b + 2)
                    at = g if kind[1] == "k" else 2 - g
                    sync.dma_start((d[:, at] if kind[0] == "x" else d[at]).rearrange("a p t -> p a t"),
                                   parts[kind][:, g, :, :]).then_inc(s[f"{kind}_to_dram"], 16)
                sync.wait_ge(s[f"{kind}_to_dram"], 16 * 3 * (b + 1))
                if b >= NST:
                    sync.wait_ge(s[used[0]], used[1] * (b - NST + 1))
                elif kind == "fk":
                    sync.wait_ge(s["pool_init"], NST)
                for n, base in ((3, 0), (2, 3), (1, 5)):
                    g = slice(0, n) if kind[1] == "k" else slice(3 - n, 3)
                    if kind[0] == "x":
                        for a in range(2):
                            sync.dma_start(stack_tile[64 * a + XD * base:64 * a + XD * (base + n), :, :],
                                           d[a, g].rearrange("g (d q) t -> (g d) q t", d=XD))\
                                .then_inc(s[f"{kind}_stack"], 16)
                    else:
                        sync.dma_start(stack_tile[AD * base:AD * (base + n), :, :],
                                       d[g].rearrange("g a (d q) t -> (g a d) q t", d=AR))\
                            .then_inc(s[f"{kind}_stack"], 16)

            def maxes(b):
                sync.wait_ge(s["maxT"], b + 1)
                for c in range(3):
                    sync.dma_start(fstack["fq"][b][96 + c:97 + c, :, :], maxT[b][AH * c:AH * c + AH, :])\
                        .then_inc(s["max_stack"], 16)

            def store(b):
                sync.wait_ge(s["acc"], NE * (b + 1))
                sync.dma_start(out_d[b], acc[b][:]).then_inc(s["stored"], 16)

            steps = {"ctx": ctx, "xk_m": lambda b: split("xk", b, xstack["xk"][b], ("xs_ps", 16)),
                     "xq_m": lambda b: split("xq", b, xstack["xq"][b], ("xs_ps", 16)),
                     "fk_m": lambda b: split("fk", b, fstack["fk"][b], ("fs_ps", 8)),
                     "fq_m": lambda b: split("fq", b, fstack["fq"][b], ("fs_ps", 8)),
                     "mtb": maxes, "store": store}
            for step, b in SCHEDULE:
                if step in steps:
                    steps[step](b)
            sync.wait_ge(s["stored"], 16 * NB)

        RUNS = {"xk": 6, "xq": 6, "fk": 3, "fq": 3}

        @block.tensor
        def _(pe):
            mm = nc.tensor.matmul

            def claim(table, step, b, i=0):
                after_last_user(pe, table, step, b, i)

            def transposes(step, b, ready, src, done):
                if ready == "xn" and b == 0:
                    pe.wait_ge(s["w_tables"], 16)
                pe.wait_ge(s[ready], b + 1)
                claim(WORK_AT, step, b)
                ps = work(step, b)
                for k in range(KD):
                    for t in range(T):
                        last = nc.tensor.transpose(ps[:, k * SEQ + t * P:k * SEQ + (t + 1) * P],
                                                   src[:, t, k * P:(k + 1) * P], ident)
                last.then_inc(s[done], 1)

            def ln1(b):
                transposes("l1b", b, "xn", xn[0], "xnT_ps")

            def dt(b):
                if b == 0:
                    pe.wait_ge(s["w_xbc"], 32)
                pe.wait_ge(s["xnT"], b + 1)
                claim(WORK_AT, "dta", b)
                for t in range(T):
                    for k in range(KD):
                        last = mm(work("dta", b)[:, t * NHM:(t + 1) * NHM], xnT[b][:, k, t * P:(t + 1) * P],
                                  w_in[:, k, WIN - NHM:WIN], start=k == 0, stop=k == KD - 1)
                last.then_inc(s["dt_ps"], 1)

            def project(step, b, i, first, done):
                claim(WORK_AT, step, b, i)
                for f in range(2):
                    for k in range(KD):
                        last = mm(work(step, b, i)[:, f * SEQ:(f + 1) * SEQ],
                                  w_in[:, k, first + f * P:first + (f + 1) * P], xnT[b][:, k, :],
                                  start=k == 0, stop=k == KD - 1)
                last.then_inc(s[done], 1)

            def inx(b, i):
                project(f"inx{i}", b, 0, DI + 2 * i * P, "xbc_ps")

            def gate_in(b, i):
                if b == 0:
                    pe.wait_ge(s["w_z"], 16)
                project(f"z{i}", b, 0, 2 * i * P, "z_ps")

            def cs(b):
                pe.wait_ge(s["dA"], b + 1)
                claim(WORK_AT, "cs", b)
                for t in range(T):
                    o = work("cs", b)[:, t * 2 * NHM:(t + 1) * 2 * NHM]
                    mm(o[:, 0:NHM], upto, dA[b][:, t, :], start=True, stop=True)
                    last = mm(o[:, NHM:2 * NHM], after, dA[b][:, t, :], start=True, stop=True)
                last.then_inc(s["cs_ps"], 1)

            def ssd_a(t, b):
                step, tok, n = f"s{t}a", slice(t * P, (t + 1) * P), T * b + t
                pe.wait_ge(s["xbc"], b + 1)
                claim(WORK_AT, step, b, 0)
                g = work(step, b, 0)
                last = mm(g[:, 0:P], xbc[b][:, XF, tok], xbc[b][:, XF + 1, tok], start=True, stop=True)
                if t == 0:
                    last = nc.tensor.transpose(g[:, P:2 * P], xbc[b][:, XF, tok], ident)
                last.then_inc(s["g_ps"], 1)
                claim(WORK_AT, step, b, 1)
                for f in range(XF):
                    last = nc.tensor.transpose(work(step, b, 1)[:, f * P:(f + 1) * P], xbc[b][:, f, tok], ident)
                last.then_inc(s["xtok_ps"], 1)
                pe.wait_ge(s["R"], n + 1)
                claim(PAIR_AT, step, b)
                for i in range(2):
                    last = mm(pair(step, b)[:, 512 * i:512 * (i + 1)], after, R[b][:, 4 * i:4 * i + 4, :],
                              start=True, stop=True)
                last.then_inc(s["diff_ps"], 1)

            def ssd_b(t, b):
                step, tok = f"s{t}b", slice(t * P, (t + 1) * P)
                claim(WORK_AT, step, b, 0)
                if t == 0:
                    pe.wait_ge(s["dtxd"], b + 1)
                    mm(work(step, b)[:, :], btok[b][:, :], dtxd[b][:, :], start=True, stop=True)\
                        .then_inc(s["state_ps"], 1)
                else:
                    pe.wait_ge(s["state"], b + 1)
                    mm(work(step, b)[:, :], xbc[b][:, XF + 1, tok], state[b][:, :], start=True, stop=True)\
                        .then_inc(s["yoff_ps"], 1)

            def ssd_c(t, b):
                step, n = f"s{t}c", T * b + t
                pe.wait_ge(s["M"], n + 1)
                pe.wait_ge(s["dtx"], n + 1)
                if t == 1:
                    pe.wait_ge(s["yoff"], b + 1)
                claim(WORK_AT, step, b)
                y = work(step, b)
                for hp in range(XF):
                    for a in range(2):
                        head = 2 * hp + a
                        last = mm(y[64 * a:64 * a + 64, hp * P:(hp + 1) * P], dtx[b][:, head * HP:(head + 1) * HP],
                                  L[b][:, head, :], start=True, stop=t == 0)
                    if t == 1:
                        last = mm(y[:, hp * P:(hp + 1) * P], yoff[b][:, hp * P:(hp + 1) * P], ident,
                                  start=False, stop=True)
                last.then_inc(s["y_ps"], 1)

            def out_proj(b):
                pe.wait_ge(s["ysum"], 2 * b + 2)
                claim(WORK_AT, "ob", b, 0)
                for t in range(T):
                    last = mm(work("ob", b, 0)[:, t:t + 1], ysq[b][:, 0, t * P:(t + 1) * P], ones[:, :],
                              start=True, stop=True)
                last.then_inc(s["ss_ps"], 1)
                if b == 0:
                    pe.wait_ge(s["w_norm_out"], XF)
                claim(WORK_AT, "ob", b, 1)
                for t in range(T):
                    for f in range(XF):
                        last = mm(work("ob", b, 1)[:, t * D:(t + 1) * D], yg[b][:, f, t * P:(t + 1) * P],
                                  w_out[:, f, :], start=f == 0, stop=f == XF - 1)
                last.then_inc(s["out_ps"], 1)

            def ctx(b):
                if b == 0:
                    pe.wait_ge(s["w_tables"], 16)
                pe.wait_ge(s["ctx_in"], 16 * (b + 1))
                claim(WORK_AT, "ctx", b)
                for k in range(KD):
                    for t in range(T):
                        last = nc.tensor.transpose(work("ctx", b)[:, k * SEQ + t * P:k * SEQ + (t + 1) * P],
                                                   ctx_t[b][:, t, k * P:(k + 1) * P], ident)
                last.then_inc(s["ctxT_ps"], 1)

            def heads_p(kind, b, weight, src, src_ready):
                if kind == "xk" and b == 0:
                    pe.wait_ge(s["w_cross"], 16)
                pe.wait_ge(s[src_ready], b + 1)
                claim(WORK_AT, f"{kind}_p", b)
                for f in range(2):
                    for k in range(KD):
                        last = mm(work(f"{kind}_p", b)[:, f * SEQ:(f + 1) * SEQ], weight[:, k, f * P:(f + 1) * P],
                                  src[b][:, k, :], start=k == 0, stop=k == KD - 1)
                last.then_inc(s[f"{kind}_ps"], 1)

            def heads_s(kind, b):
                pe.wait_ge(s[f"{kind}_sq"], b + 1)
                claim(WORK_AT, f"{kind}_s", b)
                mm(work(f"{kind}_s", b)[:, :], alike, full[kind][:, :], start=True, stop=True)\
                    .then_inc(s[f"{kind}_sum"], 1)

            def xv(b):
                claim(WORK_AT, "xv", b)
                for t in range(T):
                    for k in range(KD):
                        last = mm(work("xv", b)[:, t * D:(t + 1) * D], ctxT[b][:, k, t * P:(t + 1) * P], wv[:, k, :],
                                  start=k == 0, stop=k == KD - 1)
                last.then_inc(s["xv_ps"], 1)

            def x_scores(b, n):
                step = f"x{n}"
                if n == 0:
                    pe.wait_ge(s["xk_stack"], 16 * RUNS["xk"] * (b + 1))
                    pe.wait_ge(s["xq_stack"], 16 * RUNS["xq"] * (b + 1))
                for i in range(2):
                    q = 2 * n + i
                    claim(PAIR_AT, step, b, i)
                    for a in range(2):
                        rows = slice(64 * a, 64 * a + 6 * XD)
                        for kt in range(T):
                            last = mm(pair(step, b, i)[:, a * 512 + kt * SEQ:a * 512 + (kt + 1) * SEQ],
                                      xstack["xk"][b][rows, q, kt * P:(kt + 1) * P], xstack["xq"][b][rows, q, :],
                                      start=True, stop=True)
                    last.then_inc(s["xs_ps"], 1)

            def x_values(b, n):
                rnd, i = n // 3, n % 3
                q = 16 * b + 2 * n
                if n == 0:
                    pe.wait_ge(s["xv"], b + 1)
                if i == 0:
                    claim(OUT_AT, f"x{3 * rnd + 1}", b)
                pe.wait_ge(s["xp"], q + 2)
                o = outs(f"x{3 * rnd + 1}", b)
                end = min(2, 7 - 3 * rnd)
                for kt in range(T):
                    for j in range(4):
                        head = 4 * n + j
                        last = mm(o[32 * j:32 * j + 32, :], xvals[b][:, kt, head, :],
                                  probs(f"x{n}", b, j // 2)[:, j % 2, kt * SEQ:(kt + 1) * SEQ],
                                  start=i == 0 and kt == 0, stop=i == end and kt == T - 1)
                last.then_inc(s["xo_quad"], 1)

            def x_back(b, rnd):
                step = f"xb{rnd}"
                pe.wait_ge(s["xot"], 3 * b + rnd + 1)
                claim(WORK_AT, step, b)
                for t in range(T):
                    last = nc.tensor.transpose(work(step, b)[:, t * P:(t + 1) * P], xot[b][:, t * P:(t + 1) * P],
                                               ident)
                last.then_inc(s["xback_ps"], 1)

            def cross(b, n):
                if n < 8:
                    x_scores(b, n)
                if n > 0:
                    x_values(b, n - 1)

            def proj_a(b):
                if b == 0:
                    pe.wait_ge(s["w_latent"], 32)
                pe.wait_ge(s["xnT3"], b + 1)
                claim(WORK_AT, "pa", b, 0)
                for k in range(KD):
                    last = mm(work("pa", b, 0)[:, 0:SEQ], w_down[:, k, :], xnT[b][:, k, :],
                              start=k == 0, stop=k == KD - 1)
                last.then_inc(s["lat_ps"], 1)
                if b == 0:
                    pe.wait_ge(s["pool_init"], NST + 10)
                claim(WORK_AT, "pa", b, 1)
                for i, weight in enumerate((w_rope_k, w_rope_k2)):
                    for k in range(KD):
                        last = mm(work("pa", b, 1)[:, i * SEQ:(i + 1) * SEQ], weight[:, k, :], xnT[b][:, k, :],
                                  start=k == 0, stop=k == KD - 1)
                last.then_inc(s["kr_ps"], 1)

            def proj_b(b):
                pe.wait_ge(s["lat"], b + 1)
                kv, qd = slice(0, LAT), slice(LAT, 2 * LAT)
                for i, rows in enumerate((kv, qd)):
                    claim(WORK_AT, "pb", b, i)
                    mm(work("pb", b, i)[:, 0:SEQ], w_up[rows, :], lat[b][rows, :], start=True, stop=True)\
                        .then_inc(s["plain_ps"], 1)
                claim(WORK_AT, "pb", b, 2)
                mm(work("pb", b, 2)[:, 0:SEQ], w_second[qd, 0:P], lat[b][qd, :], start=True, stop=True)
                mm(work("pb", b, 2)[:, SEQ:2 * SEQ], w_rope_q2[qd, :], lat[b][qd, :], start=True, stop=True)\
                    .then_inc(s["qr_ps"], 1)
                claim(WORK_AT, "pb", b, 3)
                for t in range(T):
                    last = mm(work("pb", b, 3)[:, t * D:(t + 1) * D], lat[b][kv, t * P:(t + 1) * P],
                              w_second[kv, :], start=True, stop=True)
                last.then_inc(s["fv_ps"], 1)

            def f_max(b, n):
                step = f"max{n}"
                if n == 0:
                    pe.wait_ge(s["fk_stack"], 16 * RUNS["fk"] * (b + 1))
                    pe.wait_ge(s["fq_stack"], 16 * RUNS["fq"] * (b + 1))
                claim(PAIR_AT, step, b)
                ps = pair(step, b)
                if n < 2:
                    t, heads, keys = 0, range(8 * n, 8 * n + 8), P
                else:
                    t, heads, keys = 1, range(4 * (n - 2), 4 * (n - 2) + 4), SEQ
                for i, head in enumerate(heads):
                    o = ps[:, i * keys:(i + 1) * keys]
                    mm(o, fstack["fq"][b][0:96, head, t * P:(t + 1) * P], fstack["fk"][b][0:96, head, 0:keys],
                       start=True, stop=False)
                    last = mm(o[:, keys - P:keys], ident16, mask_q, start=False, stop=True)
                last.then_inc(s["fm_ps"], 1)

            def max_back(b):
                pe.wait_ge(s["max_parts"], b + 1)
                claim(WORK_AT, "mtb", b)
                o16 = work("mtb", b)[:, 0:P].bitcast(BF16)
                for t in range(T):
                    last = nc.tensor.transpose(o16[0:3 * AH, t * P:(t + 1) * P],
                                               fmp[b][:, t, :, :].rearrange("p c h -> p (c h)"), ident16)
                last.then_inc(s["maxT_ps"], 1)

            def f_scores(b, n):
                step = f"f{n}"
                if n == 0:
                    pe.wait_ge(s["max_stack"], 16 * 3 * (b + 1))
                for i in range(2):
                    claim(PAIR_AT, step, b, i)
                    for a in range(2):
                        head = 4 * n + 2 * i + a
                        o = pair(step, b, i)[:, 512 * a:512 * a + 384]
                        mm(o[:, 0:SEQ], fstack["fk"][b][0:99, head, 0:P], fstack["fq"][b][0:99, head, :],
                           start=True, stop=False)
                        mm(o[:, 0:P], ident16, mask_k, start=False, stop=True)
                        mm(o[:, SEQ:SEQ + P], fstack["fk"][b][0:99, head, P:SEQ], fstack["fq"][b][0:99, head, P:SEQ],
                           start=True, stop=False)
                        last = mm(o[:, SEQ:SEQ + P], ident16, mask_k, start=False, stop=True)
                    last.then_inc(s["fs_ps"], 1)

            def f_values(b, n):
                q = 8 * b + 2 * n
                if n == 0:
                    pe.wait_ge(s["fv"], b + 1)
                claim(WORK_AT, f"f{n + 1}", b)
                pe.wait_ge(s["fp"], q + 2)
                o = work(f"f{n + 1}", b)[:, 0:SEQ]
                for kt in range(T):
                    for j in range(4):
                        pr = probs(f"f{n}", b, j // 2)[:, j % 2, :]
                        last = mm(o[32 * j:32 * j + 32, kt * P:SEQ], fvals[b][:, kt, 4 * n + j, :],
                                  pr[:, 0:SEQ] if kt == 0 else pr[:, SEQ:SEQ + P], start=kt == 0, stop=kt == T - 1)
                last.then_inc(s["fo_ps"], 1)

            def f_back(b, n):
                pe.wait_ge(s["fot"], 4 * b + n + 1)
                for t in range(T):
                    last = nc.tensor.transpose(work(f"f{n + 1}", b)[:, SEQ + t * P:SEQ + (t + 1) * P],
                                               fot[b][:, t * P:(t + 1) * P], ident)
                last.then_inc(s["fback_ps"], 1)

            def causal(b, n):
                if n < 4:
                    f_scores(b, n)
                if n > 0:
                    f_values(b, n - 1)

            def oproj_a(b):
                pe.wait_ge(s["ao"], 4 * (b + 1))
                claim(WORK_AT, "opa", b)
                for k in range(KD):
                    for t in range(T):
                        last = nc.tensor.transpose(work("opa", b)[:, k * SEQ + t * P:k * SEQ + (t + 1) * P],
                                                   ao[b][:, t, k * P:(k + 1) * P], ident)
                last.then_inc(s["aoT_ps"], 1)

            def oproj_b(b):
                pe.wait_ge(s["aoT"], b + 1)
                claim(WORK_AT, "opb", b)
                for t in range(T):
                    for k in range(KD):
                        last = mm(work("opb", b)[:, t * D:(t + 1) * D], aoT[b][:, k, t * P:(t + 1) * P],
                                  w_o[:, k, :], start=k == 0, stop=k == KD - 1)
                last.then_inc(s["o_ps"], 1)

            def router(b):
                pe.wait_ge(s["hT"], b + 1)
                claim(WORK_AT, "ra", b)
                for t in range(T):
                    for k in range(KD):
                        last = mm(work("ra", b)[:, t * NR:(t + 1) * NR], hT[b][:, k, t * P:(t + 1) * P],
                                  w_router[:, k, :], start=k == 0, stop=k == KD - 1)
                last.then_inc(s["router_ps"], 1)

            def expert(b, e):
                n = NE * b + e
                if n == 0:
                    pe.wait_ge(s["w_experts"], 16)
                claim(WORK_AT, f"e{e}", b, 0)
                for g in range(2):
                    for k in range(KD):
                        last = mm(work(f"e{e}", b, 0)[:, g * SEQ:(g + 1) * SEQ], gate_up[:, e, k, g, :],
                                  hT[b][:, k, :], start=k == 0, stop=k == KD - 1)
                last.then_inc(s["gu_ps"], 1)

            def expert_step(b, e):
                if e < NE:
                    expert(b, e)
                if e > 1:
                    expert_down(b, e - 2)

            def expert_down(b, e):
                n, at = NE * b + e, down_at(b, e)
                pe.wait_ge(s["hidden"], n + 1)
                claim(WORK_AT, *at)
                for t in range(T):
                    last = mm(work(*at)[:, t * D:(t + 1) * D], hid[n % NG][:, t * P:(t + 1) * P],
                              down_w[:, e, :], start=True, stop=True)
                last.then_inc(s["down_ps"], 1)

            steps = {"l1b": ln1, "dta": dt, **{f"inx{i}": lambda b, i=i: inx(b, i) for i in range(CF // 2)}, "cs": cs,
                     **{f"z{i}": lambda b, i=i: gate_in(b, i) for i in range(2)}, "ob": out_proj,
                     **{f"s{t}{c}": (lambda b, f=f, t=t: f(t, b)) for t in range(T)
                        for c, f in (("a", ssd_a), ("b", ssd_b), ("c", ssd_c))},
                     "ctx": ctx, "xk_p": lambda b: heads_p("xk", b, wk, ctxT, "ctxT"), "xv": xv,
                     "xk_s": lambda b: heads_s("xk", b), "xq_s": lambda b: heads_s("xq", b),
                     "l2b": lambda b: transposes("l2b", b, "xn2", xn[1], "xnT2_ps"),
                     "xq_p": lambda b: heads_p("xq", b, wq, xnT, "xnT2"),
                     **{f"x{n}": lambda b, n=n: cross(b, n) for n in range(9)},
                     **{f"xb{n}": lambda b, n=n: x_back(b, n) for n in range(3)},
                     "l3b": lambda b: transposes("l3b", b, "xn3", xn[0], "xnT3_ps"), "pa": proj_a, "pb": proj_b,
                     **{f"max{n}": lambda b, n=n: f_max(b, n) for n in range(6)}, "mtb": max_back,
                     **{f"f{n}": lambda b, n=n: causal(b, n) for n in range(5)},
                     **{f"fb{n}": lambda b, n=n: f_back(b, n) for n in range(4)},
                     "opa": oproj_a, "opb": oproj_b,
                     "l4b": lambda b: transposes("l4b", b, "xn4", xn[1], "hT_ps"), "ra": router,
                     **{f"e{n}": lambda b, n=n: expert_step(b, n) for n in range(NE + 1)},
                     "store": lambda b: expert_down(b, NE - 1)}
            for step, b in SCHEDULE:
                if step in steps:
                    steps[step](b)

        @block.scalar
        def _(act):
            count = [0]

            nc.scalar.preload_act_table_set("natural_log_exp_and_others")
            run = nc.scalar.activation

            def then(ins):
                count[0] += 1
                ins.then_inc(s["act_chain"], 1)
                act.wait_ge(s["act_chain"], count[0])

            def sigmoid_log(dst, src):
                then(run(dst, src, ACT.Abs))
                then(run(dst, dst, ACT.Exp, scale=-1.0))
                return run(dst, dst, ACT.Ln, bias=1.0)

            def inv_sqrt(dst, src, done):
                then(run(dst, src, ACT.Ln, bias=eps[:, 0:1]))
                run(dst, dst, ACT.Exp, scale=-0.5).then_inc(s[done], 1)

            def ln(i, b):
                if i == 0 and b == 0:
                    act.wait_ge(s["eps"], 2)
                act.wait_ge(s[f"mv{i}"], b + 1)
                inv_sqrt(rstd[b][:, i, :], mv[b][:, i, :, 1], f"rstd{i}")

            def rms3(b):
                act.wait_ge(s["ms3"], b + 1)
                inv_sqrt(rstd[b][:, 5, :], rstd[b][:, 4, :], "rms3")

            def dt(b):
                act.wait_ge(s["dt_abs"], b + 1)
                then(run(sp[b][:, 2, :], sp[b][:, 1, :], ACT.Exp, scale=-1.0))
                run(sp[b][:, 3, :], sp[b][:, 2, :], ACT.Ln, bias=1.0).then_inc(s["dt_exp"], 1)

            def inx(b, i):
                act.wait_ge(s["xbc_ps"], 3 * b + i + 1)
                if b > 0 and i == 0:
                    act.wait_ge(s["y_done"], 2 * b)
                ps = work(f"inx{i}", b)
                for f in range(2):
                    c = 2 * i + f
                    last = run(conv[b][:, c, :], ps[:, f * SEQ:(f + 1) * SEQ], ACT.Identity,
                               scale=conv_w[:, c * TAPS + 3:c * TAPS + 4], bias=conv_b[:, c:c + 1])
                last.then_inc(s["conv_in"], 1)

            def cs(b):
                act.wait_ge(s["cs_ps"], b + 1)
                run(ecs[b][:, :, :, :].rearrange("p t c h -> p (t c h)"), work("cs", b)[:, 0:T * 2 * NHM], ACT.Exp)\
                    .then_inc(s["ecs"], 1)

            def xbc_gate(b):
                act.wait_ge(s["taps"], CF * (b + 1))
                if b > 0:
                    act.wait_ge(s["ysq"], b)
                    act.wait_ge(s["out_ps"], b)
                    act.wait_ge(s["y_ps"], 2 * b)
                bc = dtx[b][:, :]
                sigmoid_log(yg[b][:, :, :], conv[b][:, 0:XF, :]).then_inc(s["sig_xbc"], 1)
                sigmoid_log(bc, conv[b][:, XF:CF, :].rearrange("p f n -> p (f n)")).then_inc(s["sig_xbc"], 1)

            def xbc_exp(b):
                bc = dtx[b][:, :]
                act.wait_ge(s["min_xbc"], 2 * b + 1)
                run(yg[b][:, :, :], yg[b][:, :, :], ACT.Exp).then_inc(s["sig_xbc"], 1)
                act.wait_ge(s["min_xbc"], 2 * b + 2)
                run(bc, bc, ACT.Exp).then_inc(s["sig_xbc"], 1)

            def z_gate(b, i):
                if i == 0:
                    xbc_exp(b)
                else:
                    z_exp(b, i - 1)
                if i < 2:
                    z_log(b, i)

            def z_exp(b, i):
                z = sz[b][:, 2 * i:2 * i + 2, :].rearrange("p f n -> p (f n)")
                act.wait_ge(s["min_z"], 2 * b + i + 1)
                run(z, z, ACT.Exp).then_inc(s["sig_z"], 1)

            def z_log(b, i):
                if b > 0 and i == 0:
                    act.wait_ge(s["ysum"], 2 * b)
                    act.wait_ge(s["ss_ps"], b)
                act.wait_ge(s["z_ps"], 2 * b + i + 1)
                z = sz[b][:, 2 * i:2 * i + 2, :].rearrange("p f n -> p (f n)")
                sigmoid_log(z, work(f"z{i}", b)[:, :]).then_inc(s["sig_z"], 1)

            def ssd_a(t, b):
                n = T * b + t
                act.wait_ge(s["diff_ps"], n + 1)
                if n > 0:
                    act.wait_ge(s["y_ps"], n)
                run(L[b][:, :, :].rearrange("p h n -> p (h n)"), pair(f"s{t}a", b)[:, :], ACT.Exp)\
                    .then_inc(s["L"], 1)

            def out_a(b):
                act.wait_ge(s["y_done"], 2 * (b + 1))
                run(ysq[b][:, :, :], yg[b][:, :, :], ACT.Square).then_inc(s["ysq"], 1)

            def out_b(b):
                act.wait_ge(s["ss_ps"], b + 1)
                run(rstd[b][:, 4, :], work("ob", b, 0)[:, 0:T], ACT.Ln, scale=1.0 / DI, bias=eps[:, 0:1])\
                    .then_inc(s["gate_ln"], 1)
                act.wait_ge(s["gate_ln"], b + 1)
                run(rstd[b][:, 5, :], rstd[b][:, 4, :], ACT.Exp, scale=-0.5).then_inc(s["gate_rs"], 1)

            def heads_p(kind, b):
                act.wait_ge(s[f"{kind}_ps"], b + 1)
                after_last_user(act, SHARED_AT["full_" + kind[1]], f"{kind}_p", b)
                run(full[kind][:, :], work(f"{kind}_p", b)[:, :], ACT.Square).then_inc(s[f"{kind}_sq"], 1)

            def heads_s(kind, b):
                act.wait_ge(s[f"{kind}_sum"], b + 1)
                if b > 0:
                    act.wait_ge(s[f"{kind}_full"], b)
                run(rs[kind][:, :], work(f"{kind}_s", b)[:, :], ACT.Ln, scale=1.0 / XD, bias=eps[:, 1:2])\
                    .then_inc(s[f"{kind}_ln"], 1)
                act.wait_ge(s[f"{kind}_ln"], b + 1)
                run(rs[kind][:, :], rs[kind][:, :], ACT.Exp, scale=-0.5).then_inc(s[f"{kind}_rs"], 1)

            def cross(b, n):
                for i in range(2):
                    q = 16 * b + 2 * n + i
                    act.wait_ge(s["xs_ps"], q + 1)
                    after_last_user(act, PROB_AT, f"x{n}", b, i)
                    run(probs(f"x{n}", b, i)[:, :, :].rearrange("p a n -> p (a n)"), pair(f"x{n}", b, i)[:, :], ACT.Exp,
                        scale=float(XD) ** -0.5).then_inc(s["xp"], 1)

            def proj_a(b):
                act.wait_ge(s["lat_ps"], b + 1)
                if b > 0:
                    act.wait_ge(s["fv_ps"], b)
                run(lat[b][:, :], work("pa", b, 0)[:, 0:SEQ], ACT.Copy).then_inc(s["lat"], 1)

            def proj_b(b):
                for i, kind in enumerate(("fk", "fq")):
                    act.wait_ge(s["plain_ps"], 2 * b + i + 1)
                    after_last_user(act, SHARED_AT["full_" + kind[1]], ("pa", "pb")[i], b)
                    run(full[kind][:, 0:SEQ], work("pb", b, i)[:, 0:SEQ], ACT.Copy).then_inc(s["plain"], 1)

            def causal(b, n):
                for i in range(2):
                    q = 8 * b + 2 * n + i
                    act.wait_ge(s["fs_ps"], q + 1)
                    after_last_user(act, PROB_AT, f"f{n}", b, i)
                    run(probs(f"f{n}", b, i)[:, :, 0:384],
                        pair(f"f{n}", b, i)[:, :].rearrange("p (a n) -> p a n", a=2)[:, :, 0:384], ACT.Exp,
                        scale=float(AD) ** -0.5).then_inc(s["fp"], 1)

            def router(b):
                act.wait_ge(s["logits"], b + 1)
                run(rt[b][:, 1, :, :], rt[b][:, 0, :, :], ACT.Exp, scale=-1.0).then_inc(s["router_exp"], 1)

            def expert(b, e):
                n = NE * b + e
                act.wait_ge(s["gu_ps"], n + 1)
                if n >= NG:
                    act.wait_ge(s["down_ps"], n - NG + 1)
                sigmoid_log(sg[n % NG][:, :], work(f"e{e}", b, 0)[:, 0:SEQ]).then_inc(s["sig_gate"], 1)

            def expert_exp(b, e):
                n = NE * b + e
                act.wait_ge(s["gated"], 2 * n + 1)
                run(sg[n % NG][:, :], sg[n % NG][:, :], ACT.Exp).then_inc(s["sig_gate"], 1)

            def expert_step(b, e):
                if e > 0:
                    expert_exp(b, e - 1)
                if e < NE:
                    expert(b, e)

            steps = {**{f"l{i + 1}a": lambda b, i=i: ln(i, b) for i in range(4)}, "l3m": rms3,
                     "dta": dt, **{f"inx{i}": lambda b, i=i: inx(b, i) for i in range(CF // 2)}, "cs": cs,
                     "xbc": xbc_gate, **{f"z{i}": lambda b, i=i: z_gate(b, i) for i in range(3)},
                     "s0a": lambda b: ssd_a(0, b), "s1a": lambda b: ssd_a(1, b), "oa": out_a, "ob": out_b,
                     **{f"{kind}_p": lambda b, kind=kind: heads_p(kind, b) for kind in ("xk", "xq")},
                     **{f"{kind}_s": lambda b, kind=kind: heads_s(kind, b) for kind in ("xk", "xq")},
                     **{f"x{n}": lambda b, n=n: cross(b, n) for n in range(8)}, "pa": proj_a, "pb": proj_b,
                     **{f"f{n}": lambda b, n=n: causal(b, n) for n in range(4)},
                     "ra": router, **{f"e{n}": lambda b, n=n: expert_step(b, n) for n in range(NE + 1)}}
            for step, b in SCHEDULE:
                if step in steps:
                    steps[step](b)

        @block.vector
        def _(dve):
            count = [0]
            vec = nc.vector

            def then(ins):
                count[0] += 1
                ins.then_inc(s["dve_chain"], 1)
                dve.wait_ge(s["dve_chain"], count[0])

            vec.memset(ones[:, :], 1.0)
            vec.memset(eps[:, 0:1], EPS).then_inc(s["eps"], 1)
            vec.memset(eps[:, 1:2], X_EPS).then_inc(s["eps"], 1)

            def ln(i, b, src, ready, value):
                dve.wait_ge(s[ready], value)
                for t in range(T):
                    then(vec.bn_stats(stats[b][:, i, t, :], src[:, t, :]))
                then(vec.bn_aggr(mv[b][:, i, 0, :], stats[b][:, i, 0, :]))
                last = vec.bn_aggr(mv[b][:, i, 1, :], stats[b][:, i, 1, :])
                if i < 3:
                    last.then_inc(s[f"mv{i}"], 1)
                    return
                then(last)
                m2 = sp[b][:, 7, 0:T]
                then(vec.tensor_tensor(m2, mv[b][:, 3, :, 0], mv[b][:, 3, :, 0], ALU.mult))
                vec.tensor_tensor(mv[b][:, 3, :, 1], mv[b][:, 3, :, 1], m2, ALU.add).then_inc(s["mv3"], 1)

            def ln_apply(i, b, src, xn_sem):
                after_last_user(dve, SHARED_AT[f"xn_{i % 2}"], f"l{i + 1}b", b)
                dve.wait_ge(s[f"rstd{i}"], b + 1)
                for t in range(T):
                    last = vec.tensor_scalar(xn[i % 2][:, t, :], src[:, t, :], mv[b][:, i, t, 0:1],
                                             rstd[b][:, i, t:t + 1], ALU.subtract, ALU.mult)
                last.then_inc(s[xn_sem], 1)

            def copy_T(step, b, ready, dst, done, free=None):
                dve.wait_ge(s[ready], b + 1)
                if free is not None and free[1]:
                    dve.wait_ge(s[free[0]], free[1])
                vec.tensor_copy(dst[:, :, :].rearrange("p k n -> p (k n)"), work(step, b)[:, :]).then_inc(s[done], 1)

            def l1c(b):
                free_xnT(b, 0)
                copy_T("l1b", b, "xnT_ps", xnT[b], "xnT")

            def free_xnT(b, use):
                if use == 0:
                    if b >= 2:
                        dve.wait_ge(s["kr_ps"], b - 1)
                elif use == 1:
                    dve.wait_ge(s["z_ps"], 2 * (b + 1))
                    dve.wait_ge(s["dt_ps"], b + 1)
                else:
                    dve.wait_ge(s["xq_ps"], b + 1)

            def dt(b):
                dve.wait_ge(s["dt_ps"], b + 1)
                if b == 0:
                    dve.wait_ge(s["w_xbc"], 32)
                S = sp[b]
                vec.tensor_tensor(S[:, 0, :].rearrange("p (t h) -> p t h", t=T),
                                  work("dta", b)[:, 0:T * NHM].rearrange("p (t h) -> p t h", t=T),
                                  dt_bias[:, :].unsqueeze(1).to_broadcast([P, T, NHM]), ALU.add)\
                    .then_inc(s["dt_raw"], 1)
                dve.wait_ge(s["dt_raw"], b + 1)
                vec.scalar_tensor_tensor(out=S[:, 1, :], in0=S[:, 0, :], scalar=-1.0, in1=S[:, 0, :], op0=ALU.mult,
                                         op1=ALU.max).then_inc(s["dt_abs"], 1)

            def dt_b(b):
                S = sp[b]
                dve.wait_ge(s["dt_exp"], b + 1)
                then(vec.tensor_scalar(S[:, 4, :], S[:, 2, :], 1.0, None, ALU.add))
                then(vec.tensor_scalar(S[:, 5, :], S[:, 4, :], -1.0, None, ALU.add))
                then(vec.tensor_tensor(S[:, 5, :], S[:, 2, :], S[:, 5, :], ALU.subtract))
                then(vec.reciprocal(S[:, 4, :], S[:, 4, :]))
                then(vec.tensor_tensor(S[:, 5, :], S[:, 5, :], S[:, 4, :], ALU.mult))
                then(vec.scalar_tensor_tensor(out=S[:, 6, :], in0=S[:, 0, :], scalar=0.0, in1=S[:, 3, :],
                                              op0=ALU.max, op1=ALU.add))
                then(vec.tensor_tensor(dt_t[b][:, :, :].rearrange("p t h -> p (t h)"), S[:, 6, :], S[:, 5, :], ALU.add))
                vec.tensor_tensor(dA[b][:, :, :], dt_t[b][:, :, :],
                                  a_row[:, :].unsqueeze(1).to_broadcast([P, T, NHM]), ALU.mult)\
                    .then_inc(s["dA"], 1)

            def inx(b, i):
                dve.wait_ge(s["conv_in"], 3 * b + i + 1)
                for k in range(TAPS - 2, -1, -1):
                    back = TAPS - 1 - k
                    for f in range(2):
                        c = 2 * i + f
                        ins = vec.scalar_tensor_tensor(
                            out=conv[b][:, c, back:], in0=work(f"inx{i}", b)[:, f * SEQ:(f + 1) * SEQ - back],
                            scalar=conv_w[:, c * TAPS + k:c * TAPS + k + 1], in1=conv[b][:, c, back:],
                            op0=ALU.mult, op1=ALU.add)
                        if k == 0:
                            ins.then_inc(s["taps"], 1)
                    if k:
                        then(ins)

            def exponent(log, src):
                return vec.scalar_tensor_tensor(out=log, in0=src, scalar=0.0, in1=log, op0=ALU.min, op1=ALU.subtract)

            def xbc_exponent(b):
                gates_of = ((yg[b][:, :, :], conv[b][:, 0:XF, :]), (bc_gate(b), conv[b][:, XF:CF, :]))
                for i, (log, src) in enumerate(gates_of):
                    dve.wait_ge(s["sig_xbc"], 4 * b + i + 1)
                    exponent(log, src).then_inc(s["min_xbc"], 1)

            def bc_gate(b):
                return dtx[b][:, :].rearrange("p (f n) -> p f n", f=CF - XF)

            def z_step(b, i):
                if i == 0:
                    dve.wait_ge(s["sig_xbc"], 4 * b + 3)
                    vec.tensor_tensor(xbc[b][:, 0:XF, :], conv[b][:, 0:XF, :], yg[b][:, :, :], ALU.mult)
                    dve.wait_ge(s["sig_xbc"], 4 * b + 4)
                    vec.tensor_tensor(xbc[b][:, XF:CF, :], conv[b][:, XF:CF, :], bc_gate(b), ALU.mult)\
                        .then_inc(s["xbc"], 1)
                else:
                    z = sz[b][:, 2 * i - 2:2 * i, :].rearrange("p f n -> p (f n)")
                    dve.wait_ge(s["sig_z"], 2 * (2 * b + i - 1) + 2)
                    vec.tensor_tensor(z, z, work(f"z{i - 1}", b)[:, :], ALU.mult).then_inc(s["sz"], 1)
                if i < 2:
                    z = sz[b][:, 2 * i:2 * i + 2, :].rearrange("p f n -> p (f n)")
                    dve.wait_ge(s["sig_z"], 2 * (2 * b + i) + 1)
                    exponent(z, work(f"z{i}", b)[:, :]).then_inc(s["min_z"], 1)

            def ssd_a(t, b):
                n, step = T * b + t, f"s{t}a"
                dve.wait_ge(s["g_ps"], n + 1)
                if n > 0:
                    dve.wait_ge(s["y_ps"], n)
                if t == 0:
                    then(vec.tensor_copy(btok[b][:, :], work(step, b, 0)[:, P:2 * P]))
                vec.tensor_tensor(Gm[b][:, :], work(step, b, 0)[:, 0:P], upto, ALU.mult).then_inc(s["gm"], 1)
                dve.wait_ge(s["xtok_ps"], n + 1)
                vec.tensor_tensor(dtx[b][:, :].rearrange("p (h d) -> p h d", h=NHM),
                                  work(step, b, 1)[:, :].rearrange("p (h d) -> p h d", h=NHM),
                                  dt_t[b][:, t, :].unsqueeze(2).to_broadcast([P, NHM, HP]), ALU.mult)\
                    .then_inc(s["dtx"], 1)

            def ssd_b(t, b):
                n, step = T * b + t, f"s{t}b"
                if t == 0:
                    dve.wait_ge(s["dtx"], n + 1)
                    dve.wait_ge(s["ecs"], b + 1)
                    vec.tensor_tensor(dtxd[b][:, :].rearrange("p (h d) -> p h d", h=NHM),
                                      dtx[b][:, :].rearrange("p (h d) -> p h d", h=NHM),
                                      ecs[b][:, 0, 1, :].unsqueeze(2).to_broadcast([P, NHM, HP]), ALU.mult)\
                        .then_inc(s["dtxd"], 1)
                dve.wait_ge(s["L"], n + 1)
                dve.wait_ge(s["gm"], n + 1)
                vec.tensor_tensor(L[b][:, :, :], L[b][:, :, :], Gm[b][:, :].unsqueeze(1).to_broadcast([P, NHM, P]),
                                  ALU.mult).then_inc(s["M"], 1)
                if t == 0:
                    dve.wait_ge(s["state_ps"], b + 1)
                    vec.tensor_copy(state[b][:, :], work(step, b)[:, :]).then_inc(s["state"], 1)
                else:
                    dve.wait_ge(s["yoff_ps"], b + 1)
                    vec.tensor_tensor(yoff[b][:, :].rearrange("p (h d) -> p h d", h=NHM),
                                      work(step, b)[:, :].rearrange("p (h d) -> p h d", h=NHM),
                                      ecs[b][:, 1, 0, :].unsqueeze(2).to_broadcast([P, NHM, HP]), ALU.mult)\
                        .then_inc(s["yoff"], 1)

            def ssd_c(t, b):
                n, step, tok = T * b + t, f"s{t}c", slice(t * P, (t + 1) * P)
                dve.wait_ge(s["y_ps"], n + 1)
                dve.wait_ge(s["xD"], b + 1)
                vec.tensor_tensor(yg[b][:, :, tok], work(step, b)[:, :].rearrange("p (f n) -> p f n", f=XF),
                                  xD[b][:, :, tok], ALU.add).then_inc(s["y"], 1)
                dve.wait_ge(s["y"], n + 1)
                dve.wait_ge(s["sz"], 2 * (b + 1))
                vec.tensor_tensor(yg[b][:, :, tok], yg[b][:, :, tok], sz[b][:, :, tok], ALU.mult)\
                    .then_inc(s["y_done"], 1)

            def out_proj(b):
                if b == 0:
                    dve.wait_ge(s["w_out"], 16)
                    for f in range(XF):
                        vec.tensor_scalar(w_out[:, f, :], w_out[:, f, :], norm_w[:, f:f + 1], None, ALU.mult)\
                           .then_inc(s["w_norm_out"], 1)
                dve.wait_ge(s["out_ps"], b + 1)
                dve.wait_ge(s["gate_rs"], b + 1)
                if b >= NF:
                    dve.wait_ge(s["base"], b - NF + 1)
                for t in range(T):
                    last = vec.scalar_tensor_tensor(out=x1[b][:, t, :], in0=work("ob", b, 1)[:, t * D:(t + 1) * D],
                                                    scalar=rstd[b][:, 5, t:t + 1], in1=x0[b][:, t, :], op0=ALU.mult,
                                                    op1=ALU.add)
                last.then_inc(s["x1"], 1)

            def ctx(b):
                if b > 0:
                    dve.wait_ge(s["xv_ps"], b)
                    dve.wait_ge(s["xk_ps"], b)
                copy_T("ctx", b, "ctxT_ps", ctxT[b], "ctxT")

            def split_hi(kind, b):
                after_last_user(dve, SHARED_AT["parts_" + kind[1]], f"{kind}_f", b)
                vec.tensor_copy(parts[kind][:, 0, :, :], full[kind][:, :].rearrange("p (f n) -> p f n", f=2))\
                    .then_inc(s[f"{kind}_rounded"], 1)

            def split_mid(kind, b):
                dve.wait_ge(s[f"{kind}_diffs"], 2 * b + 1)
                vec.tensor_copy(parts[kind][:, 1, :, :], full[kind][:, :].rearrange("p (f n) -> p f n", f=2))\
                    .then_inc(s[f"{kind}_rounded"], 1)

            def heads_f(kind, b):
                dve.wait_ge(s[f"{kind}_rs"], b + 1)
                vec.tensor_tensor(full[kind][:, :], work(f"{kind}_p", b)[:, :], rs[kind][:, :], ALU.mult)\
                    .then_inc(s[f"{kind}_full"], 1)
                dve.wait_ge(s[f"{kind}_full"], b + 1)
                split_hi(kind, b)

            def xv(b):
                dve.wait_ge(s["xv_ps"], b + 1)
                if b == 0:
                    dve.wait_ge(s["pool_init"], NST + 4)
                else:
                    dve.wait_ge(s["xo_quad"], 8 * b)
                ps = work("xv", b)
                for t in range(T):
                    for i in range(3):
                        quads = len(range(i, XH // 4, 3))
                        for m in range(quads):
                            n = i + 3 * m
                            last = vec.tensor_copy(
                                xvals[b][:, t, 4 * n:4 * n + 4, 9 * i:9 * i + XD],
                                ps[:, t * D + 32 * n:t * D + 32 * n + 32].rearrange("p (j d) -> p j d", j=4))
                last.then_inc(s["xv"], 1)

            def cross(b, n):
                if n in (3, 6, 8):
                    rnd = (3, 6, 8).index(n)
                    dve.wait_ge(s["xo_quad"], 8 * b + n)
                    if b + rnd > 0:
                        dve.wait_ge(s["xback_ps"], 3 * b + rnd)
                    vec.tensor_copy(xot[b][:, :], outs(f"x{3 * rnd + 1}", b)).then_inc(s["xot"], 1)

            def x_back(b, rnd):
                ni, step = min(3, 8 - 3 * rnd), f"xb{rnd}"
                dve.wait_ge(s["xback_ps"], 3 * b + rnd + 1)
                if b >= 2 and rnd == 0:
                    dve.wait_ge(s["base"], b - 1)
                for t in range(T):
                    v = work(step, b)[:, t * P:(t + 1) * P].rearrange("p (j c) -> p j c", j=4)[:, :, 0:9 * ni]\
                        .rearrange("p j (i d) -> p i j d", i=ni)
                    den = xden[b][:, t, 0:4 * ni].rearrange("p (i j) -> p i j", j=4)
                    then(vec.reciprocal(den, v[:, :, :, XD]))
                    o = x2[b][:, t, 96 * rnd:96 * rnd + 32 * ni]
                    last = vec.tensor_tensor(o.rearrange("p (i j d) -> p i j d", i=ni, j=4), v[:, :, :, 0:XD],
                                             den.unsqueeze(3).to_broadcast([P, ni, 4, XD]), ALU.mult)
                last.then_inc(s["xo"], 1)
                if rnd == 2:
                    dve.wait_ge(s["xo"], 3 * (b + 1))
                    vec.tensor_tensor(x2[b][:, :, :], x2[b][:, :, :], x1[b][:, :, :], ALU.add)\
                        .then_inc(s["x2"], 1)

            def l2c(b):
                free_xnT(b, 1)
                copy_T("l2b", b, "xnT2_ps", xnT[b], "xnT2")

            def l3m(b):
                dve.wait_ge(s["rstd2"], b + 1)
                r = rstd[b]
                then(vec.tensor_tensor(r[:, 4, :], r[:, 2, :], r[:, 2, :], ALU.mult))
                vec.tensor_tensor(r[:, 4, :], r[:, 4, :], mv[b][:, 2, :, 1], ALU.mult).then_inc(s["ms3"], 1)
                for t in range(T):
                    last = vec.tensor_scalar(y3[b][:, t, :], x2[b][:, t, :], mv[b][:, 2, t, 0:1], r[:, 2, t:t + 1],
                                             ALU.subtract, ALU.mult)
                then(last)

            def l3b(b):
                after_last_user(dve, SHARED_AT["xn_0"], "l3b", b)
                dve.wait_ge(s["rms3"], b + 1)
                for t in range(T):
                    last = vec.tensor_scalar(xn[0][:, t, :], y3[b][:, t, :], rstd[b][:, 5, t:t + 1], None, ALU.mult)
                last.then_inc(s["xn3"], 1)

            def l3c(b):
                dve.wait_ge(s["xnT3_ps"], b + 1)
                if b == 0:
                    dve.wait_ge(s["w_latent"], 32)
                free_xnT(b, 2)
                for k in range(KD):
                    last = vec.tensor_scalar(xnT[b][:, k, :], work("l3b", b)[:, k * SEQ:(k + 1) * SEQ],
                                             ln1_w[:, k:k + 1], None, ALU.mult)
                last.then_inc(s["xnT3"], 1)

            def rope(kind, step, i, ps_ready, done, b):
                dve.wait_ge(s[ps_ready], b + 1)
                after_last_user(dve, SHARED_AT["full_" + kind[1]], step, b)
                vec.tensor_tensor(full[kind][:, SEQ:2 * SEQ], work(step, b, i)[:, 0:SEQ], rope_cs[:, 0:SEQ],
                                  ALU.mult)
                if b > 0:
                    dve.wait_ge(s[f"{kind}_full"], b)
                vec.tensor_tensor(rope_t[:, KIND[kind] - 2, :], work(step, b, i)[:, SEQ:2 * SEQ],
                                  rope_cs[:, SEQ:2 * SEQ], ALU.mult).then_inc(s[done], 1)

            def proj_a(b):
                rope("fk", "pa", 1, "kr_ps", "k_rope", b)

            def proj_b(b):
                rope("fq", "pb", 2, "qr_ps", "q_rope", b)
                dve.wait_ge(s["fv_ps"], b + 1)
                if b == 0:
                    dve.wait_ge(s["pool_init"], NST + 4)
                else:
                    dve.wait_ge(s["fo_ps"], 4 * b)
                vec.tensor_copy(fvals[b][:, :, :, 0:AD],
                                work("pb", b, 3)[:, :].rearrange("p (t h d) -> p t h d", t=T, h=AH))\
                    .then_inc(s["fv"], 1)

            def f_split(kind, b):
                dve.wait_ge(s[f"{kind}_full"], b + 1)
                dve.wait_ge(s["plain"], 2 * b + (1 if kind == "fk" else 2))
                split_hi(kind, b)

            def f_max(b, n):
                dve.wait_ge(s["fm_ps"], 6 * b + n + 1)
                ps = pair(f"max{n}", b)
                if n < 2:
                    src = ps[:, :].rearrange("p (h k) -> p h k", h=8)
                    dst = fmx[b][:, 0, 8 * n:8 * n + 8]
                else:
                    src = ps[:, :].rearrange("p (h k) -> p h k", h=4)
                    dst = fmx[b][:, 1, 4 * (n - 2):4 * (n - 2) + 4]
                vec.tensor_reduce(dst, src, AX.X, ALU.max, negate=True).then_inc(s["mx"], 1)

            def maxT_(b):
                dve.wait_ge(s["mx"], 6 * (b + 1))
                f, r = fmx[b][:, :, :], fmr[b][:, :].rearrange("p (t h) -> p t h", t=T)
                then(vec.tensor_copy(fmp[b][:, :, 0, :], f))
                then(vec.tensor_tensor(r, f, fmp[b][:, :, 0, :], ALU.subtract))
                then(vec.tensor_copy(fmp[b][:, :, 1, :], r))
                vec.tensor_tensor(fmp[b][:, :, 2, :], r, fmp[b][:, :, 1, :], ALU.subtract).then_inc(s["max_parts"], 1)

            def max_row(b):
                dve.wait_ge(s["maxT_ps"], b + 1)
                if b > 0:
                    dve.wait_ge(s["max_stack"], 48 * b)
                vec.tensor_copy(maxT[b][:, :], work("mtb", b)[:, 0:P].bitcast(BF16)[0:3 * AH, 0:SEQ])\
                    .then_inc(s["maxT"], 1)

            def causal(b, n):
                if n > 0:
                    dve.wait_ge(s["fo_ps"], 4 * b + n)
                    if b + n > 1:
                        dve.wait_ge(s["fback_ps"], 4 * b + n - 1)
                    vec.tensor_copy(fot[b][:, :], work(f"f{n}", b)[:, 0:SEQ]).then_inc(s["fot"], 1)

            def f_back(b, n):
                dve.wait_ge(s["fback_ps"], 4 * b + n + 1)
                if b > 0 and n == 0:
                    dve.wait_ge(s["aoT_ps"], b)
                v = work(f"f{n + 1}", b)[:, SEQ:SEQ + T * P].rearrange("p (t j c) -> p t j c", t=T, j=4)
                then(vec.reciprocal(fden[b][:, :, :], v[:, :, :, AD]))
                for t in range(T):
                    last = vec.tensor_tensor(ao[b][:, t, 64 * n:64 * n + 64].rearrange("p (j d) -> p j d", j=4),
                                             v[:, t, :, 0:AD], fden[b][:, t, :].unsqueeze(2).to_broadcast([P, 4, AD]),
                                             ALU.mult)
                last.then_inc(s["ao"], 1)

            def oproj_a(b):
                copy_T("opa", b, "aoT_ps", aoT[b], "aoT", ("o_ps", b))

            def oproj_b(b):
                dve.wait_ge(s["o_ps"], b + 1)
                vec.tensor_tensor(h4[b][:, :, :], work("opb", b)[:, :].rearrange("p (t n) -> p t n", t=T),
                                  y3[b][:, :, :], ALU.add).then_inc(s["h"], 1)

            def l4b(b):
                after_last_user(dve, SHARED_AT["xn_1"], "l4b", b)
                dve.wait_ge(s["rstd3"], b + 1)
                for t in range(T):
                    last = vec.tensor_scalar(xn[1][:, t, :], h4[b][:, t, :], rstd[b][:, 3, t:t + 1], None, ALU.mult)
                last.then_inc(s["xn4"], 1)

            def l4c(b):
                dve.wait_ge(s["hT_ps"], b + 1)
                if b > 0:
                    dve.wait_ge(s["router_ps"], b)
                    dve.wait_ge(s["gu_ps"], NE * b)
                for k in range(KD):
                    last = vec.tensor_scalar(hT[b][:, k, :], work("l4b", b)[:, k * SEQ:(k + 1) * SEQ],
                                             ln2_w[:, k:k + 1], None, ALU.mult)
                last.then_inc(s["hT"], 1)

            def router(b):
                r = rt[b]
                dve.wait_ge(s["router_ps"], b + 1)
                vec.tensor_tensor(r[:, 0, :, :], work("ra", b)[:, 0:T * NR].rearrange("p (t e) -> p t e", t=T),
                                  router_b[:, :].unsqueeze(1).to_broadcast([P, T, NR]), ALU.add)\
                    .then_inc(s["logits"], 1)

            def router_b_(b):
                r = rt[b]
                dve.wait_ge(s["router_exp"], b + 1)
                then(vec.tensor_scalar(r[:, 2, :, :], r[:, 1, :, :], 1.0, None, ALU.add))
                then(vec.reciprocal(r[:, 3, :, :], r[:, 2, :, :]))
                prob = r[:, 3, :, :]
                for t in range(T):
                    mine = prob[:, t, :].unsqueeze(2).to_broadcast([P, NR, NR])
                    other = prob[:, t, :].unsqueeze(1).to_broadcast([P, NR, NR])
                    c = [cmp_[b][:, i, t, :].rearrange("p (e j) -> p e j", e=NR) for i in range(2)]
                    then(vec.tensor_tensor(c[0], other, mine, ALU.is_gt))
                    then(vec.tensor_tensor(c[1], other, mine, ALU.is_equal))
                    then(vec.tensor_tensor(c[1], c[1], before, ALU.mult))
                    then(vec.tensor_tensor(c[0], c[0], c[1], ALU.add))
                    then(vec.tensor_reduce(r[:, 4, t, :], c[0], AX.X, ALU.add))
                then(vec.tensor_scalar(r[:, 5, :, :], r[:, 4, :, :], 1.5, None, ALU.is_lt))
                then(vec.tensor_tensor(r[:, 5, :, :], r[:, 5, :, :], prob, ALU.mult))
                then(vec.tensor_reduce(rsum[b][:, 0, :], r[:, 5, :, :], AX.X, ALU.add))
                then(vec.reciprocal(rsum[b][:, 1, :], rsum[b][:, 0, :]))
                then(vec.tensor_tensor(gates[b][:, :, :], r[:, 5, :, :],
                                       rsum[b][:, 1, :].unsqueeze(2).to_broadcast([P, T, NR]), ALU.mult))
                then(vec.tensor_scalar(gates[b][:, :, :], gates[b][:, :, :], 1.0 / 8, None, ALU.mult))

            def expert(b, e):
                n = NE * b + e
                dve.wait_ge(s["sig_gate"], 2 * n + 1)
                exponent(sg[n % NG][:, :], work(f"e{e}", b, 0)[:, 0:SEQ]).then_inc(s["gated"], 1)

            def expert_hidden(b, e):
                n, ps = NE * b + e, work(f"e{e}", b, 0)
                dve.wait_ge(s["sig_gate"], 2 * n + 2)
                vec.tensor_tensor(hid[n % NG][:, :], sg[n % NG][:, :], ps[:, 0:SEQ], ALU.mult).then_inc(s["gated"], 1)
                dve.wait_ge(s["gated"], 2 * n + 2)
                vec.tensor_tensor(hid[n % NG][:, :], hid[n % NG][:, :], ps[:, SEQ:2 * SEQ], ALU.mult)\
                    .then_inc(s["hidden"], 1)

            def expert_step(b, e):
                if e > 0:
                    expert_hidden(b, e - 1)
                if e > 1:
                    add_expert(b, e - 2)
                if e < NE:
                    expert(b, e)

            def add_expert(b, e):
                n = NE * b + e
                dve.wait_ge(s["down_ps"], n + 1)
                ps = work(*down_at(b, e))
                if e == 0:
                    dve.wait_ge(s["base"], b + 1)
                    vec.scalar_tensor_tensor(out=acc[b][:, :, :], in0=ps[:, :].rearrange("p (t n) -> p t n", t=T),
                                             scalar=1.0 / 8, in1=acc[b][:, :, :], op0=ALU.mult, op1=ALU.add)\
                       .then_inc(s["acc"], 1)
                else:
                    dve.wait_ge(s["acc"], n)
                    for t in range(T):
                        last = vec.scalar_tensor_tensor(out=acc[b][:, t, :], in0=ps[:, t * D:(t + 1) * D],
                                                        scalar=gates[b][:, t, e - 1:e], in1=acc[b][:, t, :],
                                                        op0=ALU.mult, op1=ALU.add)
                    last.then_inc(s["acc"], 1)

            steps = {"l1a": lambda b: ln(0, b, x0[b], "x_in" if b else "x_in_first", 16 * (NB - 1) if b else 16),
                     "l2a": lambda b: ln(1, b, x1[b], "x1", b + 1), "l3a": lambda b: ln(2, b, x2[b], "x2", b + 1),
                     "l4a": lambda b: ln(3, b, h4[b], "h", b + 1),
                     "l1b": lambda b: ln_apply(0, b, x0[b], "xn"), "l2b": lambda b: ln_apply(1, b, x1[b], "xn2"),
                     "l1c": l1c, "l2c": l2c, "l3m": l3m, "l3b": l3b, "l3c": l3c, "l4b": l4b, "l4c": l4c,
                     "dta": dt, "dtb": dt_b, **{f"inx{i}": lambda b, i=i: inx(b, i) for i in range(CF // 2)},
                     "xbc": xbc_exponent, **{f"z{i}": lambda b, i=i: z_step(b, i) for i in range(3)},
                     **{f"s{t}{c}": (lambda b, f=f, t=t: f(t, b)) for t in range(T)
                        for c, f in (("a", ssd_a), ("b", ssd_b), ("c", ssd_c))}, "ob": out_proj,
                     "ctx": ctx, "xv": xv, "xk_f": lambda b: heads_f("xk", b), "xq_f": lambda b: heads_f("xq", b),
                     "fk_f": lambda b: f_split("fk", b), "fq_f": lambda b: f_split("fq", b),
                     **{f"{kind}_m": lambda b, kind=kind: split_mid(kind, b) for kind in KIND},
                     **{f"x{n}": lambda b, n=n: cross(b, n) for n in range(9)},
                     **{f"xb{n}": lambda b, n=n: x_back(b, n) for n in range(3)}, "pa": proj_a, "pb": proj_b,
                     **{f"max{n}": lambda b, n=n: f_max(b, n) for n in range(6)}, "mta": maxT_, "mtb": max_row,
                     **{f"f{n}": lambda b, n=n: causal(b, n) for n in range(5)},
                     **{f"fb{n}": lambda b, n=n: f_back(b, n) for n in range(4)},
                     "opa": oproj_a, "opb": oproj_b, "ra": router, "rb": router_b_,
                     **{f"e{n}": lambda b, n=n: expert_step(b, n) for n in range(NE + 1)},
                     "store": lambda b: add_expert(b, NE - 1)}
            for step, b in SCHEDULE:
                if step in steps:
                    steps[step](b)

        @block.gpsimd
        def _(pool):
            gp = nc.gpsimd
            for i in range(NST):
                gp.memset(fstack["fk"][i][96:99, :, :], 1.0).then_inc(s["pool_init"], 1)
                pool.wait_ge(s["pool_init"], i + 1)
            gp.memset(xvals[0][:, :, :, :], 0.0).then_inc(s["pool_init"], 1)
            gp.memset(fvals[0][:, :, :, :], 0.0).then_inc(s["pool_init"], 1)
            pool.wait_ge(s["pool_init"], NST + 2)
            for n in range(XH // 4):
                i = n % 3
                last = gp.memset(xvals[0][:, :, 4 * n:4 * n + 4, 9 * i + XD:9 * i + XD + 1], 1.0)
            last.then_inc(s["pool_init"], 1)
            gp.memset(fvals[0][:, :, :, AD:AD + 1], 1.0).then_inc(s["pool_init"], 1)

            def turned(dst, src):
                gp.tensor_scalar(dst[:, 0:P // 2], src[:, P // 2:P], -1.0, None, ALU.mult).then_inc(s["pool_init"], 1)
                gp.tensor_copy(dst[:, P // 2:P], src[:, 0:P // 2]).then_inc(s["pool_init"], 1)

            def turn_weights(b):
                if b == 0:
                    pool.wait_ge(s["w_latent"], 32)
                    pool.wait_ge(s["pool_init"], NST + 4)
                    for k in range(KD):
                        turned(w_rope_k2[:, k, :], w_rope_k[:, k, :])
                    pool.wait_ge(s["pool_init"], NST + 8)
                    turned(w_rope_q2[LAT:2 * LAT, :], w_second[LAT:2 * LAT, 0:P])
                    pool.wait_ge(s["pool_init"], NST + 10)

            def skip(b):
                pool.wait_ge(s["xbc"], b + 1)
                if b > 0:
                    pool.wait_ge(s["out_ps"], b)
                    pool.wait_ge(s["ysq"], b)
                gp.tensor_tensor(xD[b][:, :, :], xbc[b][:, 0:XF, :],
                                 d_skip[:, :].unsqueeze(2).to_broadcast([P, XF, SEQ]), ALU.mult)\
                    .then_inc(s["xD"], 1)

            def decays(t, b):
                n = T * b + t
                pool.wait_ge(s["dA"], b + 1)
                if n > 0:
                    pool.wait_ge(s["diff_ps"], n)
                gp.tensor_tensor(R[b][:, :, :], upto.unsqueeze(1).to_broadcast([P, NHM, P]),
                                 dA[b][:, t, :].unsqueeze(2).to_broadcast([P, NHM, P]), ALU.mult)\
                    .then_inc(s["R"], 1)

            def out_proj(b):
                pool.wait_ge(s["ysq"], b + 1)
                gp.tensor_tensor(ysq[b][:, 0:2, :], ysq[b][:, 0:2, :], ysq[b][:, 2:4, :], ALU.add)\
                    .then_inc(s["ysum"], 1)
                pool.wait_ge(s["ysum"], 2 * b + 1)
                gp.tensor_tensor(ysq[b][:, 0, :], ysq[b][:, 0, :], ysq[b][:, 1, :], ALU.add).then_inc(s["ysum"], 1)

            def difference(kind, b, i):
                pool.wait_ge(s[f"{kind}_rounded"], 2 * b + i + 1)
                f3 = full[kind][:, :].rearrange("p (f n) -> p f n", f=2)
                gp.tensor_tensor(f3 if i == 0 else parts[kind][:, 2, :, :], f3, parts[kind][:, i, :, :],
                                 ALU.subtract).then_inc(s[f"{kind}_diffs"], 1)

            def rope(kind, done, b):
                pool.wait_ge(s[done], b + 1)
                gp.tensor_tensor(full[kind][:, SEQ:2 * SEQ], full[kind][:, SEQ:2 * SEQ],
                                 rope_t[:, KIND[kind] - 2, :], ALU.add).then_inc(s[f"{kind}_full"], 1)

            def router(b):
                pool.wait_ge(s["h"], b + 1)
                gp.tensor_tensor(acc[b][:, :, :], x2[b][:, :, :], h4[b][:, :, :], ALU.add).then_inc(s["base"], 1)

            steps = {"cs": lambda b: decays(0, b), "s0a": skip, "s0b": lambda b: decays(1, b), "oa": out_proj,
                     "l2a": turn_weights,
                     "pa": lambda b: rope("fk", "k_rope", b), "pb": lambda b: rope("fq", "q_rope", b),
                     **{f"{kind}_f": lambda b, kind=kind: difference(kind, b, 0) for kind in KIND},
                     **{f"{kind}_m": lambda b, kind=kind: difference(kind, b, 1) for kind in KIND}, "ra": router}
            for step, b in SCHEDULE:
                if step in steps:
                    steps[step](b)


def _rows(a, k):
    a = np.asarray(a)
    return a.reshape(k, P, -1).transpose(1, 0, 2).reshape(P, -1)


def _spread(row):
    return np.broadcast_to(np.asarray(row), (P, np.asarray(row).shape[0]))


def _dims_first(a):
    return np.asarray(a).reshape(-1, AH, AR).transpose(0, 2, 1).reshape(-1, AH * AR)


def _by_half(a):
    return np.asarray(a).reshape(-1, XH // 2, 2, XD).transpose(0, 2, 3, 1).reshape(-1, XH * XD)


def _shape_tables():
    i = np.arange(P)
    ident = np.eye(P, dtype=np.float32)
    upto = (i[:, None] <= i[None, :]).astype(np.float32)
    after = (i[:, None] > i[None, :]).astype(np.float32)
    alike = (i[:, None] % AH == i[None, :] % AH).astype(np.float32)
    inv = (1.0 / 10000.0 ** (np.arange(0, AR, 2, dtype=np.float32) / AR)).astype(np.float32)
    ang = np.outer(np.arange(SEQ, dtype=np.float32), inv).astype(np.float32)
    ang = ang[:, i // AH % (AR // 2)].T
    rope = np.concatenate([np.cos(ang), np.sin(ang)], axis=1).astype(np.float32)
    e = np.arange(NR)
    before = (e[None, :] < e[:, None]).astype(np.float32).reshape(-1)
    shape = np.concatenate([ident, upto, after, alike, rope, _spread(before)], axis=1)
    later = np.where(i[None, :] > i[:, None], np.float32(NEG), np.float32(0))
    masks = np.stack([ident, later, later.T], axis=1)
    return shape, masks


def kernel(**inputs):
    import ml_dtypes
    import concourse.bacc as _bacc
    from concourse.bass_utils import run_bass_kernel_spmd as _run

    g = {k: np.asarray(v) for k, v in inputs.items()}
    m, c, f = ({k[len(pre):]: v for k, v in g.items() if k.startswith(pre)}
               for pre in ("L0_attn_", "L0_xattn_", "L0_ffn_"))
    kv = np.concatenate([c["Wk"], c["Wv"]], axis=0).reshape(XH * XD, 2, D)
    rope_k_w, rope_q_w, k_u_w, q_u_w = (_dims_first(f[n]) for n in ("rope_k_w", "rope_q_w", "k_u_w", "q_u_w"))
    shape, masks = _shape_tables()
    arrays = {
        "mixer": [_rows(m["conv_w"], CF), _rows(m["conv_b"], CF), _rows(m["norm_w"], XF), _spread(m["A"]),
                  _spread(m["dt_bias"]), _rows(np.repeat(m["D"], HP), XF)],
        "w_in": [_rows(m["W_in"], KD)], "w_out": [_rows(m["W_out"], XF)],
        "cross": [_rows(_by_half(c["Wq"].T), KD), _rows(_by_half(kv[:, 0].T), KD), _rows(kv[:, 1].T, KD)],
        "latent": [_rows(f["ln1_w"], KD), _rows(f["ln2_w"], KD),
                   _rows(np.concatenate([f["kv_d_w"], f["q_d_w"]], axis=1), KD), _rows(rope_k_w, KD),
                   np.concatenate([k_u_w, q_u_w], axis=0),
                   np.concatenate([f["v_u_w"], np.concatenate([rope_q_w, rope_q_w], axis=1)], axis=0),
                   _rows(f["o_w"], KD), _rows(f["router_w"], KD), _spread(f["router_b"])],
        "experts": [], "shape": [shape],
    }
    gate = np.concatenate([f["sh_gate"][None], f["r_gate"]], axis=0)
    up = np.concatenate([f["sh_up"][None], f["r_up"]], axis=0)
    down = np.concatenate([f["sh_down"][None], f["r_down"]], axis=0)
    gu = np.stack([gate, up], axis=2).reshape(NE, KD, P, 2, FI).transpose(2, 0, 1, 3, 4).reshape(P, -1)
    arrays["experts"] = [gu, down.transpose(1, 0, 2).reshape(P, -1)]

    nc = _bacc.Bacc("TRN2", target_bir_lowering=False, num_devices=1)
    data, packs = {}, {}
    for name, parts in arrays.items():
        data["pack_" + name] = np.ascontiguousarray(np.concatenate(parts, axis=1))
        packs[name] = nc.dram_tensor("pack_" + name, [P, WIDTH[name]], F32, kind="ExternalInput").ap()
    data["masks16"] = masks.astype(ml_dtypes.bfloat16)
    masks16 = nc.dram_tensor("masks16", [P, 3, P], BF16, kind="ExternalInput").ap()
    for name in ("x", "ctx_2048"):
        data[name + "_in"] = np.ascontiguousarray(g[name])
    x_ap = nc.dram_tensor("x_in", [NB, SEQ, D], F32, kind="ExternalInput").ap()
    c_ap = nc.dram_tensor("ctx_2048_in", [NB, SEQ, D], F32, kind="ExternalInput").ap()
    out = nc.dram_tensor("out_0", [NB, SEQ, D], F32, kind="ExternalOutput").ap()
    decoder_layer(nc, x_ap, c_ap, packs, masks16, out)
    r = _run(nc, [data], core_ids=[0])
    return r.results[0]["out_0"]
```
